# Optimizing a Trainium2 kernel written in Bass

```python
import numpy as np
import jax
import jax.numpy as jnp

def _softmax(x, axis=-1):
    return jax.nn.softmax(x, axis=axis)

def _gelu(x):
    return jax.nn.gelu(x, approximate=True)

def _silu(x):
    return jax.nn.silu(x)

def _sigmoid(x):
    return jax.nn.sigmoid(x)

def _layernorm(x, axis=-1, eps=1e-05):
    m = jnp.mean(x, axis=axis, keepdims=True)
    v = jnp.var(x, axis=axis, keepdims=True)
    return (x - m) / jnp.sqrt(v + eps)

def _scatter_add(tgt, idx, src, axis=0):
    return tgt.at[idx].add(src)

def _segment_sum(src, seg, n):
    return jax.ops.segment_sum(src, seg, n)
kernel_name = 'mk_gnn_resnorm_d2_gnn_r8_cada85'

def setup_inputs(seed: int=0):
    np.random.seed(seed)
    _w = jnp.asarray

    def _rec_inputs():
        import jax
        import jax.numpy as jnp
        _gk = jax.random.key(seed)
        x = -0.0003713 + 1 * jax.random.normal(jax.random.fold_in(_gk, 1), (12500, 128), jnp.float32)
        _s = jax.random.randint(jax.random.fold_in(_gk, 2), (100000,), 0, 12500, jnp.int32)
        _d = jax.random.randint(jax.random.fold_in(_gk, 3), (100000,), 0, 12500, jnp.int32)
        _loop = jnp.arange(12500, dtype=jnp.int32)
        src = jnp.concatenate([_s, _d, _loop])
        dst = jnp.concatenate([_d, _s, _loop])
        _o = jnp.argsort(dst, stable=True)
        src = src[_o]
        dst = dst[_o]
        edge_weight = jax.random.uniform(jax.random.fold_in(_gk, 13), (212500,), jnp.float32, 0.0, 1)
        return (x, src, dst, edge_weight)
    x, src, dst, edge_weight = _rec_inputs()

    def _L0_gnn_setup():
        import jax, jax.numpy as jnp
        import numpy as np
        N_NODES = 12500
        N_EDGES = 75000
        HIDDEN = 128
        HEADS = 4
        HEAD_DIM = HIDDEN // HEADS
        NEG_SLOPE = 0.2

        def gat_conv(x, edge_index, W, att_src, att_dst, bias):
            N = x.shape[0]
            loops = jnp.arange(N, dtype=edge_index.dtype)
            src = jnp.concatenate([edge_index[0], loops])
            dst = jnp.concatenate([edge_index[1], loops])
            h = (x @ W).reshape(N, HEADS, HEAD_DIM)
            a_src = jnp.einsum('nhc,hc->nh', h, att_src)
            a_dst = jnp.einsum('nhc,hc->nh', h, att_dst)
            e = a_src[src] + a_dst[dst]
            e = jnp.where(e > 0, e, NEG_SLOPE * e)
            e_max = jax.ops.segment_max(e, dst, num_segments=N)
            e_max = jnp.where(jnp.isfinite(e_max), e_max, 0.0)
            ex = jnp.exp(e - e_max[dst])
            denom = jax.ops.segment_sum(ex, dst, num_segments=N)
            alpha = ex / (denom[dst] + 1e-16)
            msg = h[src] * alpha[:, :, None]
            out = jax.ops.segment_sum(msg, dst, num_segments=N)
            return out.reshape(N, HIDDEN) + bias
        key = jax.random.key(seed)
        ks = jax.random.split(key, 12)
        s_in = 1.0 / np.sqrt(HIDDEN)
        s_att = 1.0 / np.sqrt(HEAD_DIM)
        inp = {'x': jax.random.normal(ks[0], (N_NODES, HIDDEN), dtype=jnp.float32), 'edge_index': jax.random.randint(ks[1], (2, N_EDGES), 0, N_NODES, dtype=jnp.int64), 'W1': jax.random.normal(ks[2], (HIDDEN, HIDDEN), dtype=jnp.float32) * s_in, 'att_src1': jax.random.normal(ks[3], (HEADS, HEAD_DIM), dtype=jnp.float32) * s_att, 'att_dst1': jax.random.normal(ks[4], (HEADS, HEAD_DIM), dtype=jnp.float32) * s_att, 'bias1': jnp.zeros((HIDDEN,), dtype=jnp.float32), 'W2': jax.random.normal(ks[5], (HIDDEN, HIDDEN), dtype=jnp.float32) * s_in, 'att_src2': jax.random.normal(ks[6], (HEADS, HEAD_DIM), dtype=jnp.float32) * s_att, 'att_dst2': jax.random.normal(ks[7], (HEADS, HEAD_DIM), dtype=jnp.float32) * s_att, 'bias2': jnp.zeros((HIDDEN,), dtype=jnp.float32)}
        return inp
    _L0_gnn_all = _L0_gnn_setup()
    _L0_gnn_in = {k: v for k, v in _L0_gnn_all.items() if k in ('W1', 'att_src1', 'att_dst1', 'bias1', 'W2', 'att_src2', 'att_dst2', 'bias2')}
    del _L0_gnn_all

    def _L1_gnn_setup():
        import jax, jax.numpy as jnp
        import numpy as np
        N_NODES = 6250
        N_EDGES = 100000
        HID = 128
        key = jax.random.key(seed)
        ks = jax.random.split(key, 10)
        s_msg = 1.0 / np.sqrt(2 * HID + 1)
        s_u1 = 1.0 / np.sqrt(2 * HID)
        s_u2 = 1.0 / np.sqrt(HID)
        return {'z': jax.random.normal(ks[0], (N_NODES, HID), dtype=jnp.float32), 'edge_weight': jax.random.uniform(ks[1], (N_EDGES,), dtype=jnp.float32), 'edge_src': jax.random.randint(ks[2], (N_EDGES,), 0, N_NODES), 'edge_dst': jax.random.randint(ks[3], (N_EDGES,), 0, N_NODES), 'Wm': jax.random.normal(ks[4], (2 * HID + 1, HID), dtype=jnp.float32) * s_msg, 'bm': jax.random.normal(ks[5], (HID,), dtype=jnp.float32) * s_msg, 'W1': jax.random.normal(ks[6], (2 * HID, HID), dtype=jnp.float32) * s_u1, 'b1': jax.random.normal(ks[7], (HID,), dtype=jnp.float32) * s_u1, 'W2': jax.random.normal(ks[8], (HID, HID), dtype=jnp.float32) * s_u2, 'b2': jax.random.normal(ks[9], (HID,), dtype=jnp.float32) * s_u2}
    _L1_gnn_all = _L1_gnn_setup()
    _L1_gnn_in = {k: v for k, v in _L1_gnn_all.items() if k in ('Wm', 'bm', 'W1', 'b1', 'W2', 'b2')}
    del _L1_gnn_all
    return {'x': x, 'src': src, 'dst': dst, 'edge_weight': edge_weight, 'L0_gnn_W1': _L0_gnn_in['W1'], 'L0_gnn_att_src1': _L0_gnn_in['att_src1'], 'L0_gnn_att_dst1': _L0_gnn_in['att_dst1'], 'L0_gnn_bias1': _L0_gnn_in['bias1'], 'L0_gnn_W2': _L0_gnn_in['W2'], 'L0_gnn_att_src2': _L0_gnn_in['att_src2'], 'L0_gnn_att_dst2': _L0_gnn_in['att_dst2'], 'L0_gnn_bias2': _L0_gnn_in['bias2'], 'L1_gnn_Wm': _L1_gnn_in['Wm'], 'L1_gnn_bm': _L1_gnn_in['bm'], 'L1_gnn_W1': _L1_gnn_in['W1'], 'L1_gnn_b1': _L1_gnn_in['b1'], 'L1_gnn_W2': _L1_gnn_in['W2'], 'L1_gnn_b2': _L1_gnn_in['b2']}

def reference(x, src, dst, edge_weight, L0_gnn_W1, L0_gnn_att_src1, L0_gnn_att_dst1, L0_gnn_bias1, L0_gnn_W2, L0_gnn_att_src2, L0_gnn_att_dst2, L0_gnn_bias2, L1_gnn_Wm, L1_gnn_bm, L1_gnn_W1, L1_gnn_b1, L1_gnn_W2, L1_gnn_b2):
    import jax
    import jax.numpy as jnp

    def _L0_gnn_ref(x, edge_index, W1, att_src1, att_dst1, bias1, W2, att_src2, att_dst2, bias2):
        import jax, jax.numpy as jnp
        import numpy as np
        N_NODES = 12500
        N_EDGES = 75000
        HIDDEN = 128
        HEADS = 4
        HEAD_DIM = HIDDEN // HEADS
        NEG_SLOPE = 0.2

        def gat_conv(x, edge_index, W, att_src, att_dst, bias):
            N = x.shape[0]
            loops = jnp.arange(N, dtype=edge_index.dtype)
            src = jnp.concatenate([edge_index[0], loops])
            dst = jnp.concatenate([edge_index[1], loops])
            h = (x @ W).reshape(N, HEADS, HEAD_DIM)
            a_src = jnp.einsum('nhc,hc->nh', h, att_src)
            a_dst = jnp.einsum('nhc,hc->nh', h, att_dst)
            e = a_src[src] + a_dst[dst]
            e = jnp.where(e > 0, e, NEG_SLOPE * e)
            e_max = jax.ops.segment_max(e, dst, num_segments=N)
            e_max = jnp.where(jnp.isfinite(e_max), e_max, 0.0)
            ex = jnp.exp(e - e_max[dst])
            denom = jax.ops.segment_sum(ex, dst, num_segments=N)
            alpha = ex / (denom[dst] + 1e-16)
            msg = h[src] * alpha[:, :, None]
            out = jax.ops.segment_sum(msg, dst, num_segments=N)
            return out.reshape(N, HIDDEN) + bias
        x = jax.nn.relu(gat_conv(x, edge_index, W1, att_src1, att_dst1, bias1))
        x = jax.nn.relu(gat_conv(x, edge_index, W2, att_src2, att_dst2, bias2))
        return x

    def _L1_gnn_ref(z, edge_weight, edge_src, edge_dst, Wm, bm, W1, b1, W2, b2):
        import jax, jax.numpy as jnp
        import numpy as np
        N_NODES = 6250
        N_EDGES = 100000
        HID = 128
        n, H = z.shape
        Wd, Ws, ww = (Wm[:H], Wm[H:2 * H], Wm[2 * H])
        msgs = z[edge_dst] @ Wd + z[edge_src] @ Ws + edge_weight[:, None] * ww[None, :] + bm
        agg = jax.ops.segment_max(msgs, edge_dst, num_segments=n)
        deg = jax.ops.segment_sum(jnp.ones_like(edge_weight), edge_dst, num_segments=n)
        agg = jnp.where(deg[:, None] > 0, agg, jnp.zeros((), dtype=z.dtype))
        W1a, W1b = (W1[:H], W1[H:])
        hidden = jax.nn.relu(z @ W1a + agg @ W1b + b1)
        return hidden @ W2 + b2
    edge_index = jnp.stack([src, dst])
    x = _layernorm(x + _L0_gnn_ref(x, edge_index, L0_gnn_W1, L0_gnn_att_src1, L0_gnn_att_dst1, L0_gnn_bias1, L0_gnn_W2, L0_gnn_att_src2, L0_gnn_att_dst2, L0_gnn_bias2), axis=-1)
    x = _layernorm(x + _L1_gnn_ref(x, edge_weight, src, dst, L1_gnn_Wm, L1_gnn_bm, L1_gnn_W1, L1_gnn_b1, L1_gnn_W2, L1_gnn_b2), axis=-1)
    return x

_drawn_inputs = setup_inputs


def setup_inputs(seed=0):
    import zlib

    import numpy as np

    out = dict(_drawn_inputs(seed))
    spreads = {'L0_gnn_bias1': (0.0, 0.1), 'L0_gnn_bias2': (0.0, 0.1)}
    factors = {'edge_weight': 8.0,
     'L0_gnn_att_dst1': 6.88,
     'L0_gnn_att_src2': 8.0,
     'L0_gnn_att_dst2': 26.262}
    for name, (base, spread) in spreads.items():
        noise = np.random.default_rng([zlib.crc32(name.encode()), seed]).standard_normal(out[name].shape)
        drawn = base * np.exp(spread * noise) if base else spread * noise
        out[name] = jnp.asarray(drawn.astype(out[name].dtype))
    for name, factor in factors.items():
        out[name] = (out[name] * factor).astype(out[name].dtype)
    return out
```

```python
from contextlib import ExitStack

import concourse.bass as bass
from concourse import mybir

F32 = mybir.dt.float32
I32 = mybir.dt.int32
ALU = mybir.AluOpType
ACT = mybir.ActivationFunctionType
AX_X = mybir.AxisListType.X

P = 128
HID = 128
HEADS = 4
HD = HID // HEADS
N_NODES = 12500
N_EDGES = 212500
NP = 125
NT = N_NODES // NP
GT = 5
NG = NT // GT
CB = 32
BE = CB * P
NB = -(-N_EDGES // BE)
NCH = NB * CB
KB = NCH // P
E_PAD = NCH * P
FULL_CH = N_EDGES // P
TAIL = N_EDGES - FULL_CH * P
SC = 4
NS = CB // SC
SE = SC * P
ROW = HID + 2 * HEADS
BIG = 1.0e30
SLOPE = 0.2
EPS = 1.0e-5
HR = CB + 1
assert NP * NT == N_NODES and NG * GT == NT and NB % 2 == 0 and NG % 2 == 0 and HEADS * CB == P
assert KB * P == NCH and FULL_CH // P == KB - 1


def due(value):
    return not isinstance(value, int) or value > 0


def rounds(eng, count, body, done=0):
    if not done:
        body(0)
    with eng.Fori(max(done, 1), done + count) as it:
        body(it)


def gnn_program(nc, x, src, dst, edge_weight, W_1, att_src_1, att_dst_1, bias_1, W_2, att_src_2, att_dst_2,
                bias_2, Wm, bm, U1, b1, U2, b2, out):
    with ExitStack() as ctx:
        def sb(name, shape, dt=F32):
            return ctx.enter_context(nc.sbuf_tensor(name, shape, dt))

        def sem(name):
            return ctx.enter_context(nc.semaphore(name))

        def dram(name, shape, dt=F32):
            return nc.dram_tensor(name, shape, dt).ap()

        ctx.enter_context(nc.allow_non_contiguous_dma(reason="small index and weight layouts"))

        table = [dram(f"table{l}", [N_NODES, ROW]) for l in range(2)]
        ztable = dram("ztable", [N_NODES, HID])
        zdst = dram("zdst", [N_NODES, HID])
        zrow = dram("zrow", [N_NODES, HID])
        result = [dram(f"result{l}", [E_PAD, w]) for l, w in enumerate((ROW, ROW, HID))]
        adst_at = [dram(f"adst_at{l}", [E_PAD + N_NODES, HEADS]) for l in range(2)]
        d_idx = dram("d_idx", [NB, P, CB], I32)
        d_ew = dram("d_ew", [NB, P, CB])
        d_mask = dram("d_mask", [NB, HEADS, CB, 2, P])
        d_carry = dram("d_carry", [NB, HEADS, HR])
        d_dst = dram("d_dst", [NCH, P])
        d_row = dram("d_row", [NP, NT], I32)
        d_first = dram("d_first", [NP, NT], I32)
        d_last = dram("d_last", [NP, NT], I32)

        G = sb("G", [P, 2, CB, ROW])
        R = sb("R", [P, 2, CB, ROW])
        pick = sb("pick", [P, CB, HID])
        V = sb("V", [P, 2, SC, HID])
        CBC = sb("CBC", [P, 2, SE])
        ST = sb("ST", [P, 2, SE])
        idx = sb("idx", [P, 2, CB], I32)
        mask = sb("mask", [P, 2, 2, P])
        adst_in = sb("adst_in", [CB, 2, P, HEADS])
        carry_mask = sb("carry_mask", [1, 2, HEADS, HR])
        ewt = sb("ewt", [P, 2, CB])
        A = sb("A", [P, P])
        T = sb("T", [P, P])
        U = sb("U", [P, P])
        E = sb("E", [P, P])
        L = sb("L", [P, P])
        M = sb("M", [P, P + 1])
        XD = sb("XD", [P, 2, P])
        EX = sb("EX", [P, 2, P])
        D = sb("D", [P, P])
        D0 = sb("D0", [P, 1])
        m_row = sb("m_row", [1, HEADS, HR])
        m_end = sb("m_end", [1, HEADS, HR])
        k_row = sb("k_row", [1, HEADS * HR])
        k_exp = sb("k_exp", [1, HEADS * HR])
        m_pre = sb("m_pre", [1, P])
        d_pre = sb("d_pre", [1, P])
        d_rowv = sb("d_rowv", [1, HEADS, HR])
        d_end = sb("d_end", [1, HEADS, HR])
        ident = sb("ident", [P, P])
        put = sb("put", [CB, HEADS, P])
        one = sb("one", [1, P])
        ones = sb("ones", [P, NT])
        node = sb("node", [P, NT])
        edge_of = sb("edge_of", [P, NT])
        has_edge = sb("has_edge", [P, NT])
        max_bound = sb("max_bound", [P, NT])
        Wx = [sb(f"Wx{l}", [P, ROW]) for l in range(2)]
        Wz = sb("Wz", [P, 2 * HID])
        att = [sb(f"att{l}", [P, 2 * HEADS]) for l in range(2)]
        wt = sb("wt", [P, HID])
        U1z = sb("U1z", [P, HID])
        U1a = sb("U1a", [P, HID])
        U2s = sb("U2s", [P, HID])
        b1c = sb("b1c", [P, 1])
        b2r = sb("b2r", [1, HID])
        bias = [sb(f"bias{l}", [P, HID]) for l in range(2)]
        bmr = sb("bmr", [1, 2 * HID])
        wwb = sb("wwb", [P, HID])
        eps = sb("eps", [P, 1])
        chunk_first = sb("chunk_first", [P, KB], I32)
        chunk_adst = sb("chunk_adst", [P, 2, KB, HEADS])
        q_idx = sb("q_idx", [P, 2, GT], I32)
        q_adst = sb("q_adst", [P, 2, GT, HEADS])
        last_in = sb("last_in", [P, 2, GT], I32)
        ends = sb("ends", [P, 2, GT, ROW])
        own = sb("own", [P, 2, GT, ROW])
        O = sb("O", [P, 2, GT, HID])
        xg = sb("xg", [P, 2, GT, HID])
        XT = sb("XT", [P, 2, 2 * HID])
        HTt = sb("HTt", [P, 2, GT, 2 * HID])
        self_e = sb("self_e", [P, GT, HEADS])
        self_w = sb("self_w", [P, 2, GT, HEADS])
        self_x = sb("self_x", [P, 2, GT, HEADS])
        den = sb("den", [P, GT, HEADS])
        stats = sb("stats", [P, GT, 6])
        mv = sb("mv", [P, GT, 2])
        std = sb("std", [P, GT])
        rstd = sb("rstd", [P, GT])

        room = R[:, :, :, :].rearrange("p a c f -> p (a c f)")
        room2 = G[:, :, :, :].rearrange("p a c f -> p (a c f)")

        def part(r, n, dt=F32):
            v = r[:, n * NCH:(n + 1) * NCH]
            return (v if dt == F32 else v.bitcast(dt)).rearrange("p (k f) -> p k f", k=KB)

        dst_i, prev_i, src_i = (part(room, n, I32) for n in range(3))
        dst_f, prev_f = part(room, 3), part(room, 4)
        src_f, same, same_neg, ew_f = (part(room2, n) for n in range(4))
        src_t = part(room2, 4, I32)
        LT = pick[:, :, :].rearrange("p c f -> p (c f)")[:, 0:KB * (NP + 1)].rearrange("p (k f) -> p k f", k=KB)
        hit = room[:, 0:KB * NP].rearrange("p (k f) -> p k f", k=KB)
        below = room[:, NCH:NCH + KB * NT].rearrange("p (k f) -> p k f", k=KB)
        rows_dst = ends[:, :, :, 0:P]
        small = sb("small", [P, 8, NT])
        smalli = sb("smalli", [P, 3, NT], I32)
        hundreds = sb("hundreds", [P, NP + 1])
        units = sb("units", [P, NT])
        chunk_goes = sb("chunk_goes", [P, KB])
        head_big = sb("head_big", [P, HEADS])

        def pb(name):
            return ctx.enter_context(nc.psum_tensor(name, [P, 512], F32))

        psV = [pb(f"psV{i}") for i in range(2)]
        psB = [pb(f"psB{i}") for i in range(2)]
        psS = [pb(f"psS{i}") for i in range(2)]
        psC = pb("psC")
        psT = pb("psT")
        ps_asrc, ps_adst = psC[:, 0:P], psC[:, P:2 * P]
        ps_row, ps_row2 = psC[0:1, 2 * P:3 * P], psC[0:1, 3 * P:4 * P]
        ps_col, ps_col2 = psT[:, 3 * P:3 * P + 1], psT[:, 3 * P + 2:3 * P + 3]

        pads = sem("pads")
        edges_in = sem("edges_in")
        consts_in = sem("consts_in")
        dst_out = sem("dst_out")
        consts = sem("consts")
        dve_step = sem("dve_step")
        floats = sem("floats")
        masks_made = sem("masks_made")
        setup_out = sem("setup_out")
        turned = sem("turned")
        turned_used = sem("turned_used")
        zeroed = sem("zeroed")
        digits = sem("digits")
        chunk_count = sem("chunk_count")
        row_made = sem("row_made")
        row_out = sem("row_out")
        shifted = sem("shifted")
        ends_made = sem("ends_made")
        ends_out = sem("ends_out")
        attw = sem("attw")
        attw_used = sem("attw_used")
        pick_made = sem("pick_made")
        search_step = sem("search_step")
        search_in = [sem(f"search_in{i}") for i in range(2)]
        search_rows = [sem(f"search_rows{i}") for i in range(2)]
        search_used = [sem(f"search_used{i}") for i in range(2)]

        def phase_sems(tag, pairs, singles):
            named = {name: [sem(f"{tag}_{name}_{i}") for i in range(2)] for name in pairs.split()}
            named.update({name: sem(f"{tag}_{name}") for name in singles.split()})
            return named

        gat_only = "asrc logits l_made l_row m_made m_col x_made exps d_made d_rows d_scan d_col d_final weights_t chain "
        steps = "v_made v_turned c_spread c_copied scanned s_turned r_made"
        pairs = "idx_in loads gathered batch_done stored"
        gat = phase_sems("gat", pairs, gat_only + steps)
        es = [gat, gat, phase_sems("max", pairs, steps)]
        placed = phase_sems("place", "in_ sent", "first_in first_out")
        after_gat = "chain xd ex o_made o_relu "
        ns = [phase_sems(f"node{l}", "in_ stored" + (" got used" if l else "") + (" free" if l in (1, 2) else ""),
                   ("", after_gat, after_gat + "std_in std_out ", "chain o_made o_relu std_in std_out hid_ps hid ")[l] +
                   "xt_ps xt h_ps h") for l in range(4)]

        def spread(v):
            return v.rearrange("(a n) -> a n", a=1).to_broadcast([P, HID])

        const_loads = [(Wx[0][:, 0:HID], W_1), (Wx[1][:, 0:HID], W_2), (Wz[:, 0:HID], Wm[HID:2 * HID, :]), (Wz[:, HID:2 * HID], Wm[0:HID, :]),
                       (wwb[:, :], Wm[2 * HID:2 * HID + 1, :].to_broadcast([P, HID])), (bmr[0:1, HID:2 * HID], bm.rearrange("(a n) -> a n", a=1)),
                       (U1z[:, :], U1[0:HID, :]), (U1a[:, :], U1[HID:2 * HID, :]), (U2s[:, :], U2),
                       (b1c[:, :], b1.rearrange("(n a) -> n a", a=1)), (b2r[:, :], b2.rearrange("(a n) -> a n", a=1)),
                       (bias[0][:, :], spread(bias_1)), (bias[1][:, :], spread(bias_2))]
        for l, pair in enumerate(((att_src_1, att_dst_1), (att_src_2, att_dst_2))):
            for n, a in enumerate(pair):
                for h in range(HEADS):
                    col = n * HEADS + h
                    const_loads.append((att[l][h * HD:(h + 1) * HD, col:col + 1], a[h:h + 1, :].rearrange("a f -> f a")))
        N_CONSTS = len(const_loads)

        def in_dmas(l):
            return 16 * (2 if l == 1 else 3)

        block = ctx.enter_context(nc.Block())
        HALF = NB // 2
        NHALF = NG // 2
        before = [0, HALF, 0]
        node_before = [0, NHALF]

        def node_rows(t, group, width):
            return t.rearrange("(p t) f -> p t f", t=NT)[:, bass.ds(group * GT, GT), 0:width]

        @block.sync
        def _(sp):
            sp.wait_ge(pads, 4)
            for flat, to in ((dst, dst_i), (src, src_i), (edge_weight, ew_f)):
                sp.dma_start(to[:, 0:KB - 1, :], flat[0:(KB - 1) * P * P].rearrange("(k p f) -> p k f", p=P, f=P)).then_inc(edges_in, 16)
                lo = (KB - 1) * P * P
                sp.dma_start(to[0:FULL_CH - (KB - 1) * P, KB - 1, :], flat[lo:FULL_CH * P].rearrange("(p f) -> p f", f=P)).then_inc(edges_in, 16)
                r = FULL_CH - (KB - 1) * P
                sp.dma_start(to[r:r + 1, KB - 1, 0:TAIL], flat[FULL_CH * P:N_EDGES].rearrange("(p f) -> p f", p=1)).then_inc(edges_in, 16)
            sp.dma_start(prev_i[:, 1:KB - 1, :], dst[P * P - 1:(KB - 1) * P * P - 1].rearrange("(k p f) -> p k f", p=P, f=P)).then_inc(edges_in, 16)
            sp.dma_start(prev_i[1:P, 0, :], dst[P - 1:P * P - 1].rearrange("(p f) -> p f", f=P)).then_inc(edges_in, 16)
            sp.dma_start(prev_i[0:1, 0, 1:P], dst[0:P - 1].rearrange("(p f) -> p f", p=1)).then_inc(edges_in, 16)
            sp.dma_start(prev_i[0:r, KB - 1, :], dst[lo - 1:FULL_CH * P - 1].rearrange("(p f) -> p f", f=P)).then_inc(edges_in, 16)
            sp.dma_start(prev_i[r:r + 1, KB - 1, 0:TAIL + 1], dst[FULL_CH * P - 1:N_EDGES].rearrange("(p f) -> p f", p=1)).then_inc(edges_in, 16)
            sp.wait_ge(zeroed, 1)
            for l in range(2):
                z = adst_at[l][0:E_PAD, :].rearrange("(n p e) h -> n p (e h)", n=E_PAD * HEADS // (P * SE), p=P)
                for n in range(E_PAD * HEADS // (P * SE)):
                    sp.dma_start(z[n], CBC[:, 0, :]).then_inc(setup_out, 16)
            sp.wait_ge(floats, 1)
            sp.dma_start(d_dst.rearrange("(k p) f -> p k f", p=P), dst_f).then_inc(dst_out, 16)
            sp.wait_ge(masks_made, 1)
            mk = d_mask.rearrange("(k q) h c m f -> q h m c k f", q=P // CB)
            ck = d_carry.rearrange("(k q) h c -> q h c k", q=P // CB)
            for q in range(P // CB):
                rows = slice(q * CB, q * CB + CB)
                for h in range(HEADS):
                    sp.dma_start(mk[q, h, 0], same[rows]).then_inc(setup_out, 16)
                    sp.dma_start(mk[q, h, 1], same_neg[rows]).then_inc(setup_out, 16)
                    sp.dma_start(ck[q, h, 1:HR, :], chunk_goes[rows, :]).then_inc(setup_out, 16)
            sp.dma_start(d_carry[:, :, 0:1].rearrange("b h o -> b (h o)"), head_big[0:NB, :]).then_inc(setup_out, 16)
            sp.wait_ge(turned_used, 2 * KB)
            for q in range(P // CB):
                rows = slice(q * CB, q * CB + CB)
                sp.dma_start(d_idx.rearrange("(k q) p c -> q p k c", q=P // CB)[q], src_t[:, :, rows]).then_inc(setup_out, 16)
                sp.dma_start(d_ew.rearrange("(k q) p c -> q p k c", q=P // CB)[q], prev_f[:, :, rows]).then_inc(setup_out, 16)
            sp.wait_ge(row_made, 1)
            sp.dma_start(d_row, smalli[0:NP, 0, :]).then_inc(row_out, 16)
            sp.wait_ge(row_out, 16)

            def search_load(it):
                for par in range(2):
                    if due(it):
                        sp.wait_ge(search_used[par], it)
                    sp.dma_start(q_idx[0:NP, par, :], d_row[:, bass.ds((2 * it + par) * GT, GT)]).then_inc(search_in[par], 16)
            rounds(sp, NHALF, search_load)
            sp.wait_ge(ends_made, 1)
            sp.dma_start(d_first, smalli[0:NP, 1, :]).then_inc(ends_out, 16)
            sp.dma_start(d_last, smalli[0:NP, 2, :]).then_inc(ends_out, 16)
            sp.wait_ge(ends_out, 32)
            n_setup = 2 * (E_PAD * HEADS // (P * SE)) + (P // CB) * HEADS * 3 + 1 + 2 * (P // CB)
            sp.wait_ge(setup_out, 16 * n_setup)

            def place_loads(l):
                for par in range(2):
                    sp.wait_ge(ns[l]["stored"][par], 16 * NHALF)

                def body(it):
                    for par in range(2):
                        tiles = bass.ds((2 * (it - node_before[l]) + par) * GT, GT)
                        if due(16 * GT * it):
                            sp.wait_ge(placed["sent"][par], 16 * GT * it)
                        sp.dma_start(q_idx[0:NP, par, :], d_first[:, tiles]).then_inc(placed["in_"][par], 16)
                        sp.dma_start(q_adst[0:NP, par], table[l].rearrange("(p t) f -> p t f", t=NT)[:, tiles, HID + HEADS:ROW]).then_inc(placed["in_"][par], 16)
                rounds(sp, NHALF, body, node_before[l])
                for par in range(2):
                    sp.wait_ge(placed["sent"][par], 16 * GT * NHALF * (l + 1))
                sp.wait_ge(placed["first_in"], 16 * KB * (l + 1))
                starts = adst_at[l][0:E_PAD, :].rearrange("(k p e) h -> p k (e h)", p=P, e=P)[:, :, 0:HEADS]
                sp.dma_start(starts, chunk_adst[:, l]).then_inc(placed["first_out"], 16)
                sp.wait_ge(placed["first_out"], 16 * (l + 1))

            def edge_loads(l):
                s = es[l]
                def body(it):
                    for par in range(2):
                        b = 2 * (it - before[l]) + par
                        if due(16 * CB * it):
                            sp.wait_ge(s["gathered"][par], 16 * CB * it)
                        sp.dma_start(idx[:, par, :], d_idx[b]).then_inc(s["idx_in"][par], 16)
                        if due(it):
                            sp.wait_ge(s["batch_done"][par], it)
                        sp.dma_start(mask[:, par], d_mask[b].rearrange("h c m f -> (h c) m f")).then_inc(s["loads"][par], 16)
                        if l < 2:
                            sp.dma_start(adst_in[:, par], adst_at[l][bass.ds(b * BE, BE), :].rearrange("(c p) h -> c p h", p=P)).then_inc(s["loads"][par], 16)
                            sp.dma_start(carry_mask[:, par], d_carry[bass.ds(b, 1)]).then_inc(s["loads"][par], 16)
                        else:
                            sp.dma_start(ewt[:, par, :], d_ew[b]).then_inc(s["loads"][par], 16)
                rounds(sp, HALF, body, before[l])

            def node_loads(l):
                s = ns[l]
                for par in range(2):
                    sp.wait_ge(es[l - 1]["stored"][par], 16 * (before[l - 1] + HALF))

                def body(it):
                    for par in range(2):
                        g = 2 * it + par
                        if due(it):
                            sp.wait_ge(s["used"][par], it)
                        sp.dma_start(last_in[0:NP, par, :], d_last[:, bass.ds(g * GT, GT)]).then_inc(s["in_"][par], 16)
                        if l < 3:
                            sp.dma_start(own[0:NP, par], node_rows(table[l - 1], g, ROW)).then_inc(s["in_"][par], 16)
                        else:
                            sp.dma_start(own[0:NP, par, :, 0:HID], node_rows(zdst, g, HID)).then_inc(s["in_"][par], 16)
                        if l > 1:
                            sp.dma_start(xg[0:NP, par], node_rows((x, zrow)[l - 2], g, HID)).then_inc(s["in_"][par], 16)
                rounds(sp, NHALF, body)

            place_loads(0)
            edge_loads(0)
            node_loads(1)
            place_loads(1)
            edge_loads(1)
            node_loads(2)
            for par in range(2):
                sp.wait_ge(ns[2]["stored"][par], 48 * NHALF)
            edge_loads(2)
            node_loads(3)
            for par in range(2):
                sp.wait_ge(ns[3]["stored"][par], 16 * NHALF)

        @block.gpsimd
        def _(pool):
            pool.memset(ident[:, :], 0.0).then_inc(consts, 1)
            pool.wait_ge(consts, 1)
            pool.affine_select(out=ident[:, :], in_=ident[:, :], compare_op=ALU.not_equal, fill=1.0, base=0,
                               pattern=[[-1, P]], channel_multiplier=1).then_inc(consts, 1)
            pool.iota(node[:, :], [[1, NT]], base=0, channel_multiplier=NT,
                      allow_small_or_imprecise_dtypes=True).then_inc(consts, 1)
            pool.iota(hundreds[:, :], [[NT, NP + 1]], base=0, channel_multiplier=0,
                      allow_small_or_imprecise_dtypes=True).then_inc(consts, 1)
            pool.iota(units[:, :], [[1, NT]], base=0, channel_multiplier=0,
                      allow_small_or_imprecise_dtypes=True).then_inc(consts, 1)

            def gather(to, table_ap, index, s):
                pool.indirect_dma_start(to, None, table_ap, bass.IndirectOffsetOnAxis(ap=index, axis=0)).then_inc(s, 16)

            pool.wait_ge(dst_out, 16)
            def search(it):
                for par in range(2):
                    pool.wait_ge(search_in[par], 16 * it + 16)
                    pool.nop(nofuse=True)
                    for j in range(GT):
                        gather(rows_dst[0:NP, par, j, :], d_dst, q_idx[0:NP, par, j:j + 1], search_rows[par])
            rounds(pool, NHALF, search)

            def place(l):
                s = placed
                for par in range(2):
                    pool.wait_ge(ns[l]["stored"][par], 16 * NHALF)
                for k in range(KB):
                    pool.indirect_dma_start(chunk_adst[:, l, k, :], None, table[l],
                                            bass.IndirectOffsetOnAxis(ap=chunk_first[:, k:k + 1], axis=0),
                                            element_offset=HID + HEADS).then_inc(s["first_in"], 16)

                def body(it):
                    for par in range(2):
                        pool.wait_ge(s["in_"][par], 32 * it + 32)
                        pool.nop(nofuse=True)
                        for j in range(GT):
                            pool.indirect_dma_start(adst_at[l], bass.IndirectOffsetOnAxis(ap=q_idx[0:NP, par, j:j + 1], axis=0),
                                                    q_adst[0:NP, par, j, :], None).then_inc(s["sent"][par], 16)
                rounds(pool, NHALF, body, node_before[l])

            def edge_gathers(l):
                s, tab, width = es[l], (table[0], table[1], ztable)[l], (ROW, ROW, HID)[l]
                def body(it):
                    for par in range(2):
                        if due(it):
                            pool.wait_ge(s["batch_done"][par], it)
                            pool.nop(nofuse=True)
                        pool.wait_ge(s["idx_in"][par], 16 * it + 16)
                        pool.nop(nofuse=True)
                        for c in range(CB):
                            gather(G[:, par, c, 0:width], tab, idx[:, par, c:c + 1], s["gathered"][par])
                rounds(pool, HALF, body, before[l])

            def node_gathers(l):
                s, width = ns[l], (0, ROW, ROW, HID)[l]
                for par in range(2):
                    pool.wait_ge(es[l - 1]["stored"][par], 16 * (before[l - 1] + HALF))

                def body(it):
                    for par in range(2):
                        pool.wait_ge(s["in_"][par], in_dmas(l) * (it + 1))
                        pool.nop(nofuse=True)
                        for j in range(GT):
                            gather(ends[0:NP, par, j, 0:width], result[l - 1], last_in[0:NP, par, j:j + 1], s["got"][par])
                rounds(pool, NHALF, body)

            place(0)
            edge_gathers(0)
            node_gathers(1)
            place(1)
            edge_gathers(1)
            node_gathers(2)
            for par in range(2):
                pool.wait_ge(ns[2]["stored"][par], 48 * NHALF)
            edge_gathers(2)
            node_gathers(3)

        @block.tensor
        def _(pe):
            def turn(to, frm, n=P):
                return pe.transpose(to, frm, ident[0:n, 0:n])

            pe.wait_ge(consts, 2)
            pe.wait_ge(consts_in, 16 * N_CONSTS)
            pe.wait_ge(pads, 4)
            for l in range(2):
                turn(psV[l][:, 0:P], Wx[l][:, 0:HID]).then_inc(attw, 1)
                pe.wait_ge(attw_used, 2 * l + 1)
                pe.matmul(psB[l][:, 0:2 * HEADS], wt[:, :], att[l][:, :], start=True, stop=True).then_inc(attw, 1)
            pe.wait_ge(digits, 1)
            for k in range(KB):
                pe.matmul(psC[0:NP, 0:NT], LT[:, k, 0:NP], ones[:, :], start=(k == 0), stop=False)
                mm = pe.matmul(psC[0:NP, 0:NT], hit[:, k, :], below[:, k, :], start=False, stop=(k == KB - 1))
            mm.then_inc(chunk_count, 1)

            pe.wait_ge(floats, 2)
            for k in range(KB):
                for n, frm in enumerate((src_f, ew_f)):
                    if due(2 * k + n - 1):
                        pe.wait_ge(turned_used, 2 * k + n - 1)
                    if k == 0:
                        pe.wait_ge(attw_used, 4)
                    turn(psS[n][:, 0:P], frm[:, k, :]).then_inc(turned, 1)
            def project(l, frm, n_out, weights):
                s = ns[l]
                def body(it):
                    for par in range(2):
                        if l == 0:
                            pe.wait_ge(s["in_"][par], 16 * it + 16)
                        else:
                            pe.wait_ge(s["o_relu"], 2 * it + par + 1)
                        for j in range(GT):
                            n, two = (2 * it + par) * GT + j, (par * GT + j) % 2
                            if due(n - 1):
                                pe.wait_ge(s["xt"], n - 1)
                            turn(psV[two][:, 0:NP], frm[0:NP, par, j, :], NP).then_inc(s["xt_ps"], 1)
                            pe.wait_ge(s["xt"], n + 1)
                            if due(n - 1):
                                pe.wait_ge(s["h"], n - 1)
                            if l == 2:
                                pe.matmul(psB[two][0:NP, 0:n_out], one[0:1, 0:NP], bmr[0:1, :], start=True, stop=False)
                            pe.matmul(psB[two][0:NP, 0:n_out], XT[:, two, 0:NP], weights, start=(l < 2), stop=True).then_inc(s["h_ps"], 1)
                rounds(pe, NHALF, body)

            pe.wait_ge(attw_used, 4)
            project(0, xg, ROW, Wx[0][:, :])
            pe.wait_ge(shifted, 1)
            pe.matmul(psC[0:NP, 2 * P:2 * P + 1], ident[0:NP + 1, 1:NP + 1], edge_of[0:NP + 1, 0:1], start=True, stop=True).then_inc(shifted, 1)

            def edge_pe(l):
                s, gat = es[l], l < 2
                def body(it):
                    for par in range(2):
                        b = 2 * it + par
                        if gat:
                            pe.wait_ge(s["loads"][par], 48 * it + 48)
                            pe.wait_ge(s["asrc"], b + 1)
                            turn(ps_asrc, A[:, :])
                            for h in range(HEADS):
                                mm = pe.matmul(ps_adst, put[:, h, :], adst_in[:, par, :, h], start=(h == 0), stop=(h == HEADS - 1))
                            mm.then_inc(s["logits"], 1)
                            pe.wait_ge(s["l_made"], b + 1)
                            pe.matmul(ps_row, L[:, P - 1:P], ident[:, :], start=True, stop=True).then_inc(s["l_row"], 1)
                            pe.wait_ge(s["m_made"], b + 1)
                            pe.matmul(ps_col, m_pre[:, :], one[0:1, 0:1], start=True, stop=True).then_inc(s["m_col"], 1)
                            pe.wait_ge(s["d_made"], b + 1)
                            pe.matmul(ps_row2, D[:, P - 1:P], ident[:, :], start=True, stop=True).then_inc(s["d_rows"], 1)
                            pe.wait_ge(s["d_scan"], b + 1)
                            pe.matmul(ps_col2, d_pre[:, :], one[0:1, 0:1], start=True, stop=True).then_inc(s["d_col"], 1)
                            pe.wait_ge(s["d_final"], b + 1)
                            turn(psT[:, 0:P], EX[:, 0, :])
                            turn(psC[:, 0:P], M[:, 1:P + 1])
                            turn(psC[:, P:2 * P], D[:, :]).then_inc(s["weights_t"], 1)
                            coeff = EX[:, 1, :]
                        else:
                            pe.wait_ge(s["loads"][par], 32 * it + 32)
                            coeff = mask[:, par, 1, :]

                        def results(st):
                            g = b * NS + st
                            pe.wait_ge(s["scanned"], g + 1)
                            if st >= 2 or not gat:
                                if due(g - 1):
                                    pe.wait_ge(s["r_made"], g - 1)
                            for j in range(SC):
                                tr = turn(psS[st % 2][:, j * P:(j + 1) * P], ST[:, st % 2, j * P:(j + 1) * P])
                                if st == NS - 1 and j == 0:
                                    tr.then_inc(s["batch_done"][par], 1)
                            tr.then_inc(s["s_turned"], 1)

                        for st in range(NS):
                            g = b * NS + st
                            if st >= 2 or not gat:
                                if due(g - 1):
                                    pe.wait_ge(s["c_copied"], g - 1)
                            for j in range(SC):
                                mm = pe.matmul(psB[st % 2][:, j * P:(j + 1) * P], pick[:, st * SC + j, :], coeff, start=True, stop=True)
                            mm.then_inc(s["c_spread"], 1)
                            pe.wait_ge(s["v_made"], g + 1)
                            if st >= 2 or not gat:
                                if due(g - 1):
                                    pe.wait_ge(s["scanned"], g - 1)
                            for j in range(SC):
                                tr = turn(psV[st % 2][:, j * P:(j + 1) * P], V[:, st % 2, j, :])
                            tr.then_inc(s["v_turned"], 1)
                            if st:
                                results(st - 1)
                        results(NS - 1)
                rounds(pe, HALF, body, before[l])

            pe.wait_ge(pick_made, 1)
            edge_pe(0)
            project(1, O, ROW, Wx[1][:, :])
            edge_pe(1)
            project(2, O, 2 * HID, Wz[:, :])
            edge_pe(2)

            def final_pe():
                s = ns[3]
                def body(it):
                    for par in range(2):
                        pe.wait_ge(s["o_made"], 2 * it + par + 1)
                        for j in range(GT):
                            n, two = (2 * it + par) * GT + j, (par * GT + j) % 2
                            if due(n - 1):
                                pe.wait_ge(s["xt"], n - 1)
                            turn(psV[two][:, 0:NP], xg[0:NP, par, j, :], NP)
                            turn(psV[two][:, HID:HID + NP], O[0:NP, par, j, :], NP).then_inc(s["xt_ps"], 1)
                            pe.wait_ge(s["xt"], n + 1)
                            if due(n - 1):
                                pe.wait_ge(s["hid"], n - 1)
                            pe.matmul(psB[two][:, 0:NP], U1z[:, :], XT[:, two, 0:NP], start=True, stop=False)
                            pe.matmul(psB[two][:, 0:NP], U1a[:, :], XT[:, two, HID:HID + NP], start=False, stop=True).then_inc(s["hid_ps"], 1)
                            pe.wait_ge(s["hid"], n + 1)
                            if due(n - 1):
                                pe.wait_ge(s["h"], n - 1)
                            pe.matmul(psS[two][0:NP, 0:HID], one[0:1, 0:NP], b2r[0:1, :], start=True, stop=False)
                            pe.matmul(psS[two][0:NP, 0:HID], V[:, two, 0, 0:NP], U2s[:, :], start=False, stop=True).then_inc(s["h_ps"], 1)
                rounds(pe, NHALF, body)
            final_pe()

        @block.scalar
        def _(act):
            act.wait_ge(pads, 4)
            for to, frm in const_loads:
                act.dma_start(to, frm).then_inc(consts_in, 16)

            for l in range(2):
                act.wait_ge(attw, 2 * l + 1)
                act.activation(wt[:, :], psV[l][:, 0:P], ACT.Copy).then_inc(attw_used, 1)
                act.wait_ge(attw, 2 * l + 2)
                act.activation(Wx[l][:, HID:ROW], psB[l][:, 0:2 * HEADS], ACT.Copy).then_inc(attw_used, 1)

            def project_act(l):
                s, width = ns[l], (ROW, ROW, 2 * HID)[l]
                def body(it):
                    for par in range(2):
                        if l == 0:
                            act.dma_start(xg[0:NP, par], node_rows(x, 2 * it + par, HID)).then_inc(s["in_"][par], 16)
                    for par in range(2):
                        g = 2 * it + par
                        group_act(l, it, par)
                        if due((16, 16, 48)[l] * it):
                            act.wait_ge(s["stored"][par], (16, 16, 48)[l] * it)
                        for j in range(GT):
                            n, two = g * GT + j, (par * GT + j) % 2
                            act.wait_ge(s["xt_ps"], n + 1)
                            if due(n - 1):
                                act.wait_ge(s["h_ps"], n - 1)
                            act.activation(XT[:, two, 0:NP], psV[two][:, 0:NP], ACT.Copy).then_inc(s["xt"], 1)
                            act.wait_ge(s["h_ps"], n + 1)
                            act.activation(HTt[0:NP, par, j, 0:width], psB[two][0:NP, 0:width], ACT.Copy).then_inc(s["h"], 1)
                        act.wait_ge(s["h"], g * GT + GT)
                        if l < 2:
                            act.dma_start(node_rows(table[l], g, ROW), HTt[0:NP, par, :, 0:ROW]).then_inc(s["stored"][par], 16)
                        else:
                            act.dma_start(node_rows(ztable, g, HID), HTt[0:NP, par, :, 0:HID]).then_inc(s["stored"][par], 16)
                            act.dma_start(node_rows(zdst, g, HID), HTt[0:NP, par, :, HID:2 * HID]).then_inc(s["stored"][par], 16)
                            act.dma_start(node_rows(zrow, g, HID), O[0:NP, par]).then_inc(s["stored"][par], 16)
                rounds(act, NHALF, body)

            def group_act(l, it, par):
                if l == 0:
                    return
                s = ns[l]
                g = 2 * it + par
                act.wait_ge(s["xd"], g + 1)
                act.activation(self_w[0:NP], self_x[0:NP], ACT.Exp).then_inc(s["ex"], 1)
                if l == 1:
                    act.wait_ge(s["o_made"], g + 1)
                    act.activation(O[0:NP, par], O[0:NP, par], ACT.Relu).then_inc(s["o_relu"], 1)
                else:
                    act.wait_ge(s["std_in"], g + 1)
                    act.activation(std[0:NP], mv[0:NP, :, 1], ACT.Sqrt, bias=eps[0:NP, 0:1]).then_inc(s["std_out"], 1)

            project_act(0)

            def edge_act(l):
                s, gat = es[l], l < 2
                width = ROW if gat else HID
                def body(it):
                    for par in range(2):
                        b = 2 * it + par
                        if gat:
                            act.wait_ge(s["gathered"][par], 16 * CB * (it + 1))
                            act.activation(A[:, :].rearrange("p (h c) -> p c h", h=HEADS), G[:, par, :, HID:HID + HEADS], ACT.Copy).then_inc(s["asrc"], 1)
                            act.wait_ge(s["x_made"], b + 1)
                            act.activation(k_exp[:, :], k_row[:, :], ACT.Exp)
                            act.activation(EX[:, :, :], XD[:, :, :], ACT.Exp).then_inc(s["exps"], 1)
                            act.wait_ge(s["weights_t"], b + 1)
                        if due(16 * it):
                            act.wait_ge(s["stored"][par], 16 * it)
                        if gat:
                            for n in range(2):
                                act.activation(R[:, par, :, HID + n * HEADS:HID + n * HEADS + HEADS],
                                               psC[:, (1 - n) * P:(2 - n) * P].rearrange("p (h c) -> p c h", c=CB), ACT.Copy)

                        def rows(st):
                            g = b * NS + st
                            act.wait_ge(s["s_turned"], g + 1)
                            act.activation(R[:, par, st * SC:(st + 1) * SC, 0:HID],
                                           psS[st % 2][:, :].rearrange("p (c f) -> p c f", f=HID), ACT.Copy).then_inc(s["r_made"], 1)

                        for st in range(NS):
                            g = b * NS + st
                            act.wait_ge(s["c_spread"], g + 1)
                            if st >= 2 or not gat:
                                if due(g - 1):
                                    act.wait_ge(s["scanned"], g - 1)
                            act.activation(CBC[:, st % 2, :], psB[st % 2][:, :], ACT.Copy).then_inc(s["c_copied"], 1)
                            if st:
                                rows(st - 1)
                        rows(NS - 1)
                        act.wait_ge(s["r_made"], b * NS + NS)
                        act.dma_start(result[l][bass.ds((b - 2 * before[l]) * BE, BE), :].rearrange("(c p) f -> p c f", p=P),
                                      R[:, par, :, 0:width]).then_inc(s["stored"][par], 16)
                rounds(act, HALF, body, before[l])

            edge_act(0)
            project_act(1)
            edge_act(1)
            project_act(2)
            edge_act(2)

            def final_act():
                s = ns[3]
                def body(it):
                    for par in range(2):
                        g = 2 * it + par
                        for j in range(GT):
                            n, two = g * GT + j, (par * GT + j) % 2
                            act.wait_ge(s["xt_ps"], n + 1)
                            if due(n - 1):
                                act.wait_ge(s["hid_ps"], n - 1)
                            act.activation(XT[:, two, :].rearrange("p (a n) -> p a n", a=2)[:, :, 0:NP],
                                           psV[two][:, 0:2 * HID].rearrange("p (a n) -> p a n", a=2)[:, :, 0:NP], ACT.Copy).then_inc(s["xt"], 1)
                            act.wait_ge(s["hid_ps"], n + 1)
                            if due(n - 1):
                                act.wait_ge(s["h_ps"], n - 1)
                            act.activation(V[:, two, 0, 0:NP], psB[two][:, 0:NP], ACT.Relu, bias=b1c[:, 0:1]).then_inc(s["hid"], 1)
                        act.wait_ge(s["std_in"], g + 1)
                        act.activation(std[0:NP], mv[0:NP, :, 1], ACT.Sqrt, bias=eps[0:NP, 0:1]).then_inc(s["std_out"], 1)
                        act.wait_ge(s["o_relu"], g + 1)
                        act.dma_start(node_rows(out, g, HID), HTt[0:NP, par, :, 0:HID]).then_inc(s["stored"][par], 16)
                rounds(act, NHALF, body)
            final_act()

        @block.vector
        def _(dve):
            vec = nc.vector
            n_step = [0]

            def link(ins):
                n_step[0] += 1
                ins.then_inc(dve_step, 1)
                dve.wait_ge(dve_step, n_step[0])

            vec.memset(dst_i[:, KB - 1, :], N_NODES)
            vec.memset(prev_i[:, 0, :], -1)
            vec.memset(prev_i[:, KB - 1, :], N_NODES)
            vec.memset(src_i[:, KB - 1, :], 0)
            vec.memset(ew_f[:, KB - 1, :], 0.0).then_inc(pads, 1)
            vec.memset(att[0][:, :], 0.0)
            vec.memset(bmr[:, :], 0.0)
            vec.memset(att[1][:, :], 0.0).then_inc(pads, 1)
            vec.memset(one[:, :], 1.0)
            vec.memset(ones[:, :], 1.0)
            vec.memset(eps[:, :], EPS)
            vec.memset(head_big[:, :], -BIG)
            vec.memset(k_row[:, :], -BIG)
            vec.memset(edge_of[:, :], float(N_EDGES)).then_inc(pads, 1)
            vec.memset(m_end[:, :, :], -BIG)
            vec.memset(d_end[:, :, :], 0.0).then_inc(pads, 1)
            vec.memset(CBC[:, :, :], 0.0).then_inc(zeroed, 1)

            dve.wait_ge(edges_in, 16 * 14)
            vec.tensor_copy(dst_f, dst_i).then_inc(floats, 1)
            vec.tensor_copy(prev_f, prev_i)
            link(vec.tensor_copy(src_f, src_i))
            vec.tensor_scalar(chunk_first[:, :], dst_f[:, :, 0], float(N_NODES - 1), None, ALU.min)
            link(vec.tensor_tensor(same, dst_f, prev_f, ALU.is_equal))
            vec.tensor_scalar(same_neg, same, -1.0, BIG, ALU.add, ALU.mult)
            link(vec.tensor_reduce(small[:, 2, 0:KB], same, AX_X, ALU.min))
            link(vec.tensor_scalar(chunk_goes[:, :], small[:, 2, 0:KB], -1.0, BIG, ALU.add, ALU.mult))
            vec.memset(small[:, 7, 0:1], 0.0).then_inc(masks_made, 1)
            vec.memset(small[:, 7, 1:2], 0.0).then_inc(floats, 1)

            dve.wait_ge(consts, 5)
            for k in range(KB):
                last = dst_f[:, k, P - 1:P]
                vec.tensor_scalar(LT[:, k, :], hundreds[:, :], last, 0.0, ALU.is_gt, ALU.add, accum_out=small[:, 3, k:k + 1])
            link(vec.memset(small[:, 7, 2:3], 0.0))
            link(vec.tensor_scalar(small[:, 4, 0:KB], small[:, 3, 0:KB], float(NT), float(-NT * NP), ALU.mult, ALU.add))
            link(vec.tensor_tensor(small[:, 5, 0:KB], small[:, 4, 0:KB], dst_f[:, :, P - 1], ALU.add))
            vec.tensor_tensor(hit, LT[:, :, 1:NP + 1], LT[:, :, 0:NP], ALU.subtract)
            for k in range(KB):
                step = vec.tensor_scalar(below[:, k, :], units[:, :], small[:, 5, k:k + 1], None, ALU.is_gt)
            step.then_inc(digits, 1)
            dve.wait_ge(chunk_count, 1)
            link(vec.tensor_copy(small[0:NP, 6, :], psC[0:NP, 0:NT]))
            vec.tensor_copy(smalli[0:NP, 0, :], small[0:NP, 6, :]).then_inc(row_made, 1)
            for k in range(KB):
                dve.wait_ge(turned, 2 * k + 1)
                vec.tensor_copy(src_t[:, k, :], psS[0][:, 0:P]).then_inc(turned_used, 1)
                dve.wait_ge(turned, 2 * k + 2)
                vec.tensor_copy(prev_f[:, k, :], psS[1][:, 0:P]).then_inc(turned_used, 1)
            vec.tensor_copy(pick[:, :, :].rearrange("p c (h f) -> p c h f", h=HEADS),
                            ident[:, :].rearrange("p (h c) -> p c h", h=HEADS).unsqueeze(3).to_broadcast([P, CB, HEADS, HD]))
            link(vec.memset(put[:, :, :], 0.0))
            vec.memset(ST[:, :, :], 0.0)
            for h in range(HEADS):
                step = vec.tensor_copy(put[:, h, h * CB:(h + 1) * CB], ident[0:CB, 0:CB])
            step.then_inc(pick_made, 1)

            def chain_of(s, per_round):
                count = [0]

                def start():
                    count[0] = 0

                def step(ins, it):
                    count[0] += 1
                    ins.then_inc(s["chain"], 1)
                    dve.wait_ge(s["chain"], it * per_round + count[0])

                def end():
                    assert count[0] == per_round, count[0]
                return start, step, end

            def by_node(t, group):
                return t[0:NP, bass.ds(group * GT, GT)]

            def search(it):
                for par in range(2):
                    g = 2 * it + par
                    dve.wait_ge(search_rows[par], 16 * GT * (it + 1))
                    vec.tensor_tensor(O[0:NP, par], rows_dst[0:NP, par], by_node(node, g).unsqueeze(2).to_broadcast([NP, GT, P]),
                                      ALU.is_lt).then_inc(search_step, 1)
                    dve.wait_ge(search_step, g + 1)
                    vec.tensor_reduce(by_node(edge_of, g), O[0:NP, par], AX_X, ALU.add).then_inc(search_used[par], 1)
            rounds(dve, NHALF, search)
            for par in range(2):
                dve.wait_ge(search_used[par], NHALF)
            link(vec.scalar_tensor_tensor(edge_of[0:NP, :], small[0:NP, 6, :], float(P), edge_of[0:NP, :], ALU.mult, ALU.add))
            vec.tensor_copy(small[0:NP, 0, 0:NT - 1], edge_of[0:NP, 1:NT]).then_inc(shifted, 1)
            dve.wait_ge(shifted, 2)
            link(vec.tensor_copy(small[0:NP, 0, NT - 1:NT], psC[0:NP, 2 * P:2 * P + 1]))
            link(vec.tensor_tensor(has_edge[0:NP, :], small[0:NP, 0, :], edge_of[0:NP, :], ALU.is_gt))
            vec.tensor_scalar(max_bound[0:NP, :], has_edge[0:NP, :], 2 * BIG, -BIG, ALU.mult, ALU.add)
            vec.tensor_scalar(smalli[0:NP, 2, :], small[0:NP, 0, :], -1.0, 0.0, ALU.add, ALU.max)
            link(vec.tensor_scalar(small[0:NP, 2, :], node[0:NP, :], float(E_PAD), None, ALU.add))
            link(vec.tensor_tensor(small[0:NP, 3, :], edge_of[0:NP, :], small[0:NP, 2, :], ALU.subtract))
            link(vec.tensor_tensor(small[0:NP, 3, :], small[0:NP, 3, :], has_edge[0:NP, :], ALU.mult))
            vec.tensor_tensor(smalli[0:NP, 1, :], small[0:NP, 3, :], small[0:NP, 2, :], ALU.add).then_inc(ends_made, 1)

            def flat(t):
                return t.rearrange("p h c -> p (h c)")

            def edge_dve(l):
                s, gat = es[l], l < 2
                start, step, end = chain_of(s, 24)
                def body(it):
                    start()
                    for par in range(2):
                        b = 2 * it + par
                        same01, same_big = mask[:, par, 0, :], mask[:, par, 1, :]
                        p, c = EX[:, 0, :], EX[:, 1, :]
                        if gat:
                            goes_on = flat(carry_mask[:, par])
                            dve.wait_ge(s["loads"][par], 48 * it + 48)
                            dve.wait_ge(s["logits"], b + 1)
                            step(vec.tensor_tensor_scan(T[:, :], same01, ps_adst, 0.0, ALU.mult, ALU.add), it)
                            step(vec.tensor_tensor(U[:, :], ps_asrc, T[:, :], ALU.add), it)
                            step(vec.scalar_tensor_tensor(E[:, :], U[:, :], SLOPE, U[:, :], ALU.mult, ALU.max), it)
                            vec.tensor_tensor_scan(L[:, :], same_big, E[:, :], -BIG, ALU.add, ALU.max).then_inc(s["l_made"], 1)
                            vec.tensor_copy(m_row[:, :, 0], m_end[:, :, CB])
                            dve.wait_ge(s["l_row"], b + 1)
                            step(vec.tensor_copy(m_row[:, :, 1:HR], ps_row.rearrange("p (h c) -> p h c", h=HEADS)), it)
                            step(vec.tensor_tensor_scan(flat(m_end[:, :, :]), goes_on, flat(m_row[:, :, :]), -BIG, ALU.add, ALU.max), it)
                            vec.tensor_copy(m_pre[:, :].rearrange("p (h c) -> p h c", h=HEADS), m_end[:, :, 0:CB]).then_inc(s["m_made"], 1)
                            n = HEADS * HR
                            step(vec.tensor_tensor(k_row[:, 1:n], flat(m_end[:, :, :])[:, 0:n - 1], flat(m_end[:, :, :])[:, 1:n], ALU.subtract), it)
                            vec.tensor_tensor(k_row[:, 1:n], k_row[:, 1:n], goes_on[:, 1:n], ALU.add)
                            dve.wait_ge(s["m_col"], b + 1)
                            step(vec.tensor_copy(M[:, 0:1], ps_col), it)
                            step(vec.tensor_tensor_scan(M[:, 1:P + 1], same_big, E[:, :], M[:, 0:1], ALU.add, ALU.max), it)
                            step(vec.tensor_tensor(XD[:, 1, :], M[:, 0:P], same_big, ALU.add), it)
                            vec.tensor_tensor(XD[:, 0, :], E[:, :], M[:, 1:P + 1], ALU.subtract)
                            vec.tensor_tensor(XD[:, 1, :], XD[:, 1, :], M[:, 1:P + 1], ALU.subtract).then_inc(s["x_made"], 1)
                            dve.wait_ge(s["exps"], b + 1)
                            vec.tensor_tensor_scan(D[:, :], c, p, 0.0, ALU.mult, ALU.add).then_inc(s["d_made"], 1)
                            vec.tensor_copy(d_rowv[:, :, 0], d_end[:, :, CB])
                            dve.wait_ge(s["d_rows"], b + 1)
                            step(vec.tensor_copy(d_rowv[:, :, 1:HR], ps_row2.rearrange("p (h c) -> p h c", h=HEADS)), it)
                            step(vec.tensor_tensor_scan(flat(d_end[:, :, :]), k_exp[:, :], flat(d_rowv[:, :, :]), 0.0, ALU.mult, ALU.add), it)
                            vec.tensor_copy(d_pre[:, :].rearrange("p (h c) -> p h c", h=HEADS), d_end[:, :, 0:CB]).then_inc(s["d_scan"], 1)
                            dve.wait_ge(s["d_col"], b + 1)
                            step(vec.tensor_copy(D0[:, :], ps_col2), it)
                            vec.tensor_tensor_scan(D[:, :], c, p, D0[:, 0:1], ALU.mult, ALU.add).then_inc(s["d_final"], 1)
                            dve.wait_ge(s["weights_t"], b + 1)
                        else:
                            dve.wait_ge(s["loads"][par], 32 * it + 32)
                            dve.wait_ge(s["gathered"][par], 16 * CB * (it + 1))

                        def values(st):
                            if st >= 2 or not gat:
                                if due(b * NS + st - 1):
                                    dve.wait_ge(s["v_turned"], b * NS + st - 1)
                            rows = G[:, par, st * SC:(st + 1) * SC, 0:HID]
                            if gat:
                                weights = psT[:, 0:P].rearrange("p (h c) -> p c h", h=HEADS)[:, st * SC:(st + 1) * SC, :]
                                ins = vec.tensor_tensor(V[:, st % 2].rearrange("p c (h f) -> p c h f", h=HEADS),
                                                        rows.rearrange("p c (h f) -> p c h f", h=HEADS),
                                                        weights.unsqueeze(3).to_broadcast([P, SC, HEADS, HD]), ALU.mult)
                            else:
                                for j in range(SC):
                                    ins = vec.scalar_tensor_tensor(V[:, st % 2, j, :], wwb[:, :], ewt[:, par, st * SC + j:st * SC + j + 1],
                                                                   rows[:, j, :], ALU.mult, ALU.add)
                            ins.then_inc(s["v_made"], 1)

                        values(0)
                        for st in range(NS):
                            g = b * NS + st
                            if st + 1 < NS:
                                values(st + 1)
                            dve.wait_ge(s["c_copied"], g + 1)
                            dve.wait_ge(s["v_turned"], g + 1)
                            if due(g):
                                dve.wait_ge(s["scanned"], g)
                            if st >= 2 or not gat:
                                if due(g - 1):
                                    dve.wait_ge(s["s_turned"], g - 1)
                            vec.tensor_tensor_scan(ST[:, st % 2, :], CBC[:, st % 2, :], psV[st % 2][:, :], ST[:, 1 - st % 2, SE - 1:SE],
                                                   ALU.mult if gat else ALU.add, ALU.add if gat else ALU.max).then_inc(s["scanned"], 1)
                    if gat:
                        end()
                rounds(dve, HALF, body, before[l])

            def layernorm_start(l, rows, it, step):
                for j in range(GT):
                    ins = vec.bn_stats(stats[0:NP, j, :], rows[:, j, :])
                step(ins, it)
                dve.nop(nofuse=True)
                for j in range(GT):
                    ins = vec.bn_aggr(mv[0:NP, j, :], stats[0:NP, j, :])
                ins.then_inc(ns[l]["std_in"], 1)

            def layernorm_end(l, rows, g, it, step):
                dve.wait_ge(ns[l]["std_out"], g + 1)
                step(vec.reciprocal(rstd[0:NP, :], std[0:NP, :]), it)
                for j in range(GT):
                    ins = vec.tensor_scalar(rows[:, j, :], rows[:, j, :], mv[0:NP, j, 0:1], rstd[0:NP, j:j + 1], ALU.subtract, ALU.mult)
                ins.then_inc(ns[l]["o_relu"], 1)

            def node_dve(l):
                s = ns[l]
                start, step, end = chain_of(s, 20 if l == 1 else 26)
                def body(it):
                    start()
                    for par in range(2):
                        g = 2 * it + par
                        e, o = ends[0:NP, par], own[0:NP, par]
                        dve.wait_ge(s["in_"][par], in_dmas(l) * (it + 1))
                        dve.wait_ge(s["got"][par], 16 * GT * (it + 1))
                        step(vec.tensor_tensor(self_e[0:NP], o[:, :, HID:HID + HEADS], o[:, :, HID + HEADS:ROW], ALU.add), it)
                        step(vec.scalar_tensor_tensor(self_e[0:NP], self_e[0:NP], SLOPE, self_e[0:NP], ALU.mult, ALU.max), it)
                        step(vec.tensor_tensor(self_x[0:NP, 0], e[:, :, HID + HEADS:ROW],
                                               by_node(max_bound, g).unsqueeze(2).to_broadcast([NP, GT, HEADS]), ALU.min), it)
                        step(vec.tensor_tensor(den[0:NP], self_x[0:NP, 0], self_e[0:NP], ALU.max), it)
                        vec.tensor_tensor(self_x[0:NP, 0], self_x[0:NP, 0], den[0:NP], ALU.subtract)
                        vec.tensor_tensor(self_x[0:NP, 1], self_e[0:NP], den[0:NP], ALU.subtract).then_inc(s["xd"], 1)
                        dve.wait_ge(s["ex"], g + 1)
                        step(vec.tensor_tensor(den[0:NP], e[:, :, HID:HID + HEADS], self_w[0:NP, 0], ALU.mult), it)
                        step(vec.tensor_tensor(den[0:NP], den[0:NP], self_w[0:NP, 1], ALU.add), it)
                        step(vec.tensor_scalar(den[0:NP], den[0:NP], 1.0e-16, None, ALU.add), it)
                        step(vec.reciprocal(den[0:NP], den[0:NP]), it)
                        vec.tensor_tensor(self_w[0:NP, 0], self_w[0:NP, 0], den[0:NP], ALU.mult)
                        step(vec.tensor_tensor(self_w[0:NP, 1], self_w[0:NP, 1], den[0:NP], ALU.mult), it)
                        for t, n in ((e, 0), (o, 1)):
                            rows = t[:, :, 0:HID].rearrange("p t (h f) -> p t h f", h=HEADS)
                            ins = vec.tensor_tensor(rows, rows, self_w[0:NP, n].unsqueeze(3).to_broadcast([NP, GT, HEADS, HD]), ALU.mult)
                        step(ins, it)
                        if due((g - 1) * GT):
                            dve.wait_ge(s["xt_ps"], (g - 1) * GT)
                        if l == 2:
                            if due(48 * it):
                                dve.wait_ge(s["stored"][par], 48 * it)
                        vec.tensor_tensor(O[0:NP, par], e[:, :, 0:HID], o[:, :, 0:HID], ALU.add).then_inc(s["free"][par], 1)
                        dve.wait_ge(s["free"][par], it + 1)
                        biased = vec.tensor_tensor(O[0:NP, par], O[0:NP, par],
                                                   bias[l - 1][0:NP, :].unsqueeze(1).to_broadcast([NP, GT, HID]), ALU.add)
                        if l == 1:
                            biased.then_inc(s["o_made"], 1)
                            dve.wait_ge(s["o_made"], g + 1)
                            vec.memset(small[0:NP, 7, 5:6], 0.0).then_inc(s["used"][par], 1)
                        else:
                            step(biased, it)
                            vec.scalar_tensor_tensor(O[0:NP, par].rearrange("p t f -> p (t f)"), O[0:NP, par].rearrange("p t f -> p (t f)"), 0.0,
                                                     xg[0:NP, par].rearrange("p t f -> p (t f)"), ALU.max, ALU.add).then_inc(s["used"][par], 1)
                            dve.wait_ge(s["used"][par], it + 1)
                            layernorm_start(l, O[0:NP, par], it, step)
                            layernorm_end(l, O[0:NP, par], g, it, step)
                    end()
                rounds(dve, NHALF, body)

            def final_dve():
                s = ns[3]
                start, step, end = chain_of(s, 8)
                def body(it):
                    start()
                    for par in range(2):
                        g = 2 * it + par
                        dve.wait_ge(s["in_"][par], in_dmas(3) * (it + 1))
                        dve.wait_ge(s["got"][par], 16 * GT * (it + 1))
                        if due((g - 1) * GT):
                            dve.wait_ge(s["xt_ps"], (g - 1) * GT)
                        step(vec.tensor_tensor(O[0:NP, par], ends[0:NP, par, :, 0:HID], own[0:NP, par, :, 0:HID], ALU.add), it)
                        vec.tensor_tensor(O[0:NP, par], O[0:NP, par], by_node(has_edge, g).unsqueeze(2).to_broadcast([NP, GT, HID]),
                                          ALU.mult).then_inc(s["o_made"], 1)
                        if due(16 * it):
                            dve.wait_ge(s["stored"][par], 16 * it)
                        y = HTt[0:NP, par, :, 0:HID]
                        for j in range(GT):
                            dve.wait_ge(s["h_ps"], g * GT + j + 1)
                            vec.tensor_tensor(y[:, j, :], psS[(par * GT + j) % 2][0:NP, 0:HID], xg[0:NP, par, j, :], ALU.add).then_inc(s["h"], 1)
                        dve.wait_ge(s["h"], g * GT + GT)
                        step(vec.memset(small[0:NP, 7, 6:7], 0.0), it)
                        layernorm_start(3, y, it, step)
                        layernorm_end(3, y, g, it, step)
                        vec.memset(small[0:NP, 7, 7:8], 0.0).then_inc(s["used"][par], 1)
                    end()
                rounds(dve, NHALF, body)

            edge_dve(0)
            node_dve(1)
            edge_dve(1)
            node_dve(2)
            edge_dve(2)
            final_dve()


_INS = ["x", "src", "dst", "edge_weight", "L0_gnn_W1", "L0_gnn_att_src1", "L0_gnn_att_dst1", "L0_gnn_bias1", "L0_gnn_W2",
        "L0_gnn_att_src2", "L0_gnn_att_dst2", "L0_gnn_bias2", "L1_gnn_Wm", "L1_gnn_bm", "L1_gnn_W1", "L1_gnn_b1", "L1_gnn_W2", "L1_gnn_b2"]


def kernel(**inputs):
    import numpy as np
    import concourse.bacc as bacc
    from concourse.bass_utils import run_bass_kernel_spmd

    nc = bacc.Bacc("TRN2", target_bir_lowering=False, num_devices=1)
    arrays, args = {}, []
    for name in _INS:
        a = np.ascontiguousarray(inputs[name])
        arrays[f"in_{name}"] = a
        args.append(nc.dram_tensor(f"in_{name}", a.shape, mybir.dt.from_np(a.dtype), kind="ExternalInput").ap())
    args.append(nc.dram_tensor("out", (N_NODES, HID), F32, kind="ExternalOutput").ap())
    gnn_program(nc, *args)
    return run_bass_kernel_spmd(nc, [arrays], core_ids=[0]).results[0]["out"]
```

```python
from contextlib import ExitStack

import concourse.bass as bass
from concourse import mybir

F32 = mybir.dt.float32
I32 = mybir.dt.int32
ALU = mybir.AluOpType
ACT = mybir.ActivationFunctionType
AX_X = mybir.AxisListType.X

P = 128
HID = 128
HEADS = 4
HD = HID // HEADS
N_NODES = 12500
N_EDGES = 212500
NP = 125
NT = N_NODES // NP
GT = 10
NG = NT // GT
CB = 32
BE = CB * P
NB = -(-N_EDGES // BE)
NCH = NB * CB
KB = NCH // P
E_PAD = NCH * P
FULL_CH = N_EDGES // P
TAIL = N_EDGES - FULL_CH * P
SC = 4
NS = CB // SC
PARTS = 4
SE = SC * P
ROW = HID + 2 * HEADS
BT = 512 // HID
BANKS = [(a, min(a + BT, GT)) for a in range(0, GT, BT)]
BIG = 1.0e30
SLOPE = 0.2
EPS = 1.0e-5
HR = CB + 1
assert NP * NT == N_NODES and NG * GT == NT and NB % 2 == 0 and NG % 2 == 0 and HEADS * CB == P
assert len(BANKS) <= 3 and GT % 2 == 0
assert KB * P == NCH and FULL_CH // P == KB - 1


def due(value):
    return not isinstance(value, int) or value > 0


def rounds(eng, count, body, done=0, peel=1, unroll=1):
    for it in range(done, done + peel):
        body(it)
    assert (done + peel) % unroll == 0 and (done + count) % unroll == 0
    with eng.Fori((done + peel) // unroll, (done + count) // unroll) as turn:
        for n in range(unroll):
            body(turn * unroll + n if unroll > 1 else turn)


def gnn_program(nc, x, src, dst, edge_weight, W_1, att_src_1, att_dst_1, bias_1, W_2, att_src_2, att_dst_2,
                bias_2, Wm, bm, U1, b1, U2, b2, out):
    with ExitStack() as ctx:
        def sb(name, shape, dt=F32):
            return ctx.enter_context(nc.sbuf_tensor(name, shape, dt))

        def sem(name):
            return ctx.enter_context(nc.semaphore(name))

        def dram(name, shape, dt=F32):
            return nc.dram_tensor(name, shape, dt).ap()

        ctx.enter_context(nc.allow_non_contiguous_dma(reason="small index and weight layouts"))

        table = [dram(f"table{l}", [N_NODES, ROW]) for l in range(2)]
        ztable = dram("ztable", [N_NODES, HID])
        zdst = dram("zdst", [N_NODES, HID])
        zrow = dram("zrow", [N_NODES, HID])
        result = [dram(f"result{l}", [E_PAD, w]) for l, w in enumerate((ROW, ROW, HID))]
        adst_at = [dram(f"adst_at{l}", [E_PAD + N_NODES, HEADS]) for l in range(2)]
        d_idx = dram("d_idx", [NB, P, CB], I32)
        d_ew = dram("d_ew", [NB, P, CB])
        d_mask = dram("d_mask", [NB, CB, 2, P])
        d_carry = dram("d_carry", [NB, HR])
        d_dst = dram("d_dst", [NCH, P])
        d_first = dram("d_first", [NP, NT], I32)
        d_last = dram("d_last", [NP, NT], I32)

        G = sb("G", [P, 2, CB, ROW])
        R = sb("R", [P, 2, CB, ROW])
        pick = sb("pick", [P, CB, HID])
        V = sb("V", [P, 2, SC, HID])
        CBC = sb("CBC", [P, 2, SE])
        ST = sb("ST", [P, 2, SE])
        idx = sb("idx", [P, 2, CB], I32)
        mask = sb("mask", [P, 2, 2, P])
        adst_in = sb("adst_in", [CB, 2, P, HEADS])
        carry_mask = sb("carry_mask", [1, 2, HEADS, HR])
        ewt = sb("ewt", [P, 2, CB])
        A = sb("A", [P, P])
        T = sb("T", [P, P])
        U = sb("U", [P, P])
        E = sb("E", [P, P])
        L = sb("L", [P, P])
        M = sb("M", [P, P + 1])
        XD = sb("XD", [P, 2, P])
        EX = sb("EX", [P, 2, P])
        D = sb("D", [P, P])
        D0 = sb("D0", [P, 1])
        m_row = sb("m_row", [1, HEADS, HR])
        m_end = sb("m_end", [1, HEADS, HR])
        k_row = sb("k_row", [1, HEADS * HR])
        k_exp = sb("k_exp", [1, HEADS * HR])
        m_pre = sb("m_pre", [1, P])
        d_pre = sb("d_pre", [1, P])
        d_rowv = sb("d_rowv", [1, HEADS, HR])
        d_end = sb("d_end", [1, HEADS, HR])
        ident = sb("ident", [P, P])
        put = sb("put", [CB, HEADS, P])
        one = sb("one", [1, P])
        ones = sb("ones", [P, NT])
        node = sb("node", [P, NT])
        edge_of = sb("edge_of", [P, NT])
        has_edge = sb("has_edge", [P, NT])
        max_bound = sb("max_bound", [P, NT])
        Wx = [sb(f"Wx{l}", [P, ROW]) for l in range(2)]
        Wz = sb("Wz", [P, 2 * HID])
        att = [sb(f"att{l}", [P, 2 * HEADS]) for l in range(2)]
        wt = sb("wt", [P, HID])
        U1z = sb("U1z", [P, HID])
        U1a = sb("U1a", [P, HID])
        U2s = sb("U2s", [P, HID])
        b1c = sb("b1c", [P, 1])
        b2r = sb("b2r", [P, HID])
        bias1c = sb("bias1c", [P, 1])
        bias2r = sb("bias2r", [P, HID])
        bmr = sb("bmr", [1, HID])
        wwb = sb("wwb", [P, HID])
        eps = sb("eps", [P, 1])
        chunk_first = sb("chunk_first", [P, KB], I32)
        chunk_adst = sb("chunk_adst", [P, 2, KB, HEADS])
        q_idx = sb("q_idx", [P, 2, GT], I32)
        q_adst = sb("q_adst", [P, 2, GT, HEADS])
        last_in = sb("last_in", [P, 2, GT], I32)
        ends = sb("ends", [P, 2, GT, ROW])
        own = sb("own", [P, 2, GT, ROW])
        O = sb("O", [P, 2, GT, HID])
        xg = sb("xg", [P, 2, GT, HID])
        XT = sb("XT", [P, 2, 2 * HID])
        HTt = sb("HTt", [P, 2, GT, 2 * HID])
        self_e = sb("self_e", [P, GT, HEADS])
        self_w = sb("self_w", [P, 2, GT, HEADS])
        self_x = sb("self_x", [P, 2, GT, HEADS])
        den = sb("den", [P, GT, HEADS])
        stats = sb("stats", [P, GT, 6])
        mv = sb("mv", [P, GT, 2])
        std = sb("std", [P, GT])
        rstd = sb("rstd", [P, GT])

        room = R[:, :, :, :].rearrange("p a c f -> p (a c f)")
        room2 = G[:, :, :, :].rearrange("p a c f -> p (a c f)")

        def part(r, n, dt=F32):
            v = r[:, n * NCH:(n + 1) * NCH]
            return (v if dt == F32 else v.bitcast(dt)).rearrange("p (k f) -> p k f", k=KB)

        dst_i, prev_i, src_i = (part(room, n, I32) for n in range(3))
        dst_f, prev_f = part(room, 3), part(room, 4)
        src_f, same, same_neg, ew_f = (part(room2, n) for n in range(4))
        src_t = part(room2, 4, I32)
        LT = pick[:, :, :].rearrange("p c f -> p (c f)")[:, 0:KB * (NP + 1)].rearrange("p (k f) -> p k f", k=KB)
        hit = room[:, 0:KB * NP].rearrange("p (k f) -> p k f", k=KB)
        below = own[:, :, :, :].rearrange("p a t f -> p (a t f)")[:, 0:KB * NT].rearrange("p (k f) -> p k f", k=KB)
        rows_dst = ends[:, :, :, 0:P]
        small = sb("small", [P, 8, NT])
        smalli = sb("smalli", [P, 3, NT], I32)
        hundreds = sb("hundreds", [P, NP + 1])
        units = sb("units", [P, NT])
        chunk_goes = sb("chunk_goes", [P, KB])
        head_big = sb("head_big", [P, HEADS])

        def pb(name):
            return ctx.enter_context(nc.psum_tensor(name, [P, 512], F32))

        psV = [pb(f"psV{i}") for i in range(2)]
        psB = [pb(f"psB{i}") for i in range(2)]
        psS = [pb(f"psS{i}") for i in range(2)]
        psC = pb("psC")
        psT = pb("psT")
        row_bank = [psS[0], psS[1], psC]
        ps_asrc, ps_adst = psC[:, 0:P], psC[:, P:2 * P]
        ps_row, ps_row2 = psC[0:1, 2 * P:3 * P], psC[0:1, 3 * P:4 * P]
        ps_col, ps_col2 = psT[:, 3 * P:3 * P + 1], psT[:, 3 * P + 2:3 * P + 3]

        pads = sem("pads")
        dst_in = sem("dst_in")
        edges_in = sem("edges_in")
        consts_in = sem("consts_in")
        dst_out = sem("dst_out")
        consts = sem("consts")
        dve_step = sem("dve_step")
        floats = sem("floats")
        masks_made = sem("masks_made")
        setup_out = sem("setup_out")
        turned = sem("turned")
        turned_used = sem("turned_used")
        zeroed = sem("zeroed")
        digits = sem("digits")
        chunk_count = sem("chunk_count")
        shifted = sem("shifted")
        ends_made = sem("ends_made")
        ends_out = sem("ends_out")
        attw = sem("attw")
        attw_used = sem("attw_used")
        pick_made = sem("pick_made")
        search_step = sem("search_step")
        search_in = [sem(f"search_in{i}") for i in range(2)]
        search_rows = [sem(f"search_rows{i}") for i in range(2)]

        def phase_sems(tag, pairs, singles):
            named = {name: [sem(f"{tag}_{name}_{i}") for i in range(2)] for name in pairs.split()}
            named.update({name: sem(f"{tag}_{name}") for name in singles.split()})
            return named

        gat_only = "asrc logits l_made l_row m_made m_col x_made exps d_made d_rows d_scan d_col d_final weights_t chain "
        steps = "v_made v_turned c_spread c_copied scanned s_turned r_made"
        pairs = "idx_in loads gathered batch_done stored"
        gat = phase_sems("gat", pairs, gat_only + steps)
        es = [gat, gat, phase_sems("max", pairs, steps)]
        placed = phase_sems("place", "in_ sent", "first_in first_out")
        after_gat = "chain xd ex "
        ns = [phase_sems(f"node{l}", "in_ stored" + ("", " got", " got used", " got used z_in z_used")[l],
                   ("", after_gat + "o_made ", after_gat + "o_normed std_in std_out ", "chain o_made o_normed std_in std_out hid_ps hid ")[l] +
                   "xt_ps xt h_ps h") for l in range(4)]

        def spread(v):
            return v.rearrange("(a n) -> a n", a=1).to_broadcast([P, HID])

        const_loads = [(Wx[0][:, 0:HID], W_1), (Wx[1][:, 0:HID], W_2), (Wz[:, 0:HID], Wm[HID:2 * HID, :]), (Wz[:, HID:2 * HID], Wm[0:HID, :]),
                       (wwb[:, :], Wm[2 * HID:2 * HID + 1, :].to_broadcast([P, HID])), (bmr[:, :], bm.rearrange("(a n) -> a n", a=1)),
                       (U1z[:, :], U1[0:HID, :]), (U1a[:, :], U1[HID:2 * HID, :]), (U2s[:, :], U2),
                       (b1c[:, :], b1.rearrange("(n a) -> n a", a=1)), (b2r[:, :], spread(b2)),
                       (bias1c[:, :], bias_1.rearrange("(n a) -> n a", a=1)), (bias2r[:, :], spread(bias_2))]
        for l, pair in enumerate(((att_src_1, att_dst_1), (att_src_2, att_dst_2))):
            for n, a in enumerate(pair):
                for h in range(HEADS):
                    col = n * HEADS + h
                    const_loads.append((att[l][h * HD:(h + 1) * HD, col:col + 1], a[h:h + 1, :].rearrange("a f -> f a")))
        N_CONSTS = len(const_loads)

        def in_dmas(l):
            return 16 * (3 if l == 2 else 2)

        block = ctx.enter_context(nc.Block())
        HALF = NB // 2
        NHALF = NG // 2
        before = [0, HALF, 0]
        node_before = [0, NHALF]

        def node_rows(t, group, width):
            return t.rearrange("(p t) f -> p t f", t=NT)[:, bass.ds(group * GT, GT), 0:width]

        @block.sync
        def _(sp):
            sp.wait_ge(pads, 4)
            for flat, to, landed in ((dst, dst_i, dst_in), (src, src_i, edges_in), (edge_weight, ew_f, edges_in)):
                sp.dma_start(to[:, 0:KB - 1, :], flat[0:(KB - 1) * P * P].rearrange("(k p f) -> p k f", p=P, f=P)).then_inc(landed, 16)
                lo = (KB - 1) * P * P
                sp.dma_start(to[0:FULL_CH - (KB - 1) * P, KB - 1, :], flat[lo:FULL_CH * P].rearrange("(p f) -> p f", f=P)).then_inc(landed, 16)
                r = FULL_CH - (KB - 1) * P
                sp.dma_start(to[r:r + 1, KB - 1, 0:TAIL], flat[FULL_CH * P:N_EDGES].rearrange("(p f) -> p f", p=1)).then_inc(landed, 16)
            sp.dma_start(prev_i[:, 1:KB - 1, :], dst[P * P - 1:(KB - 1) * P * P - 1].rearrange("(k p f) -> p k f", p=P, f=P)).then_inc(edges_in, 16)
            sp.dma_start(prev_i[1:P, 0, :], dst[P - 1:P * P - 1].rearrange("(p f) -> p f", f=P)).then_inc(edges_in, 16)
            sp.dma_start(prev_i[0:1, 0, 1:P], dst[0:P - 1].rearrange("(p f) -> p f", p=1)).then_inc(edges_in, 16)
            sp.dma_start(prev_i[0:r, KB - 1, :], dst[lo - 1:FULL_CH * P - 1].rearrange("(p f) -> p f", f=P)).then_inc(edges_in, 16)
            sp.dma_start(prev_i[r:r + 1, KB - 1, 0:TAIL + 1], dst[FULL_CH * P - 1:N_EDGES].rearrange("(p f) -> p f", p=1)).then_inc(edges_in, 16)
            sp.wait_ge(floats, 1)
            sp.dma_start(d_dst.rearrange("(k p) f -> p k f", p=P), dst_f).then_inc(dst_out, 16)
            sp.wait_ge(masks_made, 1)
            mk = d_mask.rearrange("(k q) c m f -> q m c k f", q=P // CB)
            ck = d_carry.rearrange("(k q) c -> q c k", q=P // CB)
            for q in range(P // CB):
                rows = slice(q * CB, q * CB + CB)
                sp.dma_start(mk[q, 0], same[rows]).then_inc(setup_out, 16)
                sp.dma_start(mk[q, 1], same_neg[rows]).then_inc(setup_out, 16)
                sp.dma_start(ck[q, 1:HR, :], chunk_goes[rows, :]).then_inc(setup_out, 16)
            sp.dma_start(d_carry[:, 0:1], head_big[0:NB, 0:1]).then_inc(setup_out, 16)
            sp.wait_ge(zeroed, 1)
            for l in range(2):
                n = E_PAD * HEADS // (P * SE)
                sp.dma_start(adst_at[l][0:E_PAD, :].rearrange("(p n e) h -> p n (e h)", p=P, n=n),
                             CBC[:, 0:1, :].to_broadcast([P, n, SE])).then_inc(setup_out, 16)
            sp.wait_ge(turned_used, 2 * KB)
            for q in range(P // CB):
                rows = slice(q * CB, q * CB + CB)
                sp.dma_start(d_idx.rearrange("(k q) p c -> q p k c", q=P // CB)[q], src_t[:, :, rows]).then_inc(setup_out, 16)
                sp.dma_start(d_ew.rearrange("(k q) p c -> q p k c", q=P // CB)[q], prev_f[:, :, rows]).then_inc(setup_out, 16)
            sp.wait_ge(ends_made, 1)
            sp.dma_start(d_first, smalli[0:NP, 1, :]).then_inc(ends_out, 16)
            sp.dma_start(d_last, smalli[0:NP, 2, :]).then_inc(ends_out, 16)
            sp.wait_ge(ends_out, 32)
            n_setup = (P // CB) * 3 + 1 + 2 + 2 * (P // CB)
            sp.wait_ge(setup_out, 16 * n_setup)

            def idx_load(l, it, par):
                indices, gathered = d_idx[2 * (it - before[l]) + par], 16 * CB * it
                if due(gathered):
                    sp.wait_ge(es[l]["gathered"][par], gathered)
                sp.dma_start(idx[:, par, :], indices).then_inc(es[l]["idx_in"][par], 16)

            def place_loads(l):
                def body(it):
                    for par in range(2):
                        tiles = bass.ds((2 * (it - node_before[l]) + par) * GT, GT)
                        table_rows, sent = 16 * (it - node_before[l]) + 16, 16 * GT * it
                        sp.wait_ge(ns[l]["stored"][par], table_rows)
                        sp.nop(nofuse=True)
                        if due(sent):
                            sp.wait_ge(placed["sent"][par], sent)
                        sp.dma_start(q_idx[0:NP, par, :], d_first[:, tiles]).then_inc(placed["in_"][par], 16)
                        sp.dma_start(q_adst[0:NP, par], table[l].rearrange("(p t) f -> p t f", t=NT)[:, tiles, HID + HEADS:ROW]).then_inc(placed["in_"][par], 16)
                rounds(sp, NHALF, body, node_before[l])
                for par in range(2):
                    idx_load(l, before[l], par)
                for par in range(2):
                    sp.wait_ge(placed["sent"][par], 16 * GT * NHALF * (l + 1))
                sp.wait_ge(placed["first_in"], 16 * KB * (l + 1))
                starts = adst_at[l][0:E_PAD, :].rearrange("(k p e) h -> p k (e h)", p=P, e=P)[:, :, 0:HEADS]
                sp.dma_start(starts, chunk_adst[:, l]).then_inc(placed["first_out"], 16)
                sp.wait_ge(placed["first_out"], 16 * (l + 1))

            def edge_loads(l):
                s, width = es[l], ROW if l < 2 else HID

                def results_out(it, par):
                    b = 2 * it + par
                    rows = result[l][bass.ds((b - 2 * before[l]) * BE, BE), :].rearrange("(c p) f -> p c f", p=P)
                    for n in range(PARTS):
                        cs = slice(n * CB // PARTS, (n + 1) * CB // PARTS)
                        sp.wait_ge(s["r_made"], b * NS + (n + 1) * NS // PARTS)
                        sp.dma_start(rows[:, cs], R[:, par, cs, 0:width]).then_inc(s["stored"][par], 16)

                def body(it):
                    first = isinstance(it, int) and it == before[l]
                    for par in range(2):
                        b = 2 * (it - before[l]) + par
                        if not (first and l < 2):
                            idx_load(l, it, par)
                        if not first:
                            results_out(it - 1, par)
                        if due(it):
                            sp.wait_ge(s["batch_done"][par], it)
                        for h in range(HEADS):
                            sp.dma_start(mask[h * CB:(h + 1) * CB, par], d_mask[b]).then_inc(s["loads"][par], 16)
                        if l < 2:
                            sp.dma_start(adst_in[:, par], adst_at[l][bass.ds(b * BE, BE), :].rearrange("(c p) h -> c p h", p=P)).then_inc(s["loads"][par], 16)
                            sp.dma_start(carry_mask[:, par], d_carry[bass.ds(b, 1)].unsqueeze(1).to_broadcast([1, HEADS, HR])).then_inc(s["loads"][par], 16)
                        else:
                            sp.dma_start(ewt[:, par, :], d_ew[b]).then_inc(s["loads"][par], 16)
                rounds(sp, HALF, body, before[l])
                for par in range(2):
                    results_out(before[l] + HALF - 1, par)

            def node_loads(l):
                s = ns[l]
                def body(it):
                    for par in range(2):
                        g = 2 * it + par
                        if due(it):
                            if l == 1:
                                sp.wait_ge(s["o_made"], g - 1)
                            else:
                                sp.wait_ge(s["used"][par], it)
                        sp.dma_start(last_in[0:NP, par, :], d_last[:, bass.ds(g * GT, GT)]).then_inc(s["in_"][par], 16)
                        if l < 3:
                            sp.dma_start(own[0:NP, par], node_rows(table[l - 1], g, ROW)).then_inc(s["in_"][par], 16)
                        else:
                            sp.dma_start(own[0:NP, par, :, 0:HID], node_rows(zdst, g, HID)).then_inc(s["in_"][par], 16)
                        if l == 2:
                            sp.dma_start(xg[0:NP, par], node_rows(x, g, HID)).then_inc(s["in_"][par], 16)
                        if l == 3:
                            if due(it):
                                sp.wait_ge(s["z_used"][par], it)
                            sp.dma_start(xg[0:NP, par], node_rows(zrow, g, HID)).then_inc(s["z_in"][par], 16)
                rounds(sp, NHALF, body)

            place_loads(0)
            edge_loads(0)
            node_loads(1)
            place_loads(1)
            edge_loads(1)
            node_loads(2)
            edge_loads(2)
            for par in range(2):
                sp.wait_ge(ns[2]["stored"][par], 48 * NHALF)
            node_loads(3)
            for par in range(2):
                sp.wait_ge(ns[3]["stored"][par], 16 * NHALF)

        @block.gpsimd
        def _(pool):
            pool.memset(ident[:, :], 0.0).then_inc(consts, 1)
            pool.wait_ge(consts, 1)
            pool.affine_select(out=ident[:, :], in_=ident[:, :], compare_op=ALU.not_equal, fill=1.0, base=0,
                               pattern=[[-1, P]], channel_multiplier=1).then_inc(consts, 1)
            pool.iota(node[:, :], [[1, NT]], base=0, channel_multiplier=NT,
                      allow_small_or_imprecise_dtypes=True).then_inc(consts, 1)
            pool.iota(hundreds[:, :], [[NT, NP + 1]], base=0, channel_multiplier=0,
                      allow_small_or_imprecise_dtypes=True).then_inc(consts, 1)
            pool.iota(units[:, :], [[1, NT]], base=0, channel_multiplier=0,
                      allow_small_or_imprecise_dtypes=True).then_inc(consts, 1)

            def gather(to, table_ap, index, s):
                pool.indirect_dma_start(to, None, table_ap, bass.IndirectOffsetOnAxis(ap=index, axis=0)).then_inc(s, 16)

            pool.wait_ge(dst_out, 16)
            def search(it):
                for par in range(2):
                    pool.wait_ge(search_in[par], it + 1)
                    pool.nop(nofuse=True)
                    for j in range(GT):
                        gather(rows_dst[0:NP, par, j, :], d_dst, q_idx[0:NP, par, j:j + 1], search_rows[par])
            rounds(pool, NHALF, search)

            def place(l):
                s = placed

                def chunk_starts():
                    for par in range(2):
                        pool.wait_ge(ns[l]["stored"][par], 16 * NHALF)
                    for k in range(KB):
                        pool.indirect_dma_start(chunk_adst[:, l, k, :], None, table[l],
                                                bass.IndirectOffsetOnAxis(ap=chunk_first[:, k:k + 1], axis=0),
                                                element_offset=HID + HEADS).then_inc(s["first_in"], 16)

                def body(it):
                    for par in range(2):
                        pool.wait_ge(s["in_"][par], 32 * it + 32)
                        pool.nop(nofuse=True)
                        for j in range(GT):
                            pool.indirect_dma_start(adst_at[l], bass.IndirectOffsetOnAxis(ap=q_idx[0:NP, par, j:j + 1], axis=0),
                                                    q_adst[0:NP, par, j, :], None).then_inc(s["sent"][par], 16)

                if l == 0:
                    chunk_starts()
                rounds(pool, NHALF, body, node_before[l])
                if l == 1:
                    chunk_starts()

            def edge_gathers(l):
                s, tab, width = es[l], (table[0], table[1], ztable)[l], (ROW, ROW, HID)[l]
                def body(it):
                    for par in range(2):
                        if due(it):
                            pool.wait_ge(s["batch_done"][par], it)
                            pool.nop(nofuse=True)
                        pool.wait_ge(s["idx_in"][par], 16 * it + 16)
                        pool.nop(nofuse=True)
                        for c in range(CB):
                            gather(G[:, par, c, 0:width], tab, idx[:, par, c:c + 1], s["gathered"][par])
                rounds(pool, HALF, body, before[l], peel=2, unroll=2)

            def node_gathers(l):
                s, width = ns[l], (0, ROW, ROW, HID)[l]
                for par in range(2):
                    pool.wait_ge(es[l - 1]["stored"][par], 16 * PARTS * (before[l - 1] + HALF))

                def body(it):
                    for par in range(2):
                        pool.wait_ge(s["in_"][par], in_dmas(l) * (it + 1))
                        pool.nop(nofuse=True)
                        for j in range(GT):
                            gather(ends[0:NP, par, j, 0:width], result[l - 1], last_in[0:NP, par, j:j + 1], s["got"][par])
                rounds(pool, NHALF, body)

            place(0)
            edge_gathers(0)
            node_gathers(1)
            place(1)
            edge_gathers(1)
            node_gathers(2)
            for par in range(2):
                pool.wait_ge(ns[2]["stored"][par], 48 * NHALF)
            edge_gathers(2)
            node_gathers(3)

        @block.tensor
        def _(pe):
            def turn(to, frm, n=P):
                return pe.transpose(to, frm, ident[0:n, 0:n])

            pe.wait_ge(consts, 2)
            pe.wait_ge(pads, 4)
            pe.wait_ge(digits, 1)
            for k in range(KB):
                pe.matmul(psC[0:NP, 0:NT], LT[:, k, 0:NP], ones[:, :], start=(k == 0), stop=False)
                mm = pe.matmul(psC[0:NP, 0:NT], hit[:, k, :], below[:, k, :], start=False, stop=(k == KB - 1))
            mm.then_inc(chunk_count, 1)
            pe.wait_ge(consts_in, 16 * N_CONSTS)
            for l in range(2):
                turn(psV[l][:, 0:P], Wx[l][:, 0:HID]).then_inc(attw, 1)
                pe.wait_ge(attw_used, 2 * l + 1)
                pe.matmul(psB[l][:, 0:2 * HEADS], wt[:, :], att[l][:, :], start=True, stop=True).then_inc(attw, 1)
            pe.wait_ge(floats, 2)
            for k in range(KB):
                for n, frm in enumerate((src_f, ew_f)):
                    if due(2 * k + n - 1):
                        pe.wait_ge(turned_used, 2 * k + n - 1)
                    if k == 0:
                        pe.wait_ge(attw_used, 4)
                    turn(psS[n][:, 0:P], frm[:, k, :]).then_inc(turned, 1)
            def project(l, frm, n_out, weights):
                s = ns[l]
                def body(it):
                    for par in range(2):
                        g = 2 * it + par

                        def turn_tile(j):
                            if due(g * GT + j - 1):
                                pe.wait_ge(s["xt"], g * GT + j - 1)
                            turn(psV[j % 2][:, 0:NP], frm[0:NP, par, j, :], NP).then_inc(s["xt_ps"], 1)

                        if l == 0:
                            pe.wait_ge(s["in_"][par], 16 * it + 16)
                        else:
                            pe.wait_ge(s["o_made" if l == 1 else "o_normed"], g + 1)
                        turn_tile(0)
                        for j in range(GT):
                            n, two = g * GT + j, j % 2
                            if j + 1 < GT:
                                turn_tile(j + 1)
                            pe.wait_ge(s["xt"], n + 1)
                            if due(n - 1):
                                pe.wait_ge(s["h"], n - 1)
                            if l == 2:
                                zd = psB[two][0:NP, HID:2 * HID]
                                pe.matmul(psB[two][0:NP, 0:HID], XT[:, two, 0:NP], weights[:, 0:HID], start=True, stop=True)
                                pe.matmul(zd, one[0:1, 0:NP], bmr[0:1, :], start=True, stop=False)
                                pe.matmul(zd, XT[:, two, 0:NP], weights[:, HID:2 * HID], start=False, stop=True).then_inc(s["h_ps"], 1)
                            else:
                                pe.matmul(psB[two][0:NP, 0:n_out], XT[:, two, 0:NP], weights, start=True, stop=True).then_inc(s["h_ps"], 1)
                rounds(pe, NHALF, body)

            pe.wait_ge(attw_used, 4)
            project(0, xg, ROW, Wx[0][:, :])
            pe.wait_ge(shifted, 1)
            pe.matmul(psC[0:NP, 2 * P:2 * P + 1], ident[0:NP + 1, 1:NP + 1], edge_of[0:NP + 1, 0:1], start=True, stop=True).then_inc(shifted, 1)

            def edge_pe(l):
                s, gat = es[l], l < 2
                def body(it):
                    for par in range(2):
                        b = 2 * it + par
                        if gat:
                            pe.wait_ge(s["loads"][par], 96 * (it + 1))
                            pe.wait_ge(s["asrc"], b + 1)
                            turn(ps_asrc, A[:, :])
                            for h in range(HEADS):
                                mm = pe.matmul(ps_adst, put[:, h, :], adst_in[:, par, :, h], start=(h == 0), stop=(h == HEADS - 1))
                            mm.then_inc(s["logits"], 1)
                            pe.wait_ge(s["l_made"], b + 1)
                            pe.matmul(ps_row, L[:, P - 1:P], ident[:, :], start=True, stop=True).then_inc(s["l_row"], 1)
                            pe.wait_ge(s["m_made"], b + 1)
                            pe.matmul(ps_col, m_pre[:, :], one[0:1, 0:1], start=True, stop=True).then_inc(s["m_col"], 1)
                            pe.wait_ge(s["d_made"], b + 1)
                            pe.matmul(ps_row2, D[:, P - 1:P], ident[:, :], start=True, stop=True).then_inc(s["d_rows"], 1)
                            pe.wait_ge(s["d_scan"], b + 1)
                            pe.matmul(ps_col2, d_pre[:, :], one[0:1, 0:1], start=True, stop=True).then_inc(s["d_col"], 1)
                            pe.wait_ge(s["d_final"], b + 1)
                            turn(psT[:, 0:P], EX[:, 0, :])
                            turn(psC[:, 0:P], M[:, 1:P + 1])
                            turn(psC[:, P:2 * P], D[:, :]).then_inc(s["weights_t"], 1)
                            coeff = EX[:, 1, :]
                        else:
                            pe.wait_ge(s["loads"][par], 80 * (it + 1))
                            coeff = mask[:, par, 1, :]

                        def results(st):
                            g = b * NS + st
                            pe.wait_ge(s["scanned"], g + 1)
                            if st >= 2 or not gat:
                                if due(g - 1):
                                    pe.wait_ge(s["r_made"], g - 1)
                            for j in range(SC):
                                tr = turn(psS[st % 2][:, j * P:(j + 1) * P], ST[:, st % 2, j * P:(j + 1) * P])
                                if st == NS - 1 and j == 0:
                                    tr.then_inc(s["batch_done"][par], 1)
                            tr.then_inc(s["s_turned"], 1)

                        for st in range(NS):
                            g = b * NS + st
                            if st >= 2 or not gat:
                                if due(g - 1):
                                    pe.wait_ge(s["c_copied"], g - 1)
                            for j in range(SC):
                                mm = pe.matmul(psB[st % 2][:, j * P:(j + 1) * P], pick[:, st * SC + j, :], coeff, start=True, stop=True)
                            mm.then_inc(s["c_spread"], 1)
                            pe.wait_ge(s["v_made"], g + 1)
                            if st >= 2 or not gat:
                                if due(g - 1):
                                    pe.wait_ge(s["scanned"], g - 1)
                            for j in range(SC):
                                tr = turn(psV[st % 2][:, j * P:(j + 1) * P], V[:, st % 2, j, :])
                            tr.then_inc(s["v_turned"], 1)
                            if st:
                                results(st - 1)
                        results(NS - 1)
                rounds(pe, HALF, body, before[l])

            pe.wait_ge(pick_made, 1)
            edge_pe(0)
            project(1, O, ROW, Wx[1][:, :])
            edge_pe(1)
            project(2, O, 2 * HID, Wz[:, :])
            pe.wait_ge(ns[2]["h"], NT)
            edge_pe(2)

            def final_pe():
                s = ns[3]
                def body(it):
                    for par in range(2):
                        g = 2 * it + par

                        def turn_tile(j):
                            if due(g * GT + j - 1):
                                pe.wait_ge(s["xt"], g * GT + j - 1)
                            turn(psV[j % 2][:, 0:NP], xg[0:NP, par, j, :], NP)
                            turn(psV[j % 2][:, HID:HID + NP], O[0:NP, par, j, :], NP).then_inc(s["xt_ps"], 1)

                        def hidden(j):
                            n, two = g * GT + j, j % 2
                            pe.wait_ge(s["xt"], n + 1)
                            if due(n - 1):
                                pe.wait_ge(s["hid"], n - 1)
                            pe.matmul(psB[two][:, 0:NP], U1z[:, :], XT[:, two, 0:NP], start=True, stop=False)
                            pe.matmul(psB[two][:, 0:NP], U1a[:, :], XT[:, two, HID:HID + NP], start=False, stop=True).then_inc(s["hid_ps"], 1)

                        pe.wait_ge(s["z_in"][par], 16 * it + 16)
                        pe.wait_ge(s["o_made"], g + 1)
                        turn_tile(0)
                        turn_tile(1)
                        hidden(0)
                        for j in range(GT):
                            if j + 2 < GT:
                                turn_tile(j + 2)
                            if j + 1 < GT:
                                hidden(j + 1)
                            pe.wait_ge(s["hid"], g * GT + j + 1)
                            bank, spot = j // BT, j % BT
                            if spot == 0 and due((g - 1) * len(BANKS) + bank + 1):
                                pe.wait_ge(s["h"], (g - 1) * len(BANKS) + bank + 1)
                            pe.matmul(row_bank[bank][0:NP, spot * HID:(spot + 1) * HID], V[:, j % 2, 0, 0:NP], U2s[:, :],
                                      start=True, stop=True).then_inc(s["h_ps"], 1)
                rounds(pe, NHALF, body)
            final_pe()

        @block.scalar
        def _(act):
            act.wait_ge(pads, 4)
            act.wait_ge(dst_in, 48)
            for to, frm in const_loads:
                act.dma_start(to, frm).then_inc(consts_in, 16)

            for l in range(2):
                act.wait_ge(attw, 2 * l + 1)
                act.activation(wt[:, :], psV[l][:, 0:P], ACT.Copy).then_inc(attw_used, 1)
                act.wait_ge(attw, 2 * l + 2)
                act.activation(Wx[l][:, HID:ROW], psB[l][:, 0:2 * HEADS], ACT.Copy).then_inc(attw_used, 1)

            def project_act(l):
                s, width, per = ns[l], (ROW, ROW, 2 * HID)[l], (16, 16, 48)[l]

                def x_in(it, par):
                    act.dma_start(xg[0:NP, par], node_rows(x, 2 * it + par, HID)).then_inc(s["in_"][par], 16)

                def project(it, par):
                    g = 2 * it + par

                    def turned_rows(j):
                        n = g * GT + j
                        act.wait_ge(s["xt_ps"], n + 1)
                        if due(n - 1):
                            act.wait_ge(s["h_ps"], n - 1)
                        if l == 1:
                            act.activation(XT[:, j % 2, 0:NP], psV[j % 2][:, 0:NP], ACT.Relu, bias=bias1c[:, 0:1]).then_inc(s["xt"], 1)
                        else:
                            act.activation(XT[:, j % 2, 0:NP], psV[j % 2][:, 0:NP], ACT.Copy).then_inc(s["xt"], 1)

                    if due(per * it):
                        act.wait_ge(s["stored"][par], per * it)
                    turned_rows(0)
                    for j in range(GT):
                        if j + 1 < GT:
                            turned_rows(j + 1)
                        act.wait_ge(s["h_ps"], g * GT + j + 1)
                        act.activation(HTt[0:NP, par, j, 0:width], psB[j % 2][0:NP, 0:width], ACT.Copy).then_inc(s["h"], 1)
                    act.wait_ge(s["h"], g * GT + GT)
                    if l < 2:
                        act.dma_start(node_rows(table[l], g, ROW), HTt[0:NP, par, :, 0:ROW]).then_inc(s["stored"][par], 16)
                    else:
                        act.dma_start(node_rows(ztable, g, HID), HTt[0:NP, par, :, 0:HID]).then_inc(s["stored"][par], 16)
                        act.dma_start(node_rows(zdst, g, HID), HTt[0:NP, par, :, HID:2 * HID]).then_inc(s["stored"][par], 16)
                        act.dma_start(node_rows(zrow, g, HID), O[0:NP, par]).then_inc(s["stored"][par], 16)

                if l == 0:
                    def body(it):
                        for par in range(2):
                            project(it, par)
                            x_in(it + 1, par)
                    for par in range(2):
                        x_in(0, par)
                    rounds(act, NHALF - 1, body)
                    for par in range(2):
                        project(NHALF - 1, par)
                else:
                    def body(it):
                        for par in range(2):
                            g = 2 * it + par
                            if l == 2 and due(g):
                                act.wait_ge(s["std_in"], g)
                                act.activation(std[0:NP], mv[0:NP, :, 1], ACT.Sqrt, bias=eps[0:NP, 0:1]).then_inc(s["std_out"], 1)
                            act.wait_ge(s["xd"], g + 1)
                            act.activation(self_w[0:NP], self_x[0:NP], ACT.Exp).then_inc(s["ex"], 1)
                            if par:
                                project(it, 0)
                            elif due(it):
                                project(it - 1, 1)
                    rounds(act, NHALF, body, peel=2)
                    if l == 2:
                        act.wait_ge(s["std_in"], NG)
                        act.activation(std[0:NP], mv[0:NP, :, 1], ACT.Sqrt, bias=eps[0:NP, 0:1]).then_inc(s["std_out"], 1)
                    project(NHALF - 1, 1)

            project_act(0)

            def edge_act(l):
                s, gat = es[l], l < 2
                width = ROW if gat else HID
                def body(it):
                    for par in range(2):
                        b = 2 * it + par
                        if gat:
                            act.wait_ge(s["gathered"][par], 16 * CB * (it + 1))
                            act.activation(A[:, :].rearrange("p (h c) -> p c h", h=HEADS), G[:, par, :, HID:HID + HEADS], ACT.Copy).then_inc(s["asrc"], 1)
                            act.wait_ge(s["x_made"], b + 1)
                            act.activation(k_exp[:, :], k_row[:, :], ACT.Exp)
                            act.activation(EX[:, :, :], XD[:, :, :], ACT.Exp).then_inc(s["exps"], 1)
                            act.wait_ge(s["weights_t"], b + 1)
                        if due(16 * PARTS * it):
                            act.wait_ge(s["stored"][par], 16 * PARTS * it)
                        if gat:
                            for n in range(2):
                                act.activation(R[:, par, :, HID + n * HEADS:HID + n * HEADS + HEADS],
                                               psC[:, (1 - n) * P:(2 - n) * P].rearrange("p (h c) -> p c h", c=CB), ACT.Copy)

                        def rows(st):
                            g = b * NS + st
                            act.wait_ge(s["s_turned"], g + 1)
                            act.activation(R[:, par, st * SC:(st + 1) * SC, 0:HID],
                                           psS[st % 2][:, :].rearrange("p (c f) -> p c f", f=HID), ACT.Copy).then_inc(s["r_made"], 1)

                        for st in range(NS):
                            g = b * NS + st
                            act.wait_ge(s["c_spread"], g + 1)
                            if st >= 2 or not gat:
                                if due(g - 1):
                                    act.wait_ge(s["scanned"], g - 1)
                            act.activation(CBC[:, st % 2, :], psB[st % 2][:, :], ACT.Copy).then_inc(s["c_copied"], 1)
                            if st:
                                rows(st - 1)
                        rows(NS - 1)
                rounds(act, HALF, body, before[l])

            edge_act(0)
            project_act(1)
            edge_act(1)
            project_act(2)
            edge_act(2)

            def final_act():
                s = ns[3]

                def turned_rows(g, j):
                    n = g * GT + j
                    act.wait_ge(s["xt_ps"], n + 1)
                    if due(n - 1):
                        act.wait_ge(s["hid_ps"], n - 1)
                    act.activation(XT[:, j % 2, :].rearrange("p (a n) -> p a n", a=2)[:, :, 0:NP],
                                   psV[j % 2][:, 0:2 * HID].rearrange("p (a n) -> p a n", a=2)[:, :, 0:NP], ACT.Copy).then_inc(s["xt"], 1)

                def deviation(g):
                    act.wait_ge(s["std_in"], g + 1)
                    act.activation(std[0:NP], mv[0:NP, :, 1], ACT.Sqrt, bias=eps[0:NP, 0:1]).then_inc(s["std_out"], 1)

                def rows_out(it, par):
                    act.wait_ge(s["o_normed"], 2 * it + par + 1)
                    act.dma_start(node_rows(out, 2 * it + par, HID), HTt[0:NP, par, :, 0:HID]).then_inc(s["stored"][par], 16)

                def body(it):
                    for par in range(2):
                        g = 2 * it + par
                        turned_rows(g, 0)
                        for j in range(GT):
                            if j + 1 < GT:
                                turned_rows(g, j + 1)
                            n = g * GT + j
                            act.wait_ge(s["hid_ps"], n + 1)
                            if due(n - 1):
                                act.wait_ge(s["h_ps"], n - 1)
                            act.activation(V[:, j % 2, 0, 0:NP], psB[j % 2][:, 0:NP], ACT.Relu, bias=b1c[:, 0:1]).then_inc(s["hid"], 1)
                            if j == 1 and due(g):
                                deviation(g - 1)
                        if due(g):
                            if par:
                                rows_out(it, 0)
                            else:
                                rows_out(it - 1, 1)
                rounds(act, NHALF, body)
                deviation(NG - 1)
                rows_out(NHALF - 1, 1)
            final_act()

        @block.vector
        def _(dve):
            vec = nc.vector
            n_step = [0]

            def link(ins):
                n_step[0] += 1
                ins.then_inc(dve_step, 1)
                dve.wait_ge(dve_step, n_step[0])

            vec.memset(dst_i[:, KB - 1, :], N_NODES)
            vec.memset(prev_i[:, 0, :], -1)
            vec.memset(prev_i[:, KB - 1, :], N_NODES)
            vec.memset(src_i[:, KB - 1, :], 0)
            vec.memset(ew_f[:, KB - 1, :], 0.0).then_inc(pads, 1)
            vec.memset(att[0][:, :], 0.0)
            vec.memset(att[1][:, :], 0.0).then_inc(pads, 1)
            vec.memset(one[:, :], 1.0)
            vec.memset(ones[:, :], 1.0)
            vec.memset(eps[:, :], EPS)
            vec.memset(head_big[:, :], -BIG)
            vec.memset(k_row[:, :], -BIG)
            vec.memset(edge_of[:, :], float(N_EDGES)).then_inc(pads, 1)
            vec.memset(m_end[:, :, :], -BIG)
            vec.memset(d_end[:, :, :], 0.0).then_inc(pads, 1)
            vec.memset(CBC[:, :, :], 0.0).then_inc(zeroed, 1)

            dve.wait_ge(dst_in, 48)
            vec.tensor_copy(dst_f, dst_i).then_inc(floats, 1)
            dve.wait_ge(floats, 1)
            vec.tensor_scalar(chunk_first[:, :], dst_f[:, :, 0], float(N_NODES - 1), None, ALU.min)

            dve.wait_ge(consts, 5)
            for k in range(KB):
                last = dst_f[:, k, P - 1:P]
                vec.tensor_scalar(LT[:, k, :], hundreds[:, :], last, 0.0, ALU.is_gt, ALU.add, accum_out=small[:, 3, k:k + 1])
            link(vec.memset(small[:, 7, 2:3], 0.0))
            link(vec.tensor_scalar(small[:, 4, 0:KB], small[:, 3, 0:KB], float(NT), float(-NT * NP), ALU.mult, ALU.add))
            link(vec.tensor_tensor(small[:, 5, 0:KB], small[:, 4, 0:KB], dst_f[:, :, P - 1], ALU.add))
            vec.tensor_tensor(hit, LT[:, :, 1:NP + 1], LT[:, :, 0:NP], ALU.subtract)
            for k in range(KB):
                step = vec.tensor_scalar(below[:, k, :], units[:, :], small[:, 5, k:k + 1], None, ALU.is_gt)
            step.then_inc(digits, 1)

            dve.wait_ge(edges_in, 16 * 11)
            vec.tensor_copy(prev_f, prev_i)
            link(vec.tensor_copy(src_f, src_i))
            link(vec.tensor_tensor(same, dst_f, prev_f, ALU.is_equal))
            vec.memset(small[:, 7, 1:2], 0.0).then_inc(floats, 1)
            vec.tensor_scalar(same_neg, same, -1.0, BIG, ALU.add, ALU.mult)
            link(vec.tensor_reduce(small[:, 2, 0:KB], same, AX_X, ALU.min))
            link(vec.tensor_scalar(chunk_goes[:, :], small[:, 2, 0:KB], -1.0, BIG, ALU.add, ALU.mult))
            vec.memset(small[:, 7, 0:1], 0.0).then_inc(masks_made, 1)

            def search_chunks(g, par):
                vec.tensor_copy(q_idx[0:NP, par, :], smalli[0:NP, 0, bass.ds(g * GT, GT)]).then_inc(search_in[par], 1)

            dve.wait_ge(chunk_count, 1)
            link(vec.tensor_copy(small[0:NP, 6, :], psC[0:NP, 0:NT]))
            link(vec.tensor_copy(smalli[0:NP, 0, :], small[0:NP, 6, :]))
            for par in range(2):
                search_chunks(par, par)
            for k in range(KB):
                dve.wait_ge(turned, 2 * k + 1)
                vec.tensor_copy(src_t[:, k, :], psS[0][:, 0:P]).then_inc(turned_used, 1)
                dve.wait_ge(turned, 2 * k + 2)
                vec.tensor_copy(prev_f[:, k, :], psS[1][:, 0:P]).then_inc(turned_used, 1)
            vec.tensor_copy(pick[:, :, :].rearrange("p c (h f) -> p c h f", h=HEADS),
                            ident[:, :].rearrange("p (h c) -> p c h", h=HEADS).unsqueeze(3).to_broadcast([P, CB, HEADS, HD]))
            link(vec.memset(put[:, :, :], 0.0))
            vec.memset(ST[:, :, :], 0.0)
            for h in range(HEADS):
                step = vec.tensor_copy(put[:, h, h * CB:(h + 1) * CB], ident[0:CB, 0:CB])
            step.then_inc(pick_made, 1)

            def chain_of(s, per_round, late=0):
                count = [0]

                def start(it):
                    count[0] = 0 if isinstance(it, int) and it == 0 else -late

                def step(ins, it):
                    count[0] += 1
                    ins.then_inc(s["chain"], 1)
                    dve.wait_ge(s["chain"], it * per_round + count[0])

                def end():
                    assert count[0] == per_round - late, count[0]
                return start, step, end

            def by_node(t, group):
                return t[0:NP, bass.ds(group * GT, GT)]

            def count_before(it, par):
                g = 2 * it + par
                dve.wait_ge(search_rows[par], 16 * GT * (it + 1))
                vec.tensor_tensor(O[0:NP, par], rows_dst[0:NP, par], by_node(node, g).unsqueeze(2).to_broadcast([NP, GT, P]),
                                  ALU.is_lt).then_inc(search_step, 1)
                dve.wait_ge(search_step, g + 1)
                return vec.tensor_reduce(by_node(edge_of, g), O[0:NP, par], AX_X, ALU.add)

            def search(it):
                for par in range(2):
                    count_before(it, par)
                    search_chunks(2 * (it + 1) + par, par)
            rounds(dve, NHALF - 1, search)
            for par in range(2):
                step = count_before(NHALF - 1, par)
            link(step)
            link(vec.scalar_tensor_tensor(edge_of[0:NP, :], small[0:NP, 6, :], float(P), edge_of[0:NP, :], ALU.mult, ALU.add))
            vec.tensor_copy(small[0:NP, 0, 0:NT - 1], edge_of[0:NP, 1:NT]).then_inc(shifted, 1)
            dve.wait_ge(shifted, 2)
            link(vec.tensor_copy(small[0:NP, 0, NT - 1:NT], psC[0:NP, 2 * P:2 * P + 1]))
            link(vec.tensor_tensor(has_edge[0:NP, :], small[0:NP, 0, :], edge_of[0:NP, :], ALU.is_gt))
            vec.tensor_scalar(max_bound[0:NP, :], has_edge[0:NP, :], 2 * BIG, -BIG, ALU.mult, ALU.add)
            vec.tensor_scalar(smalli[0:NP, 2, :], small[0:NP, 0, :], -1.0, 0.0, ALU.add, ALU.max)
            link(vec.tensor_scalar(small[0:NP, 2, :], node[0:NP, :], float(E_PAD), None, ALU.add))
            link(vec.tensor_tensor(small[0:NP, 3, :], edge_of[0:NP, :], small[0:NP, 2, :], ALU.subtract))
            link(vec.tensor_tensor(small[0:NP, 3, :], small[0:NP, 3, :], has_edge[0:NP, :], ALU.mult))
            vec.tensor_tensor(smalli[0:NP, 1, :], small[0:NP, 3, :], small[0:NP, 2, :], ALU.add).then_inc(ends_made, 1)

            def flat(t):
                return t.rearrange("p h c -> p (h c)")

            def edge_dve(l):
                s, gat = es[l], l < 2
                start, step, end = chain_of(s, 24)
                def body(it):
                    start(it)
                    for par in range(2):
                        b = 2 * it + par
                        same01, same_big = mask[:, par, 0, :], mask[:, par, 1, :]
                        p, c = EX[:, 0, :], EX[:, 1, :]
                        if gat:
                            goes_on = flat(carry_mask[:, par])
                            dve.wait_ge(s["loads"][par], 96 * (it + 1))
                            dve.wait_ge(s["logits"], b + 1)
                            step(vec.tensor_tensor_scan(T[:, :], same01, ps_adst, 0.0, ALU.mult, ALU.add), it)
                            step(vec.tensor_tensor(U[:, :], ps_asrc, T[:, :], ALU.add), it)
                            step(vec.scalar_tensor_tensor(E[:, :], U[:, :], SLOPE, U[:, :], ALU.mult, ALU.max), it)
                            vec.tensor_tensor_scan(L[:, :], same_big, E[:, :], -BIG, ALU.add, ALU.max).then_inc(s["l_made"], 1)
                            vec.tensor_copy(m_row[:, :, 0], m_end[:, :, CB])
                            dve.wait_ge(s["l_row"], b + 1)
                            step(vec.tensor_copy(m_row[:, :, 1:HR], ps_row.rearrange("p (h c) -> p h c", h=HEADS)), it)
                            step(vec.tensor_tensor_scan(flat(m_end[:, :, :]), goes_on, flat(m_row[:, :, :]), -BIG, ALU.add, ALU.max), it)
                            vec.tensor_copy(m_pre[:, :].rearrange("p (h c) -> p h c", h=HEADS), m_end[:, :, 0:CB]).then_inc(s["m_made"], 1)
                            n = HEADS * HR
                            step(vec.tensor_tensor(k_row[:, 1:n], flat(m_end[:, :, :])[:, 0:n - 1], flat(m_end[:, :, :])[:, 1:n], ALU.subtract), it)
                            vec.tensor_tensor(k_row[:, 1:n], k_row[:, 1:n], goes_on[:, 1:n], ALU.add)
                            dve.wait_ge(s["m_col"], b + 1)
                            step(vec.tensor_copy(M[:, 0:1], ps_col), it)
                            step(vec.tensor_tensor_scan(M[:, 1:P + 1], same_big, E[:, :], M[:, 0:1], ALU.add, ALU.max), it)
                            step(vec.tensor_tensor(XD[:, 1, :], M[:, 0:P], same_big, ALU.add), it)
                            vec.tensor_tensor(XD[:, 0, :], E[:, :], M[:, 1:P + 1], ALU.subtract)
                            vec.tensor_tensor(XD[:, 1, :], XD[:, 1, :], M[:, 1:P + 1], ALU.subtract).then_inc(s["x_made"], 1)
                            dve.wait_ge(s["exps"], b + 1)
                            vec.tensor_tensor_scan(D[:, :], c, p, 0.0, ALU.mult, ALU.add).then_inc(s["d_made"], 1)
                            vec.tensor_copy(d_rowv[:, :, 0], d_end[:, :, CB])
                            dve.wait_ge(s["d_rows"], b + 1)
                            step(vec.tensor_copy(d_rowv[:, :, 1:HR], ps_row2.rearrange("p (h c) -> p h c", h=HEADS)), it)
                            step(vec.tensor_tensor_scan(flat(d_end[:, :, :]), k_exp[:, :], flat(d_rowv[:, :, :]), 0.0, ALU.mult, ALU.add), it)
                            vec.tensor_copy(d_pre[:, :].rearrange("p (h c) -> p h c", h=HEADS), d_end[:, :, 0:CB]).then_inc(s["d_scan"], 1)
                            dve.wait_ge(s["d_col"], b + 1)
                            step(vec.tensor_copy(D0[:, :], ps_col2), it)
                            vec.tensor_tensor_scan(D[:, :], c, p, D0[:, 0:1], ALU.mult, ALU.add).then_inc(s["d_final"], 1)
                            dve.wait_ge(s["weights_t"], b + 1)
                        else:
                            dve.wait_ge(s["loads"][par], 80 * (it + 1))
                            dve.wait_ge(s["gathered"][par], 16 * CB * (it + 1))

                        def values(st):
                            if st >= 2 or not gat:
                                if due(b * NS + st - 1):
                                    dve.wait_ge(s["v_turned"], b * NS + st - 1)
                            rows = G[:, par, st * SC:(st + 1) * SC, 0:HID]
                            if gat:
                                weights = psT[:, 0:P].rearrange("p (h c) -> p c h", h=HEADS)[:, st * SC:(st + 1) * SC, :]
                                ins = vec.tensor_tensor(V[:, st % 2].rearrange("p c (h f) -> p c h f", h=HEADS),
                                                        rows.rearrange("p c (h f) -> p c h f", h=HEADS),
                                                        weights.unsqueeze(3).to_broadcast([P, SC, HEADS, HD]), ALU.mult)
                            else:
                                for j in range(SC):
                                    ins = vec.scalar_tensor_tensor(V[:, st % 2, j, :], wwb[:, :], ewt[:, par, st * SC + j:st * SC + j + 1],
                                                                   rows[:, j, :], ALU.mult, ALU.add)
                            ins.then_inc(s["v_made"], 1)

                        values(0)
                        for st in range(NS):
                            g = b * NS + st
                            if st + 1 < NS:
                                values(st + 1)
                            dve.wait_ge(s["c_copied"], g + 1)
                            dve.wait_ge(s["v_turned"], g + 1)
                            if due(g):
                                dve.wait_ge(s["scanned"], g)
                            if st >= 2 or not gat:
                                if due(g - 1):
                                    dve.wait_ge(s["s_turned"], g - 1)
                            vec.tensor_tensor_scan(ST[:, st % 2, :], CBC[:, st % 2, :], psV[st % 2][:, :], ST[:, 1 - st % 2, SE - 1:SE],
                                                   ALU.mult if gat else ALU.add, ALU.add if gat else ALU.max).then_inc(s["scanned"], 1)
                    if gat:
                        end()
                rounds(dve, HALF, body, before[l])

            def layernorm_start(l, rows, it, step):
                for j in range(GT):
                    ins = vec.bn_stats(stats[0:NP, j, :], rows[:, j, :])
                step(ins, it)
                dve.nop(nofuse=True)
                for j in range(GT):
                    ins = vec.bn_aggr(mv[0:NP, j, :], stats[0:NP, j, :])
                ins.then_inc(ns[l]["std_in"], 1)

            def layernorm_end(l, rows, g, it, step):
                dve.wait_ge(ns[l]["std_out"], g + 1)
                step(vec.reciprocal(rstd[0:NP, :], std[0:NP, :]), it)
                for j in range(GT):
                    ins = vec.tensor_scalar(rows[:, j, :], rows[:, j, :], mv[0:NP, j, 0:1], rstd[0:NP, j:j + 1], ALU.subtract, ALU.mult)
                ins.then_inc(ns[l]["o_normed"], 1)

            def banked(n):
                a, z = BANKS[n]
                return row_bank[n][0:NP, 0:(z - a) * HID].rearrange("p (t f) -> p t f", f=HID), slice(a, z)

            def node_dve(l):
                s = ns[l]
                start, step, end = chain_of(s, *((20, 0), (28, 1))[l - 1])
                weight = psT[0:NP, 0:2 * GT * HEADS].rearrange("p (n t h) -> p n t h", n=2, t=GT)

                def by_head(t):
                    return t.rearrange("p t (h f) -> p t h f", h=HEADS)

                def body(it):
                    start(it)
                    for par in range(2):
                        g = 2 * it + par
                        e, o = ends[0:NP, par], own[0:NP, par]
                        dve.wait_ge(s["in_"][par], in_dmas(l) * (it + 1))
                        dve.wait_ge(s["got"][par], 16 * GT * (it + 1))
                        step(vec.tensor_tensor(self_e[0:NP], o[:, :, HID:HID + HEADS], o[:, :, HID + HEADS:ROW], ALU.add), it)
                        step(vec.scalar_tensor_tensor(self_e[0:NP], self_e[0:NP], SLOPE, self_e[0:NP], ALU.mult, ALU.max), it)
                        step(vec.tensor_tensor(self_x[0:NP, 0], e[:, :, HID + HEADS:ROW],
                                               by_node(max_bound, g).unsqueeze(2).to_broadcast([NP, GT, HEADS]), ALU.min), it)
                        step(vec.tensor_tensor(den[0:NP], self_x[0:NP, 0], self_e[0:NP], ALU.max), it)
                        vec.tensor_tensor(self_x[0:NP, 0], self_x[0:NP, 0], den[0:NP], ALU.subtract)
                        vec.tensor_tensor(self_x[0:NP, 1], self_e[0:NP], den[0:NP], ALU.subtract).then_inc(s["xd"], 1)
                        if l == 2 and due(g):
                            layernorm_end(l, O[0:NP, 1 - par], g - 1, it, step)
                        dve.wait_ge(s["ex"], g + 1)
                        step(vec.tensor_tensor(den[0:NP], e[:, :, HID:HID + HEADS], self_w[0:NP, 0], ALU.mult), it)
                        step(vec.tensor_tensor(den[0:NP], den[0:NP], self_w[0:NP, 1], ALU.add), it)
                        step(vec.tensor_scalar(den[0:NP], den[0:NP], 1.0e-16, None, ALU.add), it)
                        step(vec.reciprocal(den[0:NP], den[0:NP]), it)
                        vec.tensor_tensor(weight[:, 0], self_w[0:NP, 0], den[0:NP], ALU.mult)
                        step(vec.tensor_tensor(weight[:, 1], self_w[0:NP, 1], den[0:NP], ALU.mult), it)
                        for n in range(len(BANKS)):
                            rows, ts = banked(n)
                            size = [NP, ts.stop - ts.start, HEADS, HD]
                            vec.tensor_tensor(by_head(rows), by_head(e[:, ts, 0:HID]), weight[:, 0, ts].unsqueeze(3).to_broadcast(size), ALU.mult)
                        step(vec.tensor_tensor(by_head(o[:, :, 0:HID]), by_head(o[:, :, 0:HID]),
                                               weight[:, 1].unsqueeze(3).to_broadcast([NP, GT, HEADS, HD]), ALU.mult), it)
                        if due((g - 1) * GT):
                            dve.wait_ge(s["xt_ps"], (g - 1) * GT)
                        if l == 1:
                            for n in range(len(BANKS)):
                                rows, ts = banked(n)
                                ins = vec.tensor_tensor(O[0:NP, par, ts], rows, o[:, ts, 0:HID], ALU.add)
                            ins.then_inc(s["o_made"], 1)
                            continue
                        if due(48 * it):
                            dve.wait_ge(s["stored"][par], 48 * it)
                        for n in range(len(BANKS)):
                            rows, ts = banked(n)
                            ins = vec.tensor_tensor(rows, rows, o[:, ts, 0:HID], ALU.add)
                        step(ins, it)
                        for n in range(len(BANKS)):
                            rows, ts = banked(n)
                            ins = vec.tensor_tensor(rows, rows, bias2r[0:NP, :].unsqueeze(1).to_broadcast([NP, ts.stop - ts.start, HID]), ALU.add)
                        step(ins, it)
                        for n in range(len(BANKS)):
                            rows, ts = banked(n)
                            ins = vec.scalar_tensor_tensor(O[0:NP, par, ts], rows, 0.0, xg[0:NP, par, ts], ALU.max, ALU.add)
                        ins.then_inc(s["used"][par], 1)
                        dve.wait_ge(s["used"][par], it + 1)
                        layernorm_start(l, O[0:NP, par], it, step)
                    end()
                rounds(dve, NHALF, body)
                if l == 2:
                    start(NHALF)
                    layernorm_end(l, O[0:NP, 1], NG - 1, NHALF, step)

            def final_dve():
                s = ns[3]
                start, step, end = chain_of(s, 6, 3)
                vec.tensor_copy(psT[0:NP, 0:NT], has_edge[0:NP, :]).then_inc(dve_step, 1)
                n_step[0] += 1
                dve.wait_ge(dve_step, n_step[0])

                def result_rows(it, par, now, step):
                    g, y = 2 * it + par, HTt[0:NP, par, :, 0:HID]
                    for n in range(len(BANKS)):
                        rows, ts = banked(n)
                        dve.wait_ge(s["h_ps"], g * GT + ts.stop)
                        ins = vec.tensor_tensor(rows, rows, xg[0:NP, par, ts], ALU.add)
                    ins.then_inc(s["z_used"][par], 1)
                    dve.wait_ge(s["z_used"][par], it + 1)
                    if due(16 * it):
                        dve.wait_ge(s["stored"][par], 16 * it)
                    for n in range(len(BANKS)):
                        rows, ts = banked(n)
                        vec.tensor_tensor(y[:, ts, :], rows, b2r[0:NP, :].unsqueeze(1).to_broadcast([NP, ts.stop - ts.start, HID]),
                                          ALU.add).then_inc(s["h"], 1)
                    dve.wait_ge(s["h"], (g + 1) * len(BANKS))
                    layernorm_start(3, y, now, step)

                def body(it):
                    start(it)
                    for par in range(2):
                        g = 2 * it + par
                        dve.wait_ge(s["in_"][par], in_dmas(3) * (it + 1))
                        dve.wait_ge(s["got"][par], 16 * GT * (it + 1))
                        if due((g - 1) * GT):
                            dve.wait_ge(s["xt_ps"], (g - 1) * GT)
                        step(vec.tensor_tensor(O[0:NP, par], ends[0:NP, par, :, 0:HID], own[0:NP, par, :, 0:HID], ALU.add), it)
                        vec.memset(small[0:NP, 7, 6:7], 0.0).then_inc(s["used"][par], 1)
                        vec.tensor_tensor(O[0:NP, par], O[0:NP, par], by_node(psT, g).unsqueeze(2).to_broadcast([NP, GT, HID]),
                                          ALU.mult).then_inc(s["o_made"], 1)
                        if due(g - 1):
                            layernorm_end(3, HTt[0:NP, par, :, 0:HID], g - 2, it, step)
                        if par:
                            result_rows(it, 0, it, step)
                        elif due(it):
                            result_rows(it - 1, 1, it, step)
                    end()
                rounds(dve, NHALF, body, peel=2)
                start(NHALF)
                layernorm_end(3, HTt[0:NP, 0, :, 0:HID], NG - 2, NHALF, step)
                result_rows(NHALF - 1, 1, NHALF, step)
                layernorm_end(3, HTt[0:NP, 1, :, 0:HID], NG - 1, NHALF, step)

            edge_dve(0)
            node_dve(1)
            edge_dve(1)
            node_dve(2)
            edge_dve(2)
            final_dve()


_INS = ["x", "src", "dst", "edge_weight", "L0_gnn_W1", "L0_gnn_att_src1", "L0_gnn_att_dst1", "L0_gnn_bias1", "L0_gnn_W2",
        "L0_gnn_att_src2", "L0_gnn_att_dst2", "L0_gnn_bias2", "L1_gnn_Wm", "L1_gnn_bm", "L1_gnn_W1", "L1_gnn_b1", "L1_gnn_W2", "L1_gnn_b2"]


def kernel(**inputs):
    import numpy as np
    import concourse.bacc as bacc
    from concourse.bass_utils import run_bass_kernel_spmd

    nc = bacc.Bacc("TRN2", target_bir_lowering=False, num_devices=1)
    arrays, args = {}, []
    for name in _INS:
        a = np.ascontiguousarray(inputs[name])
        arrays[f"in_{name}"] = a
        args.append(nc.dram_tensor(f"in_{name}", a.shape, mybir.dt.from_np(a.dtype), kind="ExternalInput").ap())
    args.append(nc.dram_tensor("out", (N_NODES, HID), F32, kind="ExternalOutput").ap())
    gnn_program(nc, *args)
    return run_bass_kernel_spmd(nc, [arrays], core_ids=[0]).results[0]["out"]
```

```python
from contextlib import ExitStack

import concourse.bass as bass
from concourse import mybir

F32 = mybir.dt.float32
I32 = mybir.dt.int32
ALU = mybir.AluOpType
ACT = mybir.ActivationFunctionType
AX_X = mybir.AxisListType.X

P = 128
HID = 128
HEADS = 4
HD = HID // HEADS
N_NODES = 12500
N_EDGES = 212500
NP = 125
NT = N_NODES // NP
GT = 10
NG = NT // GT
BT = 512 // HID
BANKS = [(a, min(a + BT, GT)) for a in range(0, GT, BT)]
CB = 32
BE = CB * P
NB = -(-N_EDGES // BE)
NCH = NB * CB
KB = NCH // P
E_PAD = NCH * P
FULL_CH = N_EDGES // P
TAIL = N_EDGES - FULL_CH * P
SC = 4
NS = CB // SC
PARTS = 4
SE = SC * P
ZT = BT
NZ = NT // ZT
ROW = HID + 2 * HEADS
BIG = 1.0e30
SLOPE = 0.2
EPS = 1.0e-5
HR = CB + 1
assert NP * NT == N_NODES and NG * GT == NT and NB % 2 == 0 and NG % 2 == 0 and HEADS * CB == P
assert len(BANKS) <= 3 and GT % 2 == 0 and NZ * ZT == NT and NZ == NB // 2 - 1
assert KB * P == NCH and FULL_CH // P == KB - 1


def due(value):
    return not isinstance(value, int) or value > 0


def rounds(eng, count, body, done=0, peel=1):
    for it in range(done, done + peel):
        body(it)
    with eng.Fori(done + peel, done + count) as it:
        body(it)


def gnn_program(nc, x, src, dst, edge_weight, W_1, att_src_1, att_dst_1, bias_1, W_2, att_src_2, att_dst_2,
                bias_2, Wm, bm, U1, b1, U2, b2, out):
    with ExitStack() as ctx:
        def sb(name, shape, dt=F32):
            return ctx.enter_context(nc.sbuf_tensor(name, shape, dt))

        def sem(name):
            return ctx.enter_context(nc.semaphore(name))

        def dram(name, shape, dt=F32):
            return nc.dram_tensor(name, shape, dt).ap()

        ctx.enter_context(nc.allow_non_contiguous_dma(reason="small index and weight layouts"))

        table = [dram(f"table{l}", [N_NODES, ROW]) for l in range(2)]
        ztable = dram("ztable", [N_NODES, HID])
        zdst = dram("zdst", [N_NODES, HID])
        zrow = dram("zrow", [N_NODES, HID])
        result = [dram(f"result{l}", [E_PAD, w]) for l, w in enumerate((ROW, ROW, HID))]
        adst_at = dram("adst_at", [E_PAD + N_NODES, HEADS])
        d_idx = dram("d_idx", [NB, P, CB], I32)
        d_ew = dram("d_ew", [NB, P, CB])
        d_mask = dram("d_mask", [NB, CB, 2, P])
        d_carry = dram("d_carry", [NB, HR])
        d_dst = dram("d_dst", [NCH, P])
        d_first = dram("d_first", [NP, NT], I32)
        d_last = dram("d_last", [NP, NT], I32)

        G = sb("G", [P, 2, CB, ROW])
        R = sb("R", [P, 2, CB, ROW])
        pick = sb("pick", [P, CB, HID])
        V = sb("V", [P, 2, SC, HID])
        CBC = sb("CBC", [P, 2, SE])
        ST = sb("ST", [P, 2, SE])
        idx = sb("idx", [P, 2, CB], I32)
        mask = sb("mask", [P, 2, 2, P])
        adst_in = sb("adst_in", [CB, 2, P, HEADS])
        carry_mask = sb("carry_mask", [1, 2, HEADS, HR])
        ewt = sb("ewt", [P, 2, CB])
        A = sb("A", [P, P])
        T = sb("T", [P, P])
        U = sb("U", [P, P])
        E = sb("E", [P, P])
        L = sb("L", [P, P])
        M = sb("M", [P, P + 1])
        XD = sb("XD", [P, 2, P])
        EX = sb("EX", [P, 2, P])
        D = sb("D", [P, P])
        D0 = sb("D0", [P, 1])
        m_row = sb("m_row", [1, HEADS, HR])
        m_end = sb("m_end", [1, HEADS, HR])
        k_row = sb("k_row", [1, HEADS * HR])
        k_exp = sb("k_exp", [1, HEADS * HR])
        m_pre = sb("m_pre", [1, P])
        d_pre = sb("d_pre", [1, P])
        d_rowv = sb("d_rowv", [1, HEADS, HR])
        d_end = sb("d_end", [1, HEADS, HR])
        ident = sb("ident", [P, P])
        ident_row = sb("ident_row", [P, NP])
        put = sb("put", [CB, HEADS, P])
        one = sb("one", [1, P])
        ones = sb("ones", [P, NT])
        node = sb("node", [P, NT])
        edge_of = sb("edge_of", [P, NT])
        has_edge = sb("has_edge", [P, NT])
        max_bound = sb("max_bound", [P, NT])
        Wx = [sb(f"Wx{l}", [P, ROW]) for l in range(2)]
        Wz = sb("Wz", [P, 2 * HID])
        att = [sb(f"att{l}", [P, 2 * HEADS]) for l in range(2)]
        wt = sb("wt", [P, HID])
        U1z = sb("U1z", [P, HID])
        U1a = sb("U1a", [P, HID])
        U2s = sb("U2s", [P, HID])
        b1c = sb("b1c", [P, 1])
        b2r = sb("b2r", [1, HID])
        bias1c = sb("bias1c", [P, 1])
        bmr = sb("bmr", [1, HID])
        wwb = sb("wwb", [P, HID])
        eps = sb("eps", [P, 1])
        chunk_first = sb("chunk_first", [P, KB], I32)
        chunk_adst = sb("chunk_adst", [P, 2, KB, HEADS])
        q_idx = sb("q_idx", [P, 2, GT], I32)
        q_adst = sb("q_adst", [P, 2, GT, HEADS])
        last_in = sb("last_in", [P, 2, GT], I32)
        ends = sb("ends", [P, 2, GT, ROW])
        own = sb("own", [P, 2, GT, ROW])
        O = sb("O", [P, 2, GT, HID])
        xg = sb("xg", [P, 2, GT, HID])
        XT = sb("XT", [P, 2, 2 * HID])
        ZX = XT[:, :, :].rearrange("p a f -> p (a f)")
        HTt = sb("HTt", [P, 2, GT, ROW])
        self_e = sb("self_e", [P, GT, HEADS])
        self_w = sb("self_w", [P, 2, GT, HEADS])
        self_x = sb("self_x", [P, 2, GT, HEADS])
        den = sb("den", [P, GT, HEADS])
        stats = sb("stats", [P, GT, 6])
        mv = sb("mv", [P, GT, 2])
        std = sb("std", [P, GT])
        rstd = sb("rstd", [P, GT])

        room = R[:, :, :, :].rearrange("p a c f -> p (a c f)")
        room2 = G[:, :, :, :].rearrange("p a c f -> p (a c f)")

        def part(r, n, dt=F32):
            v = r[:, n * NCH:(n + 1) * NCH]
            return (v if dt == F32 else v.bitcast(dt)).rearrange("p (k f) -> p k f", k=KB)

        dst_i, prev_i, src_i = (part(room, n, I32) for n in range(3))
        dst_f, prev_f = part(room, 3), part(room, 4)
        src_f, same, same_neg, ew_f = (part(room2, n) for n in range(4))
        src_t = part(room2, 4, I32)
        LT = pick[:, :, :].rearrange("p c f -> p (c f)")[:, 0:KB * (NP + 1)].rearrange("p (k f) -> p k f", k=KB)
        hit = room[:, 0:KB * NP].rearrange("p (k f) -> p k f", k=KB)
        below = own[:, :, :, :].rearrange("p a t f -> p (a t f)")[:, 0:KB * NT].rearrange("p (k f) -> p k f", k=KB)
        rows_dst = ends[:, :, :, 0:P]
        small = sb("small", [P, 8, NT])
        smalli = sb("smalli", [P, 3, NT], I32)
        hundreds = sb("hundreds", [P, NP + 1])
        units = sb("units", [P, NT])
        chunk_goes = sb("chunk_goes", [P, KB])
        head_big = sb("head_big", [P, HEADS])

        def pb(name):
            return ctx.enter_context(nc.psum_tensor(name, [P, 512], F32))

        psV = [pb(f"psV{i}") for i in range(2)]
        psB = [pb(f"psB{i}") for i in range(2)]
        psS = [pb(f"psS{i}") for i in range(2)]
        psC = pb("psC")
        psT = pb("psT")
        row_bank = [psS[0], psS[1], psC]
        ps_asrc, ps_adst = psC[:, 0:P], psC[:, P:2 * P]
        ps_row, ps_row2 = psC[0:1, 2 * P:3 * P], psC[0:1, 3 * P:4 * P]
        ps_col, ps_col2 = psT[:, 3 * P:3 * P + 1], psC[:, 2 * P:2 * P + 1]

        pads = sem("pads")
        dst_in = sem("dst_in")
        edges_in = sem("edges_in")
        consts_in = sem("consts_in")
        dst_out = sem("dst_out")
        consts = sem("consts")
        dve_step = sem("dve_step")
        floats = sem("floats")
        masks_made = sem("masks_made")
        setup_out = sem("setup_out")
        turned = sem("turned")
        turned_used = sem("turned_used")
        zeroed = sem("zeroed")
        digits = sem("digits")
        chunk_count = sem("chunk_count")
        shifted = sem("shifted")
        ends_made = sem("ends_made")
        ends_out = sem("ends_out")
        attw = sem("attw")
        attw_used = sem("attw_used")
        pick_made = sem("pick_made")
        search_step = sem("search_step")
        search_in = [sem(f"search_in{i}") for i in range(2)]
        search_rows = [sem(f"search_rows{i}") for i in range(2)]

        def phase_sems(tag, pairs, singles):
            named = {name: [sem(f"{tag}_{name}_{i}") for i in range(2)] for name in pairs.split()}
            named.update({name: sem(f"{tag}_{name}") for name in singles.split()})
            return named

        gat_only = "asrc logits l_made l_row m_made m_col x_made exps d_made d_rows d_scan d_col d_final weights_t sums_t chain "
        steps = "v_made v_turned c_spread c_copied scanned s_turned r_made"
        pairs = "idx_in loads gathered batch_done stored"
        gat = phase_sems("gat", pairs, gat_only + steps)
        es = [gat, gat, phase_sems("max", pairs, steps)]
        zd_in, zd_out = sem("zd_in"), sem("zd_out")
        bias_in = sem("bias_in")
        last_read = [sem(f"last_read{i}") for i in range(2)]
        placed = phase_sems("place", "in_ sent", "first_in first_out")
        after_gat = "chain xd ex "
        ns = [phase_sems(f"node{l}", "in_ stored" + ("", " got", " got used", " got used z_in")[l],
                   ("", after_gat + "o_made ", after_gat + "weighted merged o_normed std_in std_out ", "chain o_made o_normed std_in std_out hid_ps hid ")[l] +
                   "xt_ps xt h_ps h") for l in range(4)]

        def spread(v):
            return v.rearrange("(a n) -> a n", a=1).to_broadcast([P, HID])

        const_loads = [(Wx[0][:, 0:HID], W_1), (Wx[1][:, 0:HID], W_2), (Wz[:, 0:HID], Wm[HID:2 * HID, :]), (Wz[:, HID:2 * HID], Wm[0:HID, :]),
                       (wwb[:, :], Wm[2 * HID:2 * HID + 1, :].to_broadcast([P, HID])), (bmr[:, :], bm.rearrange("(a n) -> a n", a=1)),
                       (U1z[:, :], U1[0:HID, :]), (U1a[:, :], U1[HID:2 * HID, :]), (U2s[:, :], U2),
                       (b1c[:, :], b1.rearrange("(n a) -> n a", a=1)), (b2r[:, :], b2.rearrange("(a n) -> a n", a=1)),
                       (bias1c[:, :], bias_1.rearrange("(n a) -> n a", a=1))]
        for l, pair in enumerate(((att_src_1, att_dst_1), (att_src_2, att_dst_2))):
            for n, a in enumerate(pair):
                for h in range(HEADS):
                    col = n * HEADS + h
                    const_loads.append((att[l][h * HD:(h + 1) * HD, col:col + 1], a[h:h + 1, :].rearrange("a f -> f a")))
        N_CONSTS = len(const_loads)

        def in_dmas(l):
            return 16 * (2 if l == 2 else 1)

        block = ctx.enter_context(nc.Block())
        HALF = NB // 2
        NHALF = NG // 2
        before = [0, HALF, 0]
        node_before = [0, NHALF]

        def node_rows(t, group, width):
            return t.rearrange("(p t) f -> p t f", t=NT)[:, bass.ds(group * GT, GT), 0:width]

        @block.sync
        def _(sp):
            sp.wait_ge(pads, 4)
            def edges(flat, to, landed):
                sp.dma_start(to[:, 0:KB - 1, :], flat[0:lo].rearrange("(k p f) -> p k f", p=P, f=P)).then_inc(landed, 16)
                sp.dma_start(to[0:r, KB - 1, :], flat[lo:FULL_CH * P].rearrange("(p f) -> p f", f=P)).then_inc(landed, 16)
                sp.dma_start(to[r:r + 1, KB - 1, 0:TAIL], flat[FULL_CH * P:N_EDGES].rearrange("(p f) -> p f", p=1)).then_inc(landed, 16)

            lo = (KB - 1) * P * P
            r = FULL_CH - (KB - 1) * P
            edges(dst, dst_i, dst_in)
            edges(src, src_i, edges_in)
            edges(edge_weight, ew_f, edges_in)
            sp.dma_start(prev_i[:, 1:KB - 1, :], dst[P * P - 1:(KB - 1) * P * P - 1].rearrange("(k p f) -> p k f", p=P, f=P)).then_inc(edges_in, 16)
            sp.dma_start(prev_i[1:P, 0, :], dst[P - 1:P * P - 1].rearrange("(p f) -> p f", f=P)).then_inc(edges_in, 16)
            sp.dma_start(prev_i[0:1, 0, 1:P], dst[0:P - 1].rearrange("(p f) -> p f", p=1)).then_inc(edges_in, 16)
            sp.dma_start(prev_i[0:r, KB - 1, :], dst[lo - 1:FULL_CH * P - 1].rearrange("(p f) -> p f", f=P)).then_inc(edges_in, 16)
            sp.dma_start(prev_i[r:r + 1, KB - 1, 0:TAIL + 1], dst[FULL_CH * P - 1:N_EDGES].rearrange("(p f) -> p f", p=1)).then_inc(edges_in, 16)
            sp.wait_ge(floats, 1)
            sp.dma_start(d_dst.rearrange("(k p) f -> p k f", p=P), dst_f).then_inc(dst_out, 16)
            sp.wait_ge(zeroed, 1)
            n = E_PAD * HEADS // (P * SE)
            sp.dma_start(adst_at[0:E_PAD, :].rearrange("(p n e) h -> p n (e h)", p=P, n=n),
                         CBC[:, 0:1, :].to_broadcast([P, n, SE])).then_inc(setup_out, 16)
            sp.wait_ge(masks_made, 1)
            mk = d_mask.rearrange("(k q) c m f -> q m c k f", q=P // CB)
            ck = d_carry.rearrange("(k q) c -> q c k", q=P // CB)
            for q in range(P // CB):
                rows = slice(q * CB, q * CB + CB)
                sp.dma_start(mk[q, 0], same[rows]).then_inc(setup_out, 16)
                sp.dma_start(mk[q, 1], same_neg[rows]).then_inc(setup_out, 16)
                sp.dma_start(ck[q, 1:HR, :], chunk_goes[rows, :]).then_inc(setup_out, 16)
            sp.dma_start(d_carry[:, 0:1], head_big[0:NB, 0:1]).then_inc(setup_out, 16)
            sp.wait_ge(ends_made, 1)
            sp.dma_start(d_first, smalli[0:NP, 1, :]).then_inc(ends_out, 16)
            sp.dma_start(d_last, smalli[0:NP, 2, :]).then_inc(ends_out, 16)
            sp.wait_ge(ends_out, 32)
            n_setup = (P // CB) * 3 + 1 + 1
            sp.wait_ge(setup_out, 16 * n_setup)

            def lanes_out():
                sp.wait_ge(turned_used, 2 * KB)
                for q in range(P // CB):
                    rows = slice(q * CB, q * CB + CB)
                    sp.dma_start(d_idx.rearrange("(k q) p c -> q p k c", q=P // CB)[q], src_t[:, :, rows]).then_inc(setup_out, 16)
                    sp.dma_start(d_ew.rearrange("(k q) p c -> q p k c", q=P // CB)[q], prev_f[:, :, rows]).then_inc(setup_out, 16)

            def idx_load(l, it, par):
                indices, gathered = d_idx[2 * (it - before[l]) + par], 16 * CB * it
                if due(gathered):
                    sp.wait_ge(es[l]["gathered"][par], gathered)
                sp.dma_start(idx[:, par, :], indices).then_inc(es[l]["idx_in"][par], 16)

            def place_loads(l):
                def body(it):
                    for par in range(2):
                        tiles = bass.ds((2 * (it - node_before[l]) + par) * GT, GT)
                        table_rows, sent = 16 * (it - node_before[l]) + 16, 16 * GT * it
                        sp.wait_ge(ns[l]["stored"][par], table_rows)
                        sp.nop(nofuse=True)
                        if due(sent):
                            sp.wait_ge(placed["sent"][par], sent)
                        sp.dma_start(q_idx[0:NP, par, :], d_first[:, tiles]).then_inc(placed["in_"][par], 16)
                        sp.dma_start(q_adst[0:NP, par], table[l].rearrange("(p t) f -> p t f", t=NT)[:, tiles, HID + HEADS:ROW]).then_inc(placed["in_"][par], 16)
                        if l == 0 and par and isinstance(it, int) and it == 0:
                            lanes_out()
                rounds(sp, NHALF, body, node_before[l])
                if l == 0:
                    sp.wait_ge(setup_out, 16 * (n_setup + 2 * (P // CB)))
                for par in range(2):
                    idx_load(l, before[l], par)
                for par in range(2):
                    sp.wait_ge(placed["sent"][par], 16 * GT * NHALF * (l + 1))
                sp.wait_ge(placed["first_in"], 16 * KB * (l + 1))
                starts = adst_at[0:E_PAD, :].rearrange("(k p e) h -> p k (e h)", p=P, e=P)[:, :, 0:HEADS]
                sp.dma_start(starts, chunk_adst[:, l]).then_inc(placed["first_out"], 16)
                sp.wait_ge(placed["first_out"], 16 * (l + 1))

            def edge_loads(l):
                s, width = es[l], ROW if l < 2 else HID

                def results_out(it, par):
                    b = 2 * it + par
                    rows = result[l][bass.ds((b - 2 * before[l]) * BE, BE), :].rearrange("(c p) f -> p c f", p=P)
                    for n in range(PARTS):
                        cs = slice(n * CB // PARTS, (n + 1) * CB // PARTS)
                        sp.wait_ge(s["r_made"], b * NS + (n + 1) * NS // PARTS)
                        sp.dma_start(rows[:, cs], R[:, par, cs, 0:width]).then_inc(s["stored"][par], 16)

                def body(it):
                    first = isinstance(it, int) and it == before[l]
                    for par in range(2):
                        b = 2 * (it - before[l]) + par
                        if not (first and l < 2):
                            idx_load(l, it, par)
                        if not first:
                            results_out(it - 1, par)
                        if due(it):
                            sp.wait_ge(s["batch_done"][par], it)
                        for h in range(HEADS):
                            sp.dma_start(mask[h * CB:(h + 1) * CB, par], d_mask[b]).then_inc(s["loads"][par], 16)
                        if l < 2:
                            sp.dma_start(adst_in[:, par], adst_at[bass.ds(b * BE, BE), :].rearrange("(c p) h -> c p h", p=P)).then_inc(s["loads"][par], 16)
                            sp.dma_start(carry_mask[:, par], d_carry[bass.ds(b, 1)].unsqueeze(1).to_broadcast([1, HEADS, HR])).then_inc(s["loads"][par], 16)
                        else:
                            sp.dma_start(ewt[:, par, :], d_ew[b]).then_inc(s["loads"][par], 16)
                    if l == 2 and not first:
                        for par in range(2):
                            sp.wait_ge(ns[2]["stored"][par], 32 * NHALF)
                        z_rows, turns = zrow.rearrange("(p t) f -> p t f", t=NT)[:, bass.ds((it - 1) * ZT, ZT), :], NT + it - 1
                        sp.wait_ge(ns[2]["xt_ps"], turns)
                        sp.dma_start(xg[0:NP, 0, 0:ZT], z_rows).then_inc(zd_in, 16)
                rounds(sp, HALF, body, before[l])
                for par in range(2):
                    results_out(before[l] + HALF - 1, par)

            def node_loads(l):
                s = ns[l]
                if l == 2:
                    sp.wait_ge(pick_made, 1)
                    sp.dma_start(ident_row[NP:NP + 1, :], one[0:1, 0:NP]).then_inc(bias_in, 16)
                    sp.dma_start(own[:, :, :, :].rearrange("p a t f -> p (a t) f")[NP:NP + 1, :, 0:HID],
                                 bias_2.rearrange("(a b n) -> a b n", a=1, b=1).to_broadcast([1, 2 * GT, HID])).then_inc(bias_in, 16)

                def body(it):
                    for par in range(2):
                        g = 2 * it + par
                        indices = d_last[:, bass.ds(g * GT, GT)]
                        if due(it):
                            sp.wait_ge(s["got"][par], 16 * GT * it)
                        sp.dma_start(last_in[0:NP, par, :], indices).then_inc(last_read[par], 16)
                        if due(it):
                            if l == 1:
                                sp.wait_ge(s["o_made"], g - 1)
                            else:
                                sp.wait_ge(s["used"][par], it)
                        if l < 3:
                            sp.dma_start(own[0:NP, par], node_rows(table[l - 1], g, ROW)).then_inc(s["in_"][par], 16)
                        else:
                            sp.dma_start(own[0:NP, par, :, 0:HID], node_rows(zdst, g, HID)).then_inc(s["in_"][par], 16)
                        if l == 2:
                            sp.dma_start(xg[0:NP, par], node_rows(x, g, HID)).then_inc(s["in_"][par], 16)
                        if l == 3:
                            if due(it):
                                sp.wait_ge(s["h"], (g - 1) * len(BANKS))
                            sp.dma_start(xg[0:NP, par], node_rows(zrow, g, HID)).then_inc(s["z_in"][par], 16)
                        if l == 2 and par and due(it):
                            z_out(it - 1, 0)
                        elif l == 2 and not par and due(it - 1):
                            z_out(it - 2, 1)

                def z_out(it, par):
                    g = 2 * it + par
                    products, z = node_rows(ztable, g, HID), node_rows(zrow, g, HID)
                    sp.wait_ge(s["h"], g * GT + GT)
                    sp.dma_start(products, HTt[0:NP, par, :, 0:HID]).then_inc(s["stored"][par], 16)
                    sp.dma_start(z, O[0:NP, par]).then_inc(s["stored"][par], 16)

                rounds(sp, NHALF, body, peel=2 if l == 2 else 1)
                if l == 2:
                    z_out(NHALF - 2, 1)
                    for par in range(2):
                        z_out(NHALF - 1, par)

            place_loads(0)
            edge_loads(0)
            node_loads(1)
            place_loads(1)
            edge_loads(1)
            node_loads(2)
            edge_loads(2)
            sp.wait_ge(zd_out, 16 * NZ)
            node_loads(3)
            for par in range(2):
                sp.wait_ge(ns[3]["stored"][par], 16 * NHALF)

        @block.gpsimd
        def _(pool):
            pool.memset(ident[:, :], 0.0).then_inc(consts, 1)
            pool.wait_ge(consts, 1)
            pool.affine_select(out=ident[:, :], in_=ident[:, :], compare_op=ALU.not_equal, fill=1.0, base=0,
                               pattern=[[-1, P]], channel_multiplier=1).then_inc(consts, 1)
            pool.iota(node[:, :], [[1, NT]], base=0, channel_multiplier=NT,
                      allow_small_or_imprecise_dtypes=True).then_inc(consts, 1)
            pool.iota(hundreds[:, :], [[NT, NP + 1]], base=0, channel_multiplier=0,
                      allow_small_or_imprecise_dtypes=True).then_inc(consts, 1)
            pool.iota(units[:, :], [[1, NT]], base=0, channel_multiplier=0,
                      allow_small_or_imprecise_dtypes=True).then_inc(consts, 1)

            def gather(to, table_ap, index, s):
                pool.indirect_dma_start(to, None, table_ap, bass.IndirectOffsetOnAxis(ap=index, axis=0)).then_inc(s, 16)

            pool.wait_ge(dst_out, 16)
            def search(it):
                for par in range(2):
                    pool.wait_ge(search_in[par], it + 1)
                    pool.nop(nofuse=True)
                    for j in range(GT):
                        gather(rows_dst[0:NP, par, j, :], d_dst, q_idx[0:NP, par, j:j + 1], search_rows[par])
            rounds(pool, NHALF, search)

            def place(l):
                s = placed

                def chunk_starts():
                    for par in range(2):
                        pool.wait_ge(ns[l]["stored"][par], 16 * NHALF)
                    for k in range(KB):
                        pool.indirect_dma_start(chunk_adst[:, l, k, :], None, table[l],
                                                bass.IndirectOffsetOnAxis(ap=chunk_first[:, k:k + 1], axis=0),
                                                element_offset=HID + HEADS).then_inc(s["first_in"], 16)

                def body(it):
                    for par in range(2):
                        pool.wait_ge(s["in_"][par], 32 * it + 32)
                        pool.nop(nofuse=True)
                        for j in range(GT):
                            pool.indirect_dma_start(adst_at, bass.IndirectOffsetOnAxis(ap=q_idx[0:NP, par, j:j + 1], axis=0),
                                                    q_adst[0:NP, par, j, :], None).then_inc(s["sent"][par], 16)

                if l == 0:
                    chunk_starts()
                rounds(pool, NHALF, body, node_before[l])
                if l == 1:
                    chunk_starts()

            def edge_gathers(l):
                s, tab, width = es[l], (table[0], table[1], ztable)[l], (ROW, ROW, HID)[l]
                def body(it):
                    for par in range(2):
                        if due(it):
                            pool.wait_ge(s["batch_done"][par], it)
                            pool.nop(nofuse=True)
                        pool.wait_ge(s["idx_in"][par], 16 * it + 16)
                        pool.nop(nofuse=True)
                        for c in range(CB):
                            gather(G[:, par, c, 0:width], tab, idx[:, par, c:c + 1], s["gathered"][par])
                rounds(pool, HALF, body, before[l])

            def node_gathers(l):
                s, width = ns[l], (0, ROW, ROW, HID)[l]
                for par in range(2):
                    pool.wait_ge(es[l - 1]["stored"][par], 16 * PARTS * (before[l - 1] + HALF))

                def body(it):
                    for par in range(2):
                        if due(it):
                            if l == 1:
                                pool.wait_ge(s["o_made"], 2 * it + par - 1)
                            else:
                                pool.wait_ge(s["used"][par], it)
                            pool.nop(nofuse=True)
                        pool.wait_ge(last_read[par], 16 * (it + (l - 1) * NHALF + 1))
                        pool.nop(nofuse=True)
                        for j in range(GT):
                            gather(ends[0:NP, par, j, 0:width], result[l - 1], last_in[0:NP, par, j:j + 1], s["got"][par])
                rounds(pool, NHALF, body)

            place(0)
            edge_gathers(0)
            node_gathers(1)
            place(1)
            edge_gathers(1)
            node_gathers(2)
            for par in range(2):
                pool.wait_ge(ns[2]["stored"][par], 32 * NHALF)
            edge_gathers(2)
            node_gathers(3)

        @block.tensor
        def _(pe):
            def turn(to, frm, n=P):
                return pe.transpose(to, frm, ident[0:n, 0:n])

            pe.wait_ge(consts, 2)
            pe.wait_ge(pads, 4)
            pe.wait_ge(digits, 1)
            for k in range(KB):
                pe.matmul(psC[0:NP, 0:NT], LT[:, k, 0:NP], ones[:, :], start=(k == 0), stop=False)
                mm = pe.matmul(psC[0:NP, 0:NT], hit[:, k, :], below[:, k, :], start=False, stop=(k == KB - 1))
            mm.then_inc(chunk_count, 1)
            pe.wait_ge(consts_in, 16 * N_CONSTS)
            for l in range(2):
                turn(psV[l][:, 0:P], Wx[l][:, 0:HID]).then_inc(attw, 1)
                pe.wait_ge(attw_used, 2 * l + 1)
                pe.matmul(psB[l][:, 0:2 * HEADS], wt[:, :], att[l][:, :], start=True, stop=True).then_inc(attw, 1)
            def project(l, frm, n_out, weights):
                s = ns[l]
                def multiply(it, par):
                    g = 2 * it + par

                    def turn_tile(j):
                        if due(g * GT + j - 1):
                            pe.wait_ge(s["xt"], g * GT + j - 1)
                        if l == 2:
                            pe.wait_ge(s["o_normed"], g * GT + j + 1)
                        turn(psV[j % 2][:, 0:NP], frm[0:NP, par, j, :], NP).then_inc(s["xt_ps"], 1)

                    if l == 0:
                        pe.wait_ge(s["in_"][par], 16 * it + 16)
                    elif l == 1:
                        pe.wait_ge(s["o_made"], g + 1)
                    turn_tile(0)
                    for j in range(GT):
                        n, two = g * GT + j, j % 2
                        if j + 1 < GT:
                            turn_tile(j + 1)
                        pe.wait_ge(s["xt"], n + 1)
                        if due(n - 1):
                            pe.wait_ge(s["h"], n - 1)
                        pe.matmul(psB[two][0:NP, 0:n_out], XT[:, two, 0:NP], weights, start=True, stop=True).then_inc(s["h_ps"], 1)

                def merge(it, par):
                    pe.wait_ge(s["weighted"], 2 * it + par + 1)
                    for n, (a, z) in enumerate(BANKS):
                        pe.matmul(row_bank[n][0:NP, 0:(z - a) * HID].rearrange("p (t f) -> p t f", f=HID), ident_row[0:NP + 1, :],
                                  own[0:NP + 1, par, a:z, 0:HID], start=True, stop=True).then_inc(s["merged"], 1)

                def body(it):
                    for par in range(2):
                        if l == 2:
                            merge(it, par)
                            if par:
                                multiply(it, 0)
                            elif due(it):
                                multiply(it - 1, 1)
                        else:
                            multiply(it, par)
                if l == 2:
                    pe.wait_ge(bias_in, 32)
                rounds(pe, NHALF, body)
                if l == 2:
                    multiply(NHALF - 1, 1)

            pe.wait_ge(attw_used, 4)
            project(0, xg, ROW, Wx[0][:, :])
            pe.wait_ge(shifted, 1)
            pe.matmul(psC[0:NP, 2 * P:2 * P + 1], ident[0:NP + 1, 1:NP + 1], edge_of[0:NP + 1, 0:1], start=True, stop=True).then_inc(shifted, 1)
            pe.wait_ge(floats, 2)
            for k in range(KB):
                for n, frm in enumerate((src_f, ew_f)):
                    if due(2 * k + n - 1):
                        pe.wait_ge(turned_used, 2 * k + n - 1)
                    if k == 0:
                        pe.wait_ge(attw_used, 4)
                    turn(psS[n][:, 0:P], frm[:, k, :]).then_inc(turned, 1)

            def edge_pe(l):
                s, gat = es[l], l < 2
                def body(it):
                    for par in range(2):
                        b = 2 * it + par
                        if gat:
                            pe.wait_ge(s["loads"][par], 96 * (it + 1))
                            pe.wait_ge(s["asrc"], b + 1)
                            turn(ps_asrc, A[:, :])
                            for h in range(HEADS):
                                mm = pe.matmul(ps_adst, put[:, h, :], adst_in[:, par, :, h], start=(h == 0), stop=(h == HEADS - 1))
                            mm.then_inc(s["logits"], 1)
                            pe.wait_ge(s["l_made"], b + 1)
                            pe.matmul(ps_row, L[:, P - 1:P], ident[:, :], start=True, stop=True).then_inc(s["l_row"], 1)
                            pe.wait_ge(s["m_made"], b + 1)
                            pe.matmul(ps_col, m_pre[:, :], one[0:1, 0:1], start=True, stop=True).then_inc(s["m_col"], 1)
                            pe.wait_ge(s["exps"], b + 1)
                            turn(psT[:, 0:P], EX[:, 0, :]).then_inc(s["weights_t"], 1)
                            coeff = EX[:, 1, :]
                        else:
                            pe.wait_ge(s["loads"][par], 80 * (it + 1))
                            coeff = mask[:, par, 1, :]

                        def results(st):
                            g = b * NS + st
                            pe.wait_ge(s["scanned"], g + 1)
                            if st >= 2 or not gat:
                                if due(g - 1):
                                    pe.wait_ge(s["r_made"], g - 1)
                            for j in range(SC):
                                tr = turn(psS[st % 2][:, j * P:(j + 1) * P], ST[:, st % 2, j * P:(j + 1) * P])
                                if st == NS - 1 and j == 0:
                                    tr.then_inc(s["batch_done"][par], 1)
                            tr.then_inc(s["s_turned"], 1)

                        def spread(st):
                            g = b * NS + st
                            if st >= 2 or not gat:
                                if due(g - 1):
                                    pe.wait_ge(s["c_copied"], g - 1)
                            for j in range(SC):
                                mm = pe.matmul(psB[st % 2][:, j * P:(j + 1) * P], pick[:, st * SC + j, :], coeff, start=True, stop=True)
                            mm.then_inc(s["c_spread"], 1)

                        if gat:
                            spread(0)
                            pe.wait_ge(s["d_made"], b + 1)
                            pe.matmul(ps_row2, D[:, P - 1:P], ident[:, :], start=True, stop=True).then_inc(s["d_rows"], 1)
                            spread(1)
                            pe.wait_ge(s["d_scan"], b + 1)
                            pe.matmul(ps_col2, d_pre[:, :], one[0:1, 0:1], start=True, stop=True).then_inc(s["d_col"], 1)
                        for st in range(NS):
                            g = b * NS + st
                            if st >= 2 or not gat:
                                spread(st)
                            pe.wait_ge(s["v_made"], g + 1)
                            if st >= 2 or not gat:
                                if due(g - 1):
                                    pe.wait_ge(s["scanned"], g - 1)
                            for j in range(SC):
                                tr = turn(psV[st % 2][:, j * P:(j + 1) * P], V[:, st % 2, j, :])
                            tr.then_inc(s["v_turned"], 1)
                            if gat and st == 0:
                                pe.wait_ge(s["d_final"], b + 1)
                                turn(psC[:, 0:P], M[:, 1:P + 1])
                                turn(psC[:, P:2 * P], D[:, :]).then_inc(s["sums_t"], 1)
                            if st:
                                results(st - 1)
                        results(NS - 1)
                        if not gat and due(it):
                            z, tiles = ns[2], [slice(j * P, j * P + NP) for j in range(ZT)]
                            if par == 0:
                                pe.wait_ge(zd_in, 16 * it)
                                for j in range(ZT):
                                    tr = turn(psC[:, tiles[j]], xg[0:NP, 0, j, :], NP)
                                tr.then_inc(z["xt_ps"], 1)
                            else:
                                pe.wait_ge(z["xt"], NT + it)
                                pe.nop(nofuse=True)
                                pe.wait_ge(z["h"], NT + it - 1)
                                for j in range(ZT):
                                    zd = psT[0:NP, j * HID:(j + 1) * HID]
                                    pe.matmul(zd, one[0:1, 0:NP], bmr[0:1, :], start=True, stop=False)
                                    mm = pe.matmul(zd, ZX[:, tiles[j]], Wz[:, HID:2 * HID], start=False, stop=True)
                                mm.then_inc(z["h_ps"], 1)
                rounds(pe, HALF, body, before[l])

            pe.wait_ge(pick_made, 1)
            edge_pe(0)
            project(1, O, ROW, Wx[1][:, :])
            edge_pe(1)
            project(2, O, HID, Wz[:, 0:HID])
            pe.wait_ge(ns[2]["h"], NT)
            edge_pe(2)

            def final_pe():
                s = ns[3]
                def body(it):
                    for par in range(2):
                        g = 2 * it + par

                        def turn_tile(j):
                            if due(g * GT + j - 1):
                                pe.wait_ge(s["xt"], g * GT + j - 1)
                            turn(psV[j % 2][:, 0:NP], xg[0:NP, par, j, :], NP)
                            turn(psV[j % 2][:, HID:HID + NP], O[0:NP, par, j, :], NP).then_inc(s["xt_ps"], 1)

                        def hidden(j):
                            n, two = g * GT + j, j % 2
                            pe.wait_ge(s["xt"], n + 1)
                            if due(n - 1):
                                pe.wait_ge(s["hid"], n - 1)
                            pe.matmul(psB[two][:, 0:NP], U1z[:, :], XT[:, two, 0:NP], start=True, stop=False)
                            pe.matmul(psB[two][:, 0:NP], U1a[:, :], XT[:, two, HID:HID + NP], start=False, stop=True).then_inc(s["hid_ps"], 1)

                        pe.wait_ge(s["z_in"][par], 16 * it + 16)
                        pe.wait_ge(s["o_made"], g + 1)
                        turn_tile(0)
                        turn_tile(1)
                        hidden(0)
                        for j in range(GT):
                            if j + 2 < GT:
                                turn_tile(j + 2)
                            if j + 1 < GT:
                                hidden(j + 1)
                            pe.wait_ge(s["hid"], g * GT + j + 1)
                            bank, spot = j // BT, j % BT
                            if spot == 0 and due((g - 1) * len(BANKS) + bank + 1):
                                pe.wait_ge(s["h"], (g - 1) * len(BANKS) + bank + 1)
                            rows = row_bank[bank][0:NP, spot * HID:(spot + 1) * HID]
                            pe.matmul(rows, one[0:1, 0:NP], b2r[:, :], start=True, stop=False)
                            pe.matmul(rows, V[:, j % 2, 0, 0:NP], U2s[:, :], start=False, stop=True).then_inc(s["h_ps"], 1)
                rounds(pe, NHALF, body)
            final_pe()

        @block.scalar
        def _(act):
            act.wait_ge(pads, 4)
            act.wait_ge(dst_in, 48)
            for to, frm in const_loads:
                act.dma_start(to, frm).then_inc(consts_in, 16)

            for l in range(2):
                act.wait_ge(attw, 2 * l + 1)
                act.activation(wt[:, :], psV[l][:, 0:P], ACT.Copy).then_inc(attw_used, 1)
                act.wait_ge(attw, 2 * l + 2)
                act.activation(Wx[l][:, HID:ROW], psB[l][:, 0:2 * HEADS], ACT.Copy).then_inc(attw_used, 1)

            def project_act(l):
                s, width, per = ns[l], (ROW, ROW, HID)[l], (16, 16, 32)[l]

                def x_in(it, par):
                    act.dma_start(xg[0:NP, par], node_rows(x, 2 * it + par, HID)).then_inc(s["in_"][par], 16)

                def project(it, par):
                    g = 2 * it + par

                    def turned_rows(j):
                        n = g * GT + j
                        act.wait_ge(s["xt_ps"], n + 1)
                        if due(n - 1):
                            act.wait_ge(s["h_ps"], n - 1)
                        if l == 1:
                            act.activation(XT[:, j % 2, 0:NP], psV[j % 2][:, 0:NP], ACT.Relu, bias=bias1c[:, 0:1]).then_inc(s["xt"], 1)
                        else:
                            act.activation(XT[:, j % 2, 0:NP], psV[j % 2][:, 0:NP], ACT.Copy).then_inc(s["xt"], 1)

                    if due(per * it):
                        act.wait_ge(s["stored"][par], per * it)
                    turned_rows(0)
                    for j in range(GT):
                        if j + 1 < GT:
                            turned_rows(j + 1)
                        act.wait_ge(s["h_ps"], g * GT + j + 1)
                        act.activation(HTt[0:NP, par, j, 0:width], psB[j % 2][0:NP, 0:width], ACT.Copy).then_inc(s["h"], 1)
                    if l < 2:
                        act.wait_ge(s["h"], g * GT + GT)
                        act.dma_start(node_rows(table[l], g, ROW), HTt[0:NP, par, :, 0:ROW]).then_inc(s["stored"][par], 16)

                if l == 0:
                    def body(it):
                        for par in range(2):
                            project(it, par)
                            x_in(it + 1, par)
                    for par in range(2):
                        x_in(0, par)
                    rounds(act, NHALF - 1, body)
                    for par in range(2):
                        project(NHALF - 1, par)
                else:
                    def body(it):
                        for par in range(2):
                            g = 2 * it + par
                            act.wait_ge(s["xd"], g + 1)
                            act.activation(self_w[0:NP], self_x[0:NP], ACT.Exp).then_inc(s["ex"], 1)
                            if l == 2 and due(g):
                                act.wait_ge(s["std_in"], g)
                                act.activation(std[0:NP], mv[0:NP, :, 1], ACT.Sqrt, bias=eps[0:NP, 0:1]).then_inc(s["std_out"], 1)
                            if par:
                                project(it, 0)
                            elif due(it):
                                project(it - 1, 1)
                    rounds(act, NHALF, body, peel=2)
                    if l == 2:
                        act.wait_ge(s["std_in"], NG)
                        act.activation(std[0:NP], mv[0:NP, :, 1], ACT.Sqrt, bias=eps[0:NP, 0:1]).then_inc(s["std_out"], 1)
                    project(NHALF - 1, 1)

            project_act(0)

            def zd_act(it, par):
                z, n = ns[2], NT + it
                if par == 0:
                    act.wait_ge(z["xt_ps"], n)
                    act.activation(ZX.rearrange("p (t n) -> p t n", n=P)[:, :, 0:NP], psC[:, :].rearrange("p (t n) -> p t n", n=P)[:, :, 0:NP], ACT.Copy).then_inc(z["xt"], 1)
                else:
                    act.wait_ge(z["h_ps"], n)
                    act.nop(nofuse=True)
                    for half in range(2):
                        act.wait_ge(z["stored"][half], 32 * NHALF)
                    if due(16 * (it - 1)):
                        act.wait_ge(zd_out, 16 * (it - 1))
                    act.activation(HTt[0:NP, 0, 0:ZT, 0:HID], psT[0:NP, :].rearrange("p (t f) -> p t f", f=HID), ACT.Copy).then_inc(z["h"], 1)
                    zd_rows = zdst.rearrange("(p t) f -> p t f", t=NT)[:, bass.ds((it - 1) * ZT, ZT), :]
                    act.wait_ge(z["h"], n)
                    act.dma_start(zd_rows, HTt[0:NP, 0, 0:ZT, 0:HID]).then_inc(zd_out, 16)

            def edge_act(l):
                s, gat = es[l], l < 2
                width = ROW if gat else HID
                def body(it):
                    for par in range(2):
                        b = 2 * it + par
                        if gat:
                            act.wait_ge(s["gathered"][par], 16 * CB * (it + 1))
                            act.activation(A[:, :].rearrange("p (h c) -> p c h", h=HEADS), G[:, par, :, HID:HID + HEADS], ACT.Copy).then_inc(s["asrc"], 1)
                            act.wait_ge(s["x_made"], b + 1)
                            act.activation(k_exp[:, :], k_row[:, :], ACT.Exp)
                            act.activation(EX[:, :, :], XD[:, :, :], ACT.Exp).then_inc(s["exps"], 1)

                        def before_rows():
                            if due(16 * PARTS * it):
                                act.wait_ge(s["stored"][par], 16 * PARTS * it)
                            if gat:
                                act.wait_ge(s["sums_t"], b + 1)
                                for n in range(2):
                                    act.activation(R[:, par, :, HID + n * HEADS:HID + n * HEADS + HEADS],
                                                   psC[:, (1 - n) * P:(2 - n) * P].rearrange("p (h c) -> p c h", c=CB), ACT.Copy)

                        def rows(st):
                            g = b * NS + st
                            act.wait_ge(s["s_turned"], g + 1)
                            act.activation(R[:, par, st * SC:(st + 1) * SC, 0:HID],
                                           psS[st % 2][:, :].rearrange("p (c f) -> p c f", f=HID), ACT.Copy).then_inc(s["r_made"], 1)

                        for st in range(NS):
                            g = b * NS + st
                            act.wait_ge(s["c_spread"], g + 1)
                            if st >= 2 or not gat:
                                if due(g - 1):
                                    act.wait_ge(s["scanned"], g - 1)
                            act.activation(CBC[:, st % 2, :], psB[st % 2][:, :], ACT.Copy).then_inc(s["c_copied"], 1)
                            if st == 1:
                                before_rows()
                            if st:
                                rows(st - 1)
                        rows(NS - 1)
                        if not gat and due(it):
                            zd_act(it, par)
                rounds(act, HALF, body, before[l], peel=1 if gat else 2)

            edge_act(0)
            project_act(1)
            edge_act(1)
            project_act(2)
            edge_act(2)

            def final_act():
                s = ns[3]

                def turned_rows(g, j):
                    n = g * GT + j
                    act.wait_ge(s["xt_ps"], n + 1)
                    if due(n - 1):
                        act.wait_ge(s["hid_ps"], n - 1)
                    act.activation(XT[:, j % 2, :].rearrange("p (a n) -> p a n", a=2)[:, :, 0:NP],
                                   psV[j % 2][:, 0:2 * HID].rearrange("p (a n) -> p a n", a=2)[:, :, 0:NP], ACT.Copy).then_inc(s["xt"], 1)

                def deviation(g):
                    act.wait_ge(s["std_in"], g + 1)
                    act.activation(std[0:NP], mv[0:NP, :, 1], ACT.Sqrt, bias=eps[0:NP, 0:1]).then_inc(s["std_out"], 1)

                def rows_out(it, par):
                    act.wait_ge(s["o_normed"], 2 * it + par + 1)
                    act.dma_start(node_rows(out, 2 * it + par, HID), HTt[0:NP, par, :, 0:HID]).then_inc(s["stored"][par], 16)

                def body(it):
                    for par in range(2):
                        g = 2 * it + par
                        turned_rows(g, 0)
                        for j in range(GT):
                            if j + 1 < GT:
                                turned_rows(g, j + 1)
                            n = g * GT + j
                            act.wait_ge(s["hid_ps"], n + 1)
                            if due(n - 1):
                                act.wait_ge(s["h_ps"], n - 1)
                            act.activation(V[:, j % 2, 0, 0:NP], psB[j % 2][:, 0:NP], ACT.Relu, bias=b1c[:, 0:1]).then_inc(s["hid"], 1)
                            if j == 1 and due(g):
                                deviation(g - 1)
                        if due(g):
                            if par:
                                rows_out(it, 0)
                            else:
                                rows_out(it - 1, 1)
                rounds(act, NHALF, body)
                deviation(NG - 1)
                rows_out(NHALF - 1, 1)
            final_act()

        @block.vector
        def _(dve):
            vec = nc.vector
            n_step = [0]

            def link(ins):
                n_step[0] += 1
                ins.then_inc(dve_step, 1)
                dve.wait_ge(dve_step, n_step[0])

            vec.memset(dst_i[:, KB - 1, :], N_NODES)
            vec.memset(prev_i[:, 0, :], -1)
            vec.memset(prev_i[:, KB - 1, :], N_NODES)
            vec.memset(src_i[:, KB - 1, :], 0)
            vec.memset(ew_f[:, KB - 1, :], 0.0).then_inc(pads, 1)
            vec.memset(att[0][:, :], 0.0)
            vec.memset(att[1][:, :], 0.0).then_inc(pads, 1)
            vec.memset(one[:, :], 1.0)
            vec.memset(ones[:, :], 1.0)
            vec.memset(eps[:, :], EPS)
            vec.memset(head_big[:, :], -BIG)
            vec.memset(k_row[:, :], -BIG)
            vec.memset(edge_of[:, :], float(N_EDGES)).then_inc(pads, 1)
            vec.memset(m_end[:, :, :], -BIG)
            vec.memset(d_end[:, :, :], 0.0).then_inc(pads, 1)
            vec.memset(CBC[:, :, :], 0.0).then_inc(zeroed, 1)

            dve.wait_ge(dst_in, 48)
            vec.tensor_copy(dst_f, dst_i).then_inc(floats, 1)
            dve.wait_ge(floats, 1)
            vec.tensor_scalar(chunk_first[:, :], dst_f[:, :, 0], float(N_NODES - 1), None, ALU.min)

            dve.wait_ge(consts, 5)
            for k in range(KB):
                last = dst_f[:, k, P - 1:P]
                vec.tensor_scalar(LT[:, k, :], hundreds[:, :], last, 0.0, ALU.is_gt, ALU.add, accum_out=small[:, 3, k:k + 1])
            link(vec.memset(small[:, 7, 2:3], 0.0))
            link(vec.tensor_scalar(small[:, 4, 0:KB], small[:, 3, 0:KB], float(NT), float(-NT * NP), ALU.mult, ALU.add))
            link(vec.tensor_tensor(small[:, 5, 0:KB], small[:, 4, 0:KB], dst_f[:, :, P - 1], ALU.add))
            vec.tensor_tensor(hit, LT[:, :, 1:NP + 1], LT[:, :, 0:NP], ALU.subtract)
            for k in range(KB):
                step = vec.tensor_scalar(below[:, k, :], units[:, :], small[:, 5, k:k + 1], None, ALU.is_gt)
            step.then_inc(digits, 1)

            dve.wait_ge(edges_in, 16 * 11)
            vec.tensor_copy(prev_f, prev_i)
            link(vec.tensor_copy(src_f, src_i))
            link(vec.tensor_tensor(same, dst_f, prev_f, ALU.is_equal))
            vec.memset(small[:, 7, 1:2], 0.0).then_inc(floats, 1)
            vec.tensor_scalar(same_neg, same, -1.0, BIG, ALU.add, ALU.mult)
            link(vec.tensor_reduce(small[:, 2, 0:KB], same, AX_X, ALU.min))
            link(vec.tensor_scalar(chunk_goes[:, :], small[:, 2, 0:KB], -1.0, BIG, ALU.add, ALU.mult))
            vec.memset(small[:, 7, 0:1], 0.0).then_inc(masks_made, 1)

            def search_chunks(g, par):
                vec.tensor_copy(q_idx[0:NP, par, :], smalli[0:NP, 0, bass.ds(g * GT, GT)]).then_inc(search_in[par], 1)

            dve.wait_ge(chunk_count, 1)
            link(vec.tensor_copy(small[0:NP, 6, :], psC[0:NP, 0:NT]))
            link(vec.tensor_copy(smalli[0:NP, 0, :], small[0:NP, 6, :]))
            for par in range(2):
                search_chunks(par, par)
            def chain_of(s, per_round, late=0):
                count = [0]

                def start(it):
                    count[0] = 0 if isinstance(it, int) and it == 0 else -late

                def step(ins, it):
                    count[0] += 1
                    ins.then_inc(s["chain"], 1)
                    dve.wait_ge(s["chain"], it * per_round + count[0])

                def end():
                    assert count[0] == per_round - late, count[0]
                return start, step, end

            def by_node(t, group):
                return t[0:NP, bass.ds(group * GT, GT)]

            def count_before(it, par):
                g = 2 * it + par
                dve.wait_ge(search_rows[par], 16 * GT * (it + 1))
                vec.tensor_tensor(O[0:NP, par], rows_dst[0:NP, par], by_node(node, g).unsqueeze(2).to_broadcast([NP, GT, P]),
                                  ALU.is_lt).then_inc(search_step, 1)
                dve.wait_ge(search_step, g + 1)
                return vec.tensor_reduce(by_node(edge_of, g), O[0:NP, par], AX_X, ALU.add)

            def search(it):
                for par in range(2):
                    count_before(it, par)
                    search_chunks(2 * (it + 1) + par, par)
            rounds(dve, NHALF - 1, search)
            for par in range(2):
                step = count_before(NHALF - 1, par)
            link(step)
            link(vec.scalar_tensor_tensor(edge_of[0:NP, :], small[0:NP, 6, :], float(P), edge_of[0:NP, :], ALU.mult, ALU.add))
            vec.tensor_copy(small[0:NP, 0, 0:NT - 1], edge_of[0:NP, 1:NT]).then_inc(shifted, 1)
            dve.wait_ge(shifted, 2)
            link(vec.tensor_copy(small[0:NP, 0, NT - 1:NT], psC[0:NP, 2 * P:2 * P + 1]))
            link(vec.tensor_tensor(has_edge[0:NP, :], small[0:NP, 0, :], edge_of[0:NP, :], ALU.is_gt))
            vec.tensor_scalar(max_bound[0:NP, :], has_edge[0:NP, :], 2 * BIG, -BIG, ALU.mult, ALU.add)
            vec.tensor_scalar(smalli[0:NP, 2, :], small[0:NP, 0, :], -1.0, 0.0, ALU.add, ALU.max)
            link(vec.tensor_scalar(small[0:NP, 2, :], node[0:NP, :], float(E_PAD), None, ALU.add))
            link(vec.tensor_tensor(small[0:NP, 3, :], edge_of[0:NP, :], small[0:NP, 2, :], ALU.subtract))
            link(vec.tensor_tensor(small[0:NP, 3, :], small[0:NP, 3, :], has_edge[0:NP, :], ALU.mult))
            vec.tensor_tensor(smalli[0:NP, 1, :], small[0:NP, 3, :], small[0:NP, 2, :], ALU.add).then_inc(ends_made, 1)

            for k in range(KB):
                dve.wait_ge(turned, 2 * k + 1)
                vec.tensor_copy(src_t[:, k, :], psS[0][:, 0:P]).then_inc(turned_used, 1)
                dve.wait_ge(turned, 2 * k + 2)
                vec.tensor_copy(prev_f[:, k, :], psS[1][:, 0:P]).then_inc(turned_used, 1)
            vec.tensor_copy(pick[:, :, :].rearrange("p c (h f) -> p c h f", h=HEADS),
                            ident[:, :].rearrange("p (h c) -> p c h", h=HEADS).unsqueeze(3).to_broadcast([P, CB, HEADS, HD]))
            vec.tensor_copy(ident_row[:, :], ident[:, 0:NP])
            link(vec.memset(put[:, :, :], 0.0))
            vec.memset(ST[:, :, :], 0.0)
            for h in range(HEADS):
                step = vec.tensor_copy(put[:, h, h * CB:(h + 1) * CB], ident[0:CB, 0:CB])
            step.then_inc(pick_made, 1)

            def flat(t):
                return t.rearrange("p h c -> p (h c)")

            def edge_dve(l):
                s, gat = es[l], l < 2
                start, step, end = chain_of(s, 24)
                def body(it):
                    start(it)
                    for par in range(2):
                        b = 2 * it + par
                        same01, same_big = mask[:, par, 0, :], mask[:, par, 1, :]
                        p, c = EX[:, 0, :], EX[:, 1, :]
                        if gat:
                            goes_on = flat(carry_mask[:, par])
                            dve.wait_ge(s["loads"][par], 96 * (it + 1))
                            dve.wait_ge(s["logits"], b + 1)
                            step(vec.tensor_tensor_scan(T[:, :], same01, ps_adst, 0.0, ALU.mult, ALU.add), it)
                            step(vec.tensor_tensor(U[:, :], ps_asrc, T[:, :], ALU.add), it)
                            step(vec.scalar_tensor_tensor(E[:, :], U[:, :], SLOPE, U[:, :], ALU.mult, ALU.max), it)
                            vec.tensor_tensor_scan(L[:, :], same_big, E[:, :], -BIG, ALU.add, ALU.max).then_inc(s["l_made"], 1)
                            vec.tensor_copy(m_row[:, :, 0], m_end[:, :, CB])
                            dve.wait_ge(s["l_row"], b + 1)
                            step(vec.tensor_copy(m_row[:, :, 1:HR], ps_row.rearrange("p (h c) -> p h c", h=HEADS)), it)
                            step(vec.tensor_tensor_scan(flat(m_end[:, :, :]), goes_on, flat(m_row[:, :, :]), -BIG, ALU.add, ALU.max), it)
                            vec.tensor_copy(m_pre[:, :].rearrange("p (h c) -> p h c", h=HEADS), m_end[:, :, 0:CB]).then_inc(s["m_made"], 1)
                            n = HEADS * HR
                            step(vec.tensor_tensor(k_row[:, 1:n], flat(m_end[:, :, :])[:, 0:n - 1], flat(m_end[:, :, :])[:, 1:n], ALU.subtract), it)
                            vec.tensor_tensor(k_row[:, 1:n], k_row[:, 1:n], goes_on[:, 1:n], ALU.add)
                            dve.wait_ge(s["m_col"], b + 1)
                            step(vec.tensor_copy(M[:, 0:1], ps_col), it)
                            step(vec.tensor_tensor_scan(M[:, 1:P + 1], same_big, E[:, :], M[:, 0:1], ALU.add, ALU.max), it)
                            step(vec.tensor_tensor(XD[:, 1, :], M[:, 0:P], same_big, ALU.add), it)
                            vec.tensor_tensor(XD[:, 0, :], E[:, :], M[:, 1:P + 1], ALU.subtract)
                            vec.tensor_tensor(XD[:, 1, :], XD[:, 1, :], M[:, 1:P + 1], ALU.subtract).then_inc(s["x_made"], 1)
                        else:
                            dve.wait_ge(s["loads"][par], 80 * (it + 1))
                            dve.wait_ge(s["gathered"][par], 16 * CB * (it + 1))

                        def values(st):
                            if st >= 2 or not gat:
                                if due(b * NS + st - 1):
                                    dve.wait_ge(s["v_turned"], b * NS + st - 1)
                            rows = G[:, par, st * SC:(st + 1) * SC, 0:HID]
                            if gat:
                                weights = psT[:, 0:P].rearrange("p (h c) -> p c h", h=HEADS)[:, st * SC:(st + 1) * SC, :]
                                ins = vec.tensor_tensor(V[:, st % 2].rearrange("p c (h f) -> p c h f", h=HEADS),
                                                        rows.rearrange("p c (h f) -> p c h f", h=HEADS),
                                                        weights.unsqueeze(3).to_broadcast([P, SC, HEADS, HD]), ALU.mult)
                            else:
                                for j in range(SC):
                                    ins = vec.scalar_tensor_tensor(V[:, st % 2, j, :], wwb[:, :], ewt[:, par, st * SC + j:st * SC + j + 1],
                                                                   rows[:, j, :], ALU.mult, ALU.add)
                            ins.then_inc(s["v_made"], 1)

                        if gat:
                            dve.wait_ge(s["exps"], b + 1)
                            vec.tensor_tensor_scan(D[:, :], c, p, 0.0, ALU.mult, ALU.add).then_inc(s["d_made"], 1)
                            vec.tensor_copy(d_rowv[:, :, 0], d_end[:, :, CB])
                            dve.wait_ge(s["weights_t"], b + 1)
                            values(0)
                            dve.wait_ge(s["d_rows"], b + 1)
                            step(vec.tensor_copy(d_rowv[:, :, 1:HR], ps_row2.rearrange("p (h c) -> p h c", h=HEADS)), it)
                            step(vec.tensor_tensor_scan(flat(d_end[:, :, :]), k_exp[:, :], flat(d_rowv[:, :, :]), 0.0, ALU.mult, ALU.add), it)
                            vec.tensor_copy(d_pre[:, :].rearrange("p (h c) -> p h c", h=HEADS), d_end[:, :, 0:CB]).then_inc(s["d_scan"], 1)
                            values(1)
                            dve.wait_ge(s["d_col"], b + 1)
                            step(vec.tensor_copy(D0[:, :], ps_col2), it)
                            vec.tensor_tensor_scan(D[:, :], c, p, D0[:, 0:1], ALU.mult, ALU.add).then_inc(s["d_final"], 1)
                        else:
                            values(0)
                        for st in range(NS):
                            g = b * NS + st
                            if st + 1 < NS and (st or not gat):
                                values(st + 1)
                            dve.wait_ge(s["c_copied"], g + 1)
                            dve.wait_ge(s["v_turned"], g + 1)
                            if due(g):
                                dve.wait_ge(s["scanned"], g)
                            if st >= 2 or not gat:
                                if due(g - 1):
                                    dve.wait_ge(s["s_turned"], g - 1)
                            vec.tensor_tensor_scan(ST[:, st % 2, :], CBC[:, st % 2, :], psV[st % 2][:, :], ST[:, 1 - st % 2, SE - 1:SE],
                                                   ALU.mult if gat else ALU.add, ALU.add if gat else ALU.max).then_inc(s["scanned"], 1)
                    if gat:
                        end()
                rounds(dve, HALF, body, before[l])

            def layernorm_start(l, rows, it, step):
                for j in range(GT):
                    ins = vec.bn_stats(stats[0:NP, j, :], rows[:, j, :])
                step(ins, it)
                dve.nop(nofuse=True)
                for j in range(GT):
                    ins = vec.bn_aggr(mv[0:NP, j, :], stats[0:NP, j, :])
                ins.then_inc(ns[l]["std_in"], 1)

            def layernorm_end(l, rows, g, it, step):
                dve.wait_ge(ns[l]["std_out"], g + 1)
                step(vec.reciprocal(rstd[0:NP, :], std[0:NP, :]), it)
                for j in range(GT):
                    ins = vec.tensor_scalar(rows[:, j, :], rows[:, j, :], mv[0:NP, j, 0:1], rstd[0:NP, j:j + 1], ALU.subtract, ALU.mult)
                    if l == 2:
                        ins.then_inc(ns[l]["o_normed"], 1)
                if l == 3:
                    ins.then_inc(ns[l]["o_normed"], 1)

            def banked(n):
                a, z = BANKS[n]
                return row_bank[n][0:NP, 0:(z - a) * HID].rearrange("p (t f) -> p t f", f=HID), slice(a, z)

            def node_dve(l):
                s = ns[l]
                start, step, end = chain_of(s, *((20, 0), (26, 1))[l - 1])
                weight = psT[0:NP, 0:2 * GT * HEADS].rearrange("p (n t h) -> p n t h", n=2, t=GT)

                def by_head(t):
                    return t.rearrange("p t (h f) -> p t h f", h=HEADS)

                def body(it):
                    start(it)
                    for par in range(2):
                        g = 2 * it + par
                        e, o = ends[0:NP, par], own[0:NP, par]
                        dve.wait_ge(s["in_"][par], in_dmas(l) * (it + 1))
                        dve.wait_ge(s["got"][par], 16 * GT * (it + 1))
                        step(vec.tensor_tensor(self_e[0:NP], o[:, :, HID:HID + HEADS], o[:, :, HID + HEADS:ROW], ALU.add), it)
                        step(vec.scalar_tensor_tensor(self_e[0:NP], self_e[0:NP], SLOPE, self_e[0:NP], ALU.mult, ALU.max), it)
                        step(vec.tensor_tensor(self_x[0:NP, 0], e[:, :, HID + HEADS:ROW],
                                               by_node(max_bound, g).unsqueeze(2).to_broadcast([NP, GT, HEADS]), ALU.min), it)
                        step(vec.tensor_tensor(den[0:NP], self_x[0:NP, 0], self_e[0:NP], ALU.max), it)
                        vec.tensor_tensor(self_x[0:NP, 0], self_x[0:NP, 0], den[0:NP], ALU.subtract)
                        vec.tensor_tensor(self_x[0:NP, 1], self_e[0:NP], den[0:NP], ALU.subtract).then_inc(s["xd"], 1)
                        dve.wait_ge(s["ex"], g + 1)
                        step(vec.tensor_tensor(den[0:NP], e[:, :, HID:HID + HEADS], self_w[0:NP, 0], ALU.mult), it)
                        step(vec.tensor_tensor(den[0:NP], den[0:NP], self_w[0:NP, 1], ALU.add), it)
                        step(vec.tensor_scalar(den[0:NP], den[0:NP], 1.0e-16, None, ALU.add), it)
                        step(vec.reciprocal(den[0:NP], den[0:NP]), it)
                        vec.tensor_tensor(weight[:, 0], self_w[0:NP, 0], den[0:NP], ALU.mult)
                        step(vec.tensor_tensor(weight[:, 1], self_w[0:NP, 1], den[0:NP], ALU.mult), it)
                        own_rows, whole = by_head(o[:, :, 0:HID]), [NP, GT, HEADS, HD]
                        if l == 1:
                            for n in range(len(BANKS)):
                                rows, ts = banked(n)
                                size = [NP, ts.stop - ts.start, HEADS, HD]
                                vec.tensor_tensor(by_head(rows), by_head(e[:, ts, 0:HID]), weight[:, 0, ts].unsqueeze(3).to_broadcast(size), ALU.mult)
                            step(vec.tensor_tensor(own_rows, own_rows, weight[:, 1].unsqueeze(3).to_broadcast(whole), ALU.mult), it)
                            if due((g - 1) * GT):
                                dve.wait_ge(s["xt_ps"], (g - 1) * GT)
                            for n in range(len(BANKS)):
                                rows, ts = banked(n)
                                ins = vec.tensor_tensor(O[0:NP, par, ts], rows, o[:, ts, 0:HID], ALU.add)
                            ins.then_inc(s["o_made"], 1)
                            continue
                        vec.tensor_tensor(own_rows, own_rows, weight[:, 1].unsqueeze(3).to_broadcast(whole), ALU.mult).then_inc(s["weighted"], 1)
                        sums = by_head(e[:, :, 0:HID])
                        step(vec.tensor_tensor(sums, sums, weight[:, 0].unsqueeze(3).to_broadcast(whole), ALU.mult), it)
                        if due(g):
                            layernorm_end(l, O[0:NP, 1 - par], g - 1, it, step)
                        for n in range(len(BANKS)):
                            rows, ts = banked(n)
                            dve.wait_ge(s["merged"], g * len(BANKS) + n + 1)
                            ins = vec.tensor_tensor(rows, rows, e[:, ts, 0:HID], ALU.add)
                        step(ins, it)
                        if due((g - 1) * GT):
                            dve.wait_ge(s["xt_ps"], (g - 1) * GT)
                        if due(32 * it):
                            dve.wait_ge(s["stored"][par], 32 * it)
                        for n in range(len(BANKS)):
                            rows, ts = banked(n)
                            ins = vec.scalar_tensor_tensor(O[0:NP, par, ts], rows, 0.0, xg[0:NP, par, ts], ALU.max, ALU.add)
                        ins.then_inc(s["used"][par], 1)
                        dve.wait_ge(s["used"][par], it + 1)
                        layernorm_start(l, O[0:NP, par], it, step)
                    end()
                rounds(dve, NHALF, body)
                if l == 2:
                    start(NHALF)
                    layernorm_end(l, O[0:NP, 1], NG - 1, NHALF, step)

            def final_dve():
                s = ns[3]
                start, step, end = chain_of(s, 6, 3)
                dve.wait_ge(ns[2]["h"], NT + NZ)
                vec.tensor_copy(psT[0:NP, 0:NT], has_edge[0:NP, :]).then_inc(dve_step, 1)
                n_step[0] += 1
                dve.wait_ge(dve_step, n_step[0])

                def result_rows(it, par, now, step):
                    g, y = 2 * it + par, HTt[0:NP, par, :, 0:HID]
                    if due(16 * it):
                        dve.wait_ge(s["stored"][par], 16 * it)
                    for n in range(len(BANKS)):
                        rows, ts = banked(n)
                        dve.wait_ge(s["h_ps"], g * GT + ts.stop)
                        vec.tensor_tensor(y[:, ts, :], rows, xg[0:NP, par, ts], ALU.add).then_inc(s["h"], 1)
                    dve.wait_ge(s["h"], (g + 1) * len(BANKS))
                    layernorm_start(3, y, now, step)

                def body(it):
                    start(it)
                    for par in range(2):
                        g = 2 * it + par
                        dve.wait_ge(s["in_"][par], in_dmas(3) * (it + 1))
                        dve.wait_ge(s["got"][par], 16 * GT * (it + 1))
                        if due((g - 1) * GT):
                            dve.wait_ge(s["xt_ps"], (g - 1) * GT)
                        step(vec.tensor_tensor(O[0:NP, par], ends[0:NP, par, :, 0:HID], own[0:NP, par, :, 0:HID], ALU.add), it)
                        vec.memset(small[0:NP, 7, 6:7], 0.0).then_inc(s["used"][par], 1)
                        vec.tensor_tensor(O[0:NP, par], O[0:NP, par], by_node(psT, g).unsqueeze(2).to_broadcast([NP, GT, HID]),
                                          ALU.mult).then_inc(s["o_made"], 1)
                        if due(g - 1):
                            layernorm_end(3, HTt[0:NP, par, :, 0:HID], g - 2, it, step)
                        if par:
                            result_rows(it, 0, it, step)
                        elif due(it):
                            result_rows(it - 1, 1, it, step)
                    end()
                rounds(dve, NHALF, body, peel=2)
                start(NHALF)
                layernorm_end(3, HTt[0:NP, 0, :, 0:HID], NG - 2, NHALF, step)
                result_rows(NHALF - 1, 1, NHALF, step)
                layernorm_end(3, HTt[0:NP, 1, :, 0:HID], NG - 1, NHALF, step)

            edge_dve(0)
            node_dve(1)
            edge_dve(1)
            node_dve(2)
            edge_dve(2)
            final_dve()


_INS = ["x", "src", "dst", "edge_weight", "L0_gnn_W1", "L0_gnn_att_src1", "L0_gnn_att_dst1", "L0_gnn_bias1", "L0_gnn_W2",
        "L0_gnn_att_src2", "L0_gnn_att_dst2", "L0_gnn_bias2", "L1_gnn_Wm", "L1_gnn_bm", "L1_gnn_W1", "L1_gnn_b1", "L1_gnn_W2", "L1_gnn_b2"]


def kernel(**inputs):
    import numpy as np
    import concourse.bacc as bacc
    from concourse.bass_utils import run_bass_kernel_spmd

    nc = bacc.Bacc("TRN2", target_bir_lowering=False, num_devices=1)
    arrays, args = {}, []
    for name in _INS:
        a = np.ascontiguousarray(inputs[name])
        arrays[f"in_{name}"] = a
        args.append(nc.dram_tensor(f"in_{name}", a.shape, mybir.dt.from_np(a.dtype), kind="ExternalInput").ap())
    args.append(nc.dram_tensor("out", (N_NODES, HID), F32, kind="ExternalOutput").ap())
    gnn_program(nc, *args)
    return run_bass_kernel_spmd(nc, [arrays], core_ids=[0]).results[0]["out"]
```
